# Optimizing a Trainium2 kernel written in Bass

```python
import numpy as np
import jax
import jax.numpy as jnp

def _softmax(x, axis=-1):
    return jax.nn.softmax(x, axis=axis)

def _gelu(x):
    return jax.nn.gelu(x, approximate=True)

def _silu(x):
    return jax.nn.silu(x)

def _sigmoid(x):
    return jax.nn.sigmoid(x)

def _layernorm(x, axis=-1, eps=1e-05):
    m = jnp.mean(x, axis=axis, keepdims=True)
    v = jnp.var(x, axis=axis, keepdims=True)
    return (x - m) / jnp.sqrt(v + eps)

def _scatter_add(tgt, idx, src, axis=0):
    return tgt.at[idx].add(src)

def _segment_sum(src, seg, n):
    return jax.ops.segment_sum(src, seg, n)
kernel_name = 'mk_xattn_ffn_d2_seqx_r4_4aac96'

def setup_inputs(seed: int=0):
    np.random.seed(seed)
    _w = jnp.asarray

    def _rec_inputs():
        import jax
        import jax.numpy as jnp
        _rk = jax.random.key(seed)
        x = -0.0002928 + 1 * jax.random.normal(jax.random.fold_in(_rk, 1), (8, 256, 256), jnp.float32)
        _lenS = 256 - jax.random.randint(jax.random.fold_in(_rk, 7), (8,), 0, max(1, 256 // 4) + 1, jnp.int32)
        _lenS2 = 256 - jax.random.randint(jax.random.fold_in(_rk, 8), (8,), 0, max(1, 256 // 4) + 1, jnp.int32)
        _ctx_1024P = jax.random.normal(jax.random.fold_in(_rk, 11), (8, 16, 256), jnp.float32)
        _ctx_1024c = jax.random.dirichlet(jax.random.fold_in(_rk, 511), 0.3 * jnp.ones((16,), jnp.float32), (8, 256))
        _ctx_1024t = jnp.einsum('bsk,bkd->bsd', _ctx_1024c, _ctx_1024P)
        _ctx_1024t = _ctx_1024t * jax.lax.rsqrt(jnp.mean(jnp.square(_ctx_1024t)) + 1e-12) * 0.953939
        ctx_1024 = -1.39393e-06 + 0.999914 * (_ctx_1024t + 0.3 * jax.random.normal(jax.random.fold_in(_rk, 611), (8, 256, 256), jnp.float32))
        return (x, ctx_1024)
    x, ctx_1024 = _rec_inputs()

    def _L0_xattn_setup():
        import jax, jax.numpy as jnp
        import numpy as np
        B, T, D, H = (2, 512, 256, 16)
        DH = D // H
        key = jax.random.key(seed)
        ks = jax.random.split(key, 11)
        s = 1.0 / np.sqrt(D)
        return {'q': jax.random.normal(ks[0], (B, T, D), jnp.float32), 'k': jax.random.normal(ks[1], (B, T, D), jnp.float32), 'v': jax.random.normal(ks[2], (B, T, D), jnp.float32), 'wq_w': jax.random.normal(ks[3], (D, D), jnp.float32) * s, 'wq_b': jnp.zeros((D,), jnp.float32), 'wk_w': jax.random.normal(ks[4], (D, D), jnp.float32) * s, 'wk_b': jnp.zeros((D,), jnp.float32), 'wv_w': jax.random.normal(ks[5], (D, D), jnp.float32) * s, 'wv_b': jnp.zeros((D,), jnp.float32), 'wo_w': jax.random.normal(ks[6], (D, D), jnp.float32) * s, 'wo_b': jnp.zeros((D,), jnp.float32)}
    _L0_xattn_all = _L0_xattn_setup()
    _L0_xattn_in = {k: v for k, v in _L0_xattn_all.items() if k in ('wq_w', 'wq_b', 'wk_w', 'wk_b', 'wv_w', 'wv_b', 'wo_w', 'wo_b')}
    del _L0_xattn_all

    def _L0_ffn_setup():
        import jax, jax.numpy as jnp
        import numpy as np
        DIM = 256
        DEPTH = 6
        HEADS = 16
        DIM_HEAD = 64
        WINDOW = 64
        INNER = HEADS * DIM_HEAD
        DIM_INNER = int(DIM * 4 * 2 / 3)
        QK_SCALE = 8.0

        def shift_tokens(t):
            a, s = jnp.split(t, 2, -1)
            s = jnp.pad(s, ((0, 0), (1, 0), (0, 0)))[:, :-1]
            return jnp.concatenate([a, s], -1)

        def l2norm(t):
            return t / jnp.maximum(jnp.linalg.norm(t, axis=-1, keepdims=True), 1e-12)

        def rotate_half(x):
            x1, x2 = jnp.split(x, 2, -1)
            return jnp.concatenate([-x2, x1], -1)

        def rotary_tables(n):
            half = jnp.arange(0, DIM_HEAD, 2, dtype=jnp.float32)
            inv_freq = 1.0 / 10000.0 ** (half / DIM_HEAD)
            t = jnp.arange(n, dtype=jnp.float32)
            freqs = t[:, None] * inv_freq[None, :]
            freqs = jnp.concatenate([freqs, freqs], -1)
            base_scale = (half + 0.4 * DIM_HEAD) / (1.4 * DIM_HEAD)
            power = (t - n // 2) / (WINDOW // 2)
            scale = base_scale[None, :] ** power[:, None]
            scale = jnp.concatenate([scale, scale], -1)
            return (freqs, scale)

        def local_attention(q, k, v):
            b, h, n, d = q.shape
            w = WINDOW
            nw = n // w
            bq = q.reshape(b, h, nw, w, d)
            bk = k.reshape(b, h, nw, w, d)
            bv = v.reshape(b, h, nw, w, d)

            def look(t):
                p = jnp.pad(t, ((0, 0), (0, 0), (1, 0), (0, 0), (0, 0)))
                return jnp.concatenate([p[:, :, :nw], p[:, :, 1:]], axis=3)
            bk2, bv2 = (look(bk), look(bv))
            seq = jnp.arange(n).reshape(nw, w)
            seq_p = jnp.pad(seq, ((1, 0), (0, 0)), constant_values=-1)
            jt = jnp.concatenate([seq_p[:nw], seq_p[1:]], axis=1)
            it = seq[:, :, None]
            jb = jt[:, None, :]
            mask = (it < jb) | (it > jb + w) | (jb == -1)
            sim = jnp.einsum('bhwie,bhwje->bhwij', bq, bk2) * QK_SCALE
            sim = jnp.where(mask, -jnp.finfo(sim.dtype).max, sim)
            attn = jax.nn.softmax(sim, -1)
            out = jnp.einsum('bhwij,bhwje->bhwie', attn, bv2)
            return out.reshape(b, h, n, d)

        def attn_layer(x, Wqkv, qs, ksc, Wo):
            b, n, _ = x.shape
            qkv = x @ Wqkv
            q, k, v = jnp.split(qkv, 3, -1)
            sh = lambda t: t.reshape(b, n, HEADS, DIM_HEAD).transpose(0, 2, 1, 3)
            q, k, v = (sh(q), sh(k), sh(v))
            q = l2norm(q) * qs
            k = l2norm(k) * ksc
            freqs, scale = rotary_tables(n)
            cos, sin = (jnp.cos(freqs), jnp.sin(freqs))
            q = q * cos * scale + rotate_half(q) * sin * scale
            inv = 1.0 / scale
            k = k * cos * inv + rotate_half(k) * sin * inv
            out = local_attention(q, k, v)
            out = out.transpose(0, 2, 1, 3).reshape(b, n, INNER)
            return out @ Wo

        def ffn_layer(x, g, bln, W1, b1, W2, b2):
            mu = x.mean(-1, keepdims=True)
            var = ((x - mu) ** 2).mean(-1, keepdims=True)
            xn = (x - mu) / jnp.sqrt(var + 1e-05) * g + bln
            hg = xn @ W1 + b1
            a, gate = jnp.split(hg, 2, -1)
            return a * jax.nn.gelu(gate, approximate=False) @ W2 + b2
        key = jax.random.key(seed)
        ks = jax.random.split(key, 8)
        B, N = (2, 512)
        init = lambda k, shape: jax.random.normal(k, shape, jnp.float32) * 0.02
        return {'x': jax.random.normal(ks[0], (B, N, DIM), jnp.float32), 'Wqkv': init(ks[1], (DEPTH, DIM, 3 * INNER)), 'q_scale': jnp.ones((DEPTH, DIM_HEAD), jnp.float32), 'k_scale': jnp.ones((DEPTH, DIM_HEAD), jnp.float32), 'Wo': init(ks[2], (DEPTH, INNER, DIM)), 'ln_g': jnp.ones((DEPTH, DIM), jnp.float32), 'ln_b': jnp.zeros((DEPTH, DIM), jnp.float32), 'W1': init(ks[3], (DEPTH, DIM, 2 * DIM_INNER)), 'b1': jnp.zeros((DEPTH, 2 * DIM_INNER), jnp.float32), 'W2': init(ks[4], (DEPTH, DIM_INNER, DIM)), 'b2': jnp.zeros((DEPTH, DIM), jnp.float32)}
    _L0_ffn_all = _L0_ffn_setup()
    _L0_ffn_in = {k: v for k, v in _L0_ffn_all.items() if k in ('Wqkv', 'q_scale', 'k_scale', 'Wo', 'ln_g', 'ln_b', 'W1', 'b1', 'W2', 'b2')}
    del _L0_ffn_all

    def _L1_xattn_setup():
        import jax, jax.numpy as jnp
        import numpy as np
        D_MODEL = 256
        NUM_HEADS = 16
        D_K = D_MODEL // NUM_HEADS
        B, S = (4, 512)
        key = jax.random.key(seed)
        ks = jax.random.split(key, 11)
        scale = 1.0 / np.sqrt(D_MODEL)
        inp = {'query': jax.random.normal(ks[0], (B, S, D_MODEL), dtype=jnp.float32), 'key': jax.random.normal(ks[1], (B, S, D_MODEL), dtype=jnp.float32), 'value': jax.random.normal(ks[2], (B, S, D_MODEL), dtype=jnp.float32), 'Wq': jax.random.normal(ks[3], (D_MODEL, D_MODEL), dtype=jnp.float32) * scale, 'bq': jnp.zeros((D_MODEL,), dtype=jnp.float32), 'Wk': jax.random.normal(ks[4], (D_MODEL, D_MODEL), dtype=jnp.float32) * scale, 'bk': jnp.zeros((D_MODEL,), dtype=jnp.float32), 'Wv': jax.random.normal(ks[5], (D_MODEL, D_MODEL), dtype=jnp.float32) * scale, 'bv': jnp.zeros((D_MODEL,), dtype=jnp.float32), 'Wo': jax.random.normal(ks[6], (D_MODEL, D_MODEL), dtype=jnp.float32) * scale, 'bo': jnp.zeros((D_MODEL,), dtype=jnp.float32)}
        return inp
    _L1_xattn_all = _L1_xattn_setup()
    _L1_xattn_in = {k: v for k, v in _L1_xattn_all.items() if k in ('Wq', 'bq', 'Wk', 'bk', 'Wv', 'bv', 'Wo', 'bo')}
    del _L1_xattn_all

    def _L1_ffn_setup():
        import jax, jax.numpy as jnp
        import numpy as np
        DIM = 256
        HIDDEN = 768
        SCALE = 1.0 / 127.0

        def _dequant(w_int, dtype):
            return w_int.astype(dtype) * jnp.asarray(SCALE, dtype)
        key = jax.random.key(seed)
        k_x, k_g, k_u, k_d = jax.random.split(key, 4)
        x = jax.random.normal(k_x, (4, 512, DIM), dtype=jnp.float32)
        w_gate = jax.random.randint(k_g, (HIDDEN, DIM), -127, 128, dtype=jnp.int32)
        w_up = jax.random.randint(k_u, (HIDDEN, DIM), -127, 128, dtype=jnp.int32)
        w_down = jax.random.randint(k_d, (DIM, HIDDEN), -127, 128, dtype=jnp.int32)
        return {'x': x, 'w_gate': w_gate, 'w_up': w_up, 'w_down': w_down}
    _L1_ffn_all = _L1_ffn_setup()
    _L1_ffn_in = {k: v for k, v in _L1_ffn_all.items() if k in ('w_gate', 'w_up', 'w_down')}
    del _L1_ffn_all
    return {'x': x, 'ctx_1024': ctx_1024, 'L0_xattn_wq_w': _L0_xattn_in['wq_w'], 'L0_xattn_wq_b': _L0_xattn_in['wq_b'], 'L0_xattn_wk_w': _L0_xattn_in['wk_w'], 'L0_xattn_wk_b': _L0_xattn_in['wk_b'], 'L0_xattn_wv_w': _L0_xattn_in['wv_w'], 'L0_xattn_wv_b': _L0_xattn_in['wv_b'], 'L0_xattn_wo_w': _L0_xattn_in['wo_w'], 'L0_xattn_wo_b': _L0_xattn_in['wo_b'], 'L0_ffn_Wqkv': _L0_ffn_in['Wqkv'], 'L0_ffn_q_scale': _L0_ffn_in['q_scale'], 'L0_ffn_k_scale': _L0_ffn_in['k_scale'], 'L0_ffn_Wo': _L0_ffn_in['Wo'], 'L0_ffn_ln_g': _L0_ffn_in['ln_g'], 'L0_ffn_ln_b': _L0_ffn_in['ln_b'], 'L0_ffn_W1': _L0_ffn_in['W1'], 'L0_ffn_b1': _L0_ffn_in['b1'], 'L0_ffn_W2': _L0_ffn_in['W2'], 'L0_ffn_b2': _L0_ffn_in['b2'], 'L1_xattn_Wq': _L1_xattn_in['Wq'], 'L1_xattn_bq': _L1_xattn_in['bq'], 'L1_xattn_Wk': _L1_xattn_in['Wk'], 'L1_xattn_bk': _L1_xattn_in['bk'], 'L1_xattn_Wv': _L1_xattn_in['Wv'], 'L1_xattn_bv': _L1_xattn_in['bv'], 'L1_xattn_Wo': _L1_xattn_in['Wo'], 'L1_xattn_bo': _L1_xattn_in['bo'], 'L1_ffn_w_gate': _L1_ffn_in['w_gate'], 'L1_ffn_w_up': _L1_ffn_in['w_up'], 'L1_ffn_w_down': _L1_ffn_in['w_down']}

def reference(x, ctx_1024, L0_xattn_wq_w, L0_xattn_wq_b, L0_xattn_wk_w, L0_xattn_wk_b, L0_xattn_wv_w, L0_xattn_wv_b, L0_xattn_wo_w, L0_xattn_wo_b, L0_ffn_Wqkv, L0_ffn_q_scale, L0_ffn_k_scale, L0_ffn_Wo, L0_ffn_ln_g, L0_ffn_ln_b, L0_ffn_W1, L0_ffn_b1, L0_ffn_W2, L0_ffn_b2, L1_xattn_Wq, L1_xattn_bq, L1_xattn_Wk, L1_xattn_bk, L1_xattn_Wv, L1_xattn_bv, L1_xattn_Wo, L1_xattn_bo, L1_ffn_w_gate, L1_ffn_w_up, L1_ffn_w_down):
    import jax
    import jax.numpy as jnp

    def _L0_xattn_ref(q, k, v, wq_w, wq_b, wk_w, wk_b, wv_w, wv_b, wo_w, wo_b):
        import jax, jax.numpy as jnp
        import numpy as np
        B, T, D, H = (2, 512, 256, 16)
        DH = D // H
        b, t, d = q.shape
        wq = (q @ wq_w.T + wq_b).reshape(b, t, H, DH)
        wk = (k @ wk_w.T + wk_b).reshape(b, t, H, DH)
        wv = (v @ wv_w.T + wv_b).reshape(b, t, H, DH)
        scores = jnp.einsum('bthd,bshd->bhts', wq, wk) / jnp.sqrt(jnp.float32(DH))
        probs = jax.nn.softmax(scores, axis=-1)
        attn = jnp.einsum('bhts,bshd->bthd', probs, wv)
        attn = attn.reshape(b, t, d)
        return attn @ wo_w.T + wo_b

    def _L0_ffn_ref(x, Wqkv, q_scale, k_scale, Wo, ln_g, ln_b, W1, b1, W2, b2):
        import jax, jax.numpy as jnp
        import numpy as np
        DIM = 256
        DEPTH = 6
        HEADS = 16
        DIM_HEAD = 64
        WINDOW = 64
        INNER = HEADS * DIM_HEAD
        DIM_INNER = int(DIM * 4 * 2 / 3)
        QK_SCALE = 8.0

        def shift_tokens(t):
            a, s = jnp.split(t, 2, -1)
            s = jnp.pad(s, ((0, 0), (1, 0), (0, 0)))[:, :-1]
            return jnp.concatenate([a, s], -1)

        def l2norm(t):
            return t / jnp.maximum(jnp.linalg.norm(t, axis=-1, keepdims=True), 1e-12)

        def rotate_half(x):
            x1, x2 = jnp.split(x, 2, -1)
            return jnp.concatenate([-x2, x1], -1)

        def rotary_tables(n):
            half = jnp.arange(0, DIM_HEAD, 2, dtype=jnp.float32)
            inv_freq = 1.0 / 10000.0 ** (half / DIM_HEAD)
            t = jnp.arange(n, dtype=jnp.float32)
            freqs = t[:, None] * inv_freq[None, :]
            freqs = jnp.concatenate([freqs, freqs], -1)
            base_scale = (half + 0.4 * DIM_HEAD) / (1.4 * DIM_HEAD)
            power = (t - n // 2) / (WINDOW // 2)
            scale = base_scale[None, :] ** power[:, None]
            scale = jnp.concatenate([scale, scale], -1)
            return (freqs, scale)

        def local_attention(q, k, v):
            b, h, n, d = q.shape
            w = WINDOW
            nw = n // w
            bq = q.reshape(b, h, nw, w, d)
            bk = k.reshape(b, h, nw, w, d)
            bv = v.reshape(b, h, nw, w, d)

            def look(t):
                p = jnp.pad(t, ((0, 0), (0, 0), (1, 0), (0, 0), (0, 0)))
                return jnp.concatenate([p[:, :, :nw], p[:, :, 1:]], axis=3)
            bk2, bv2 = (look(bk), look(bv))
            seq = jnp.arange(n).reshape(nw, w)
            seq_p = jnp.pad(seq, ((1, 0), (0, 0)), constant_values=-1)
            jt = jnp.concatenate([seq_p[:nw], seq_p[1:]], axis=1)
            it = seq[:, :, None]
            jb = jt[:, None, :]
            mask = (it < jb) | (it > jb + w) | (jb == -1)
            sim = jnp.einsum('bhwie,bhwje->bhwij', bq, bk2) * QK_SCALE
            sim = jnp.where(mask, -jnp.finfo(sim.dtype).max, sim)
            attn = jax.nn.softmax(sim, -1)
            out = jnp.einsum('bhwij,bhwje->bhwie', attn, bv2)
            return out.reshape(b, h, n, d)

        def attn_layer(x, Wqkv, qs, ksc, Wo):
            b, n, _ = x.shape
            qkv = x @ Wqkv
            q, k, v = jnp.split(qkv, 3, -1)
            sh = lambda t: t.reshape(b, n, HEADS, DIM_HEAD).transpose(0, 2, 1, 3)
            q, k, v = (sh(q), sh(k), sh(v))
            q = l2norm(q) * qs
            k = l2norm(k) * ksc
            freqs, scale = rotary_tables(n)
            cos, sin = (jnp.cos(freqs), jnp.sin(freqs))
            q = q * cos * scale + rotate_half(q) * sin * scale
            inv = 1.0 / scale
            k = k * cos * inv + rotate_half(k) * sin * inv
            out = local_attention(q, k, v)
            out = out.transpose(0, 2, 1, 3).reshape(b, n, INNER)
            return out @ Wo

        def ffn_layer(x, g, bln, W1, b1, W2, b2):
            mu = x.mean(-1, keepdims=True)
            var = ((x - mu) ** 2).mean(-1, keepdims=True)
            xn = (x - mu) / jnp.sqrt(var + 1e-05) * g + bln
            hg = xn @ W1 + b1
            a, gate = jnp.split(hg, 2, -1)
            return a * jax.nn.gelu(gate, approximate=False) @ W2 + b2
        for i in range(DEPTH):
            x = attn_layer(shift_tokens(x), Wqkv[i], q_scale[i], k_scale[i], Wo[i]) + x
            x = ffn_layer(shift_tokens(x), ln_g[i], ln_b[i], W1[i], b1[i], W2[i], b2[i]) + x
        return x

    def _L1_xattn_ref(query, key, value, Wq, bq, Wk, bk, Wv, bv, Wo, bo):
        import jax, jax.numpy as jnp
        import numpy as np
        D_MODEL = 256
        NUM_HEADS = 16
        D_K = D_MODEL // NUM_HEADS
        B, S = (4, 512)
        b, sq, _ = query.shape
        sk = key.shape[1]
        Q = query @ Wq + bq
        K = key @ Wk + bk
        V = value @ Wv + bv
        Q = Q.reshape(b, sq, NUM_HEADS, D_K).transpose(0, 2, 1, 3)
        K = K.reshape(b, sk, NUM_HEADS, D_K).transpose(0, 2, 1, 3)
        V = V.reshape(b, sk, NUM_HEADS, D_K).transpose(0, 2, 1, 3)
        scores = jnp.einsum('bhqd,bhkd->bhqk', Q, K) / jnp.sqrt(jnp.float32(D_K))
        attn = jax.nn.softmax(scores, axis=-1)
        out = jnp.einsum('bhqk,bhkd->bhqd', attn, V)
        out = out.transpose(0, 2, 1, 3).reshape(b, sq, D_MODEL)
        return out @ Wo + bo

    def _L1_ffn_ref(x, w_gate, w_up, w_down):
        import jax, jax.numpy as jnp
        import numpy as np
        DIM = 256
        HIDDEN = 768
        SCALE = 1.0 / 127.0

        def _dequant(w_int, dtype):
            return w_int.astype(dtype) * jnp.asarray(SCALE, dtype)
        wg = _dequant(w_gate, x.dtype)
        wu = _dequant(w_up, x.dtype)
        wd = _dequant(w_down, x.dtype)
        gate = jnp.einsum('bsd,hd->bsh', x, wg)
        up = jnp.einsum('bsd,hd->bsh', x, wu)
        h = jax.nn.silu(gate) * up
        return jnp.einsum('bsh,dh->bsd', h, wd)
    x = x + _L0_xattn_ref(_layernorm(x, axis=-1), ctx_1024, ctx_1024, L0_xattn_wq_w, L0_xattn_wq_b, L0_xattn_wk_w, L0_xattn_wk_b, L0_xattn_wv_w, L0_xattn_wv_b, L0_xattn_wo_w, L0_xattn_wo_b)
    x = x + _L0_ffn_ref(_layernorm(x, axis=-1), L0_ffn_Wqkv, L0_ffn_q_scale, L0_ffn_k_scale, L0_ffn_Wo, L0_ffn_ln_g, L0_ffn_ln_b, L0_ffn_W1, L0_ffn_b1, L0_ffn_W2, L0_ffn_b2)
    x = x + _L1_xattn_ref(_layernorm(x, axis=-1), ctx_1024, ctx_1024, L1_xattn_Wq, L1_xattn_bq, L1_xattn_Wk, L1_xattn_bk, L1_xattn_Wv, L1_xattn_bv, L1_xattn_Wo, L1_xattn_bo)
    x = x + _L1_ffn_ref(_layernorm(x, axis=-1), L1_ffn_w_gate, L1_ffn_w_up, L1_ffn_w_down)
    return x

_drawn_inputs = setup_inputs


def setup_inputs(seed=0):
    import zlib

    import numpy as np

    out = dict(_drawn_inputs(seed))
    spreads = {'L0_xattn_wq_b': (0.0, 0.307),
     'L0_xattn_wk_b': (0.0, 0.8),
     'L0_xattn_wv_b': (0.0, 0.1),
     'L0_xattn_wo_b': (0.0, 0.1),
     'L0_ffn_q_scale': (1.0, 0.6),
     'L0_ffn_k_scale': (1.0, 0.6),
     'L0_ffn_ln_g': (1.0, 0.6),
     'L0_ffn_ln_b': (0.0, 0.8),
     'L0_ffn_b1': (0.0, 0.35),
     'L0_ffn_b2': (0.0, 0.1),
     'L1_xattn_bq': (0.0, 0.571),
     'L1_xattn_bk': (0.0, 0.8),
     'L1_xattn_bv': (0.0, 0.1),
     'L1_xattn_bo': (0.0, 0.1)}
    factors = {}
    for name, (base, spread) in spreads.items():
        noise = np.random.default_rng([zlib.crc32(name.encode()), seed]).standard_normal(out[name].shape)
        drawn = base * np.exp(spread * noise) if base else spread * noise
        out[name] = jnp.asarray(drawn.astype(out[name].dtype))
    for name, factor in factors.items():
        out[name] = (out[name] * factor).astype(out[name].dtype)
    return out
```

```python
from contextlib import ExitStack

import numpy as np

import concourse.bass as bass
from concourse import mybir

F32 = mybir.dt.float32
F32R = mybir.dt.float32r
BF16 = mybir.dt.bfloat16
ALU = mybir.AluOpType
ACT = mybir.ActivationFunctionType
AX = mybir.AxisListType

P = 128
BATCH, SEQ, DIM = 8, 256, 256
TILES = SEQ // P
KD = DIM // P
DEPTH, HEADS, DH = 6, 16, 64
PAIRS = HEADS // 2
INNER = HEADS * DH
FF = 682
FT = 6
FP = 114
WINDOW = 64
QKS = 8.0
SPANS = P + (P + WINDOW)
PCOLS = 3 * P

UNITS = [512] * 16 + [KD * 2 * FP] * 6 + [512] * 3
OFFS = [sum(UNITS[:u]) for u in range(len(UNITS))]
NU = len(UNITS)
WCOLS = sum(UNITS)
U_QKV, U_WO, U_GATE, U_UP, U_W2 = 0, 12, 16, 19, 22
NPRM = 2 * KD + 2 * FT
CONSTS = 4

EPS = 1e-5
STEPS = DEPTH * BATCH


def stack_phase(nc, ctx, y, wh, wl, d_w, d_prm, d_qks, d_b2, d_const):

    def sb(name, shape, dt=F32):
        return ctx.enter_context(nc.sbuf_tensor(name, shape, dt))

    def sem(name):
        return nc.alloc_semaphore(name)

    raw = sb("raw", [P, 2, 512])
    rope_base = sb("rope_base", [P, 4, TILES, 32])
    mask = sb("mask", [P, SPANS])
    ident = sb("ident", [P, P])
    qks = sb("qks", [P, 2, 2, 32])
    qks_swapped = sb("qks_swapped", [P, 2, 2, 32])
    rope = sb("rope", [P, 2, 2, TILES, 64])
    prm = sb("prm", [P, DEPTH, NPRM])
    b2 = sb("b2", [P, DIM])
    ycur = sb("ycur", [P, TILES, DIM])
    xth = sb("xth", [P, KD, SEQ + 1], F32R)
    xtl = sb("xtl", [P, KD, SEQ + 1], F32R)
    qk_tok = sb("qk_tok", [P, 2, TILES, 512])
    rot_tmp = sb("rot_tmp", [P, 512])
    squares = sb("squares", [P, 512])
    ss = sb("ss", [P, 2, 16])
    ssc = sb("ssc", [P, 2, 16])
    rn = sb("rn", [P, 2, 16])
    minus_half = sb("minus_half", [P, 32])
    qsc = sb("qsc", [P, PAIRS, 4])
    qkT = sb("qkT", [P, 2, PAIRS, SEQ])
    v = sb("v", [P, TILES, INNER])
    probs = sb("probs", [P, 2, PCOLS])
    probsT = sb("probsT", [P, 2, PCOLS])
    mx = sb("mx", [P, 4, 4])
    nbias = sb("nbias", [P, 4, 4])
    rsum = sb("rsum", [P, 4, 4])
    rinv = sb("rinv", [P, 4, 4])
    o_tok = sb("o_tok", [P, TILES, P])
    oth = sb("oth", [P, 4, SEQ], F32R)
    otl = sb("otl", [P, 4, SEQ], F32R)
    xn = sb("xn", [P, 2, DIM])
    bst = sb("bst", [P, TILES, 2, 6])
    mv = sb("mv", [P, TILES, 2])
    rstd = sb("rstd", [P, TILES])
    vareps = sb("vareps", [P, TILES])
    xnh = sb("xnh", [P, KD, SEQ], F32R)
    xnl = sb("xnl", [P, KD, SEQ], F32R)
    hid = sb("hid", [P, FT, SEQ])
    hh = sb("hh", [P, 2, 2, SEQ], F32R)
    hl = sb("hl", [P, 2, 2, SEQ], F32R)

    ps_sim = [ctx.enter_context(nc.psum_tensor(f"ps_sim{h}", [P, 512], F32)) for h in range(2)]
    ps_pt = [ctx.enter_context(nc.psum_tensor(f"ps_pt{h}", [P, 512], F32)) for h in range(2)]
    ps_o = ctx.enter_context(nc.psum_tensor("ps_o", [P, 512], F32))
    ps_mm = [ctx.enter_context(nc.psum_tensor(f"ps_mm{b}", [P, 512], F32)) for b in range(3)]

    sim_done, pt_done, pv_done, ot_done = sem("sim_done"), sem("pt_done"), sem("pv_done"), sem("ot_done")
    qk_done, v_done, tr_done, wo_done = sem("qk_done"), sem("v_done"), sem("tr_done"), sem("wo_done")
    xt_done, xnt_done, gate_done, up_done, w2_done = (sem("xt_done"), sem("xnt_done"), sem("gate_done"),
                                                      sem("up_done"), sem("w2_done"))
    sim_masked, bias_ready, rinv_ready, o_ready = sem("sim_masked"), sem("bias_ready"), sem("rinv_ready"), sem("o_ready")
    otl_ready, rot_part, qk_free, qk_rotated = sem("otl_ready"), sem("rot_part"), sem("qk_free"), sem("qk_rotated")
    kn_ready, qsc_ready, xtl_ready, y_added = sem("kn_ready"), sem("qsc_ready"), sem("xtl_ready"), sem("y_added")
    stats_ready, mv_ready, xn_ready, xnf_ready, xnl_ready = (sem("stats_ready"), sem("mv_ready"), sem("xn_ready"),
                                                             sem("xnf_ready"), sem("xnl_ready"))
    gate_ready, h_ready, hl_ready, y_summed, y_ready = (sem("gate_ready"), sem("h_ready"), sem("hl_ready"),
                                                        sem("y_summed"), sem("y_ready"))
    zeroed, xn_free, minus_ready = sem("zeroed"), sem("xn_free"), sem("minus_ready")
    exp_done, pt_moved, oth_ready, sq_ready = sem("exp_done"), sem("pt_moved"), sem("oth_ready"), sem("sq_ready")
    v_moved, tr_moved, xth_ready, xnh_ready = sem("v_moved"), sem("tr_moved"), sem("xth_ready"), sem("xnh_ready")
    gelu_done, hh_ready = sem("gelu_done"), sem("hh_ready")
    w_hi, w_ready, rope_part, rope_ready = sem("w_hi"), sem("w_ready"), sem("rope_part"), sem("rope_ready")
    rn_part, rn_ready, rs_part, rstd_ready = sem("rn_part"), sem("rn_ready"), sem("rs_part"), sem("rstd_ready")
    raw_in = [sem("raw_in0"), sem("raw_in1")]
    const_in, qks_in, b2_in, ycur_in, shift_in = (sem("const_in"), sem("qks_in"), sem("b2_in"),
                                                          sem("ycur_in"), sem("shift_in"))

    block = ctx.enter_context(nc.Block())

    def on(m):
        return not isinstance(m, int) or 0 <= m < STEPS

    def later(m, first=0):
        return not isinstance(m, int) or m > first

    def settle(eng):
        eng.nop(nofuse=True)

    def sample(m):
        return m % BATCH

    def layer(m):
        return m // BATCH

    FULL = (3, STEPS)
    EDGES = (range(0, FULL[0]), range(FULL[1], STEPS + 3))

    QA, KA, QB, KB = 0, 2, 4, 6
    USES = [
        [("wo", 2, 2), ("w2", 0, 3), ("up", 2, 3), ("qk", KB, 1)],
        [("qk", KB + 1, 1), ("v", 0, 1), ("v", 1, 1)],
        [("wo", 3, 2), ("tr", 4, 1), ("tr", 5, 1), ("v", 2, 1), ("v", 3, 1)],
        [("tr", 6, 1), ("tr", 7, 1), ("xt", 0, 0), ("qk", QA, 0)],
        [("wo", 0, 1), ("xnt", 0, 2), ("qk", QA + 1, 0), ("qk", KA, 0)],
        [("gate", 0, 2), ("gate", 1, 2), ("qk", KA + 1, 0)],
        [("wo", 1, 1), ("gate", 2, 2), ("tr", 0, 0), ("tr", 1, 0), ("qk", QB, 0)],
        [("up", 0, 2), ("tr", 2, 0), ("tr", 3, 0), ("qk", QB + 1, 0), ("up", 1, 2)],
    ]
    ORDER = [u for slot in USES for u in slot]
    assert len(ORDER) % 3 == 0
    FREED = {"wo": (y_added, 4), "w2": (y_summed, 1), "up": (h_ready, 3), "qk": (qk_free, 8), "v": (v_moved, 4),
             "tr": (tr_moved, 8), "xt": (xtl_ready, 1), "xnt": (xnf_ready, 1), "gate": (gate_ready, 3)}

    def bank(use, idx):
        return ps_mm[[u[:2] for u in ORDER].index((use, idx)) % 3]

    def pair_on(g):
        return not isinstance(g, int) or 0 <= g < STEPS * PAIRS

    @block.tensor
    def _(pe):
        def split3(out, lhs_h, lhs_l, rhs_h, rhs_l, start, stop, **kw):
            pe.matmul(out, lhs_h, rhs_h, start=start, stop=False, **kw)
            pe.matmul(out, lhs_h, rhs_l, start=False, stop=False, **kw)
            return pe.matmul(out, lhs_l, rhs_h, start=False, stop=stop, **kw)

        def wait_bank(n, use, idx):
            at = [u[:2] for u in ORDER].index((use, idx))
            before, i, lag = ORDER[at - 3]
            m = n - lag - (1 if at < 3 else 0)
            if on(m):
                signal, per = FREED[before]
                pe.wait_ge(signal, per * m + i + 1)

        def weights(m, u):
            pe.wait_ge(w_ready, NU * layer(m) + u + 1)

        def wcols(w, u, k, width):
            return w[:, OFFS[u] + k * width:OFFS[u] + (k + 1) * width]

        def project(m, bank_, c, t, signal):
            for k in range(KD):
                u = U_QKV + 2 * c + k
                mm = split3(bank_[:], xth[:, k, t * P:(t + 1) * P], xtl[:, k, t * P:(t + 1) * P],
                            wcols(wh, u, 0, 512), wcols(wl, u, 0, 512), k == 0, k == KD - 1)
            mm.then_inc(signal, 1)

        def dense(n, use, idx, lag):
            m = n - lag
            if not on(m):
                return
            bank_ = bank(use, idx)
            if use == "w2":
                wait_bank(n, use, idx)
                for i in range(2):
                    w2_part(m, i)
                return
            wait_bank(n, use, idx)
            if use == "wo":
                pe.wait_ge(otl_ready, PAIRS * m + 2 * idx + 2)
                weights(m, U_WO + idx)
                for t in range(TILES):
                    for q in range(2):
                        r = (2 * idx + q) % 4
                        mm = split3(bank_[:, t * DIM:(t + 1) * DIM], oth[:, r, t * P:(t + 1) * P],
                                    otl[:, r, t * P:(t + 1) * P], wcols(wh, U_WO + idx, q, DIM),
                                    wcols(wl, U_WO + idx, q, DIM), q == 0, q == 1)
                mm.then_inc(wo_done, 1)
            elif use == "xt":
                pe.wait_ge(ycur_in, 16 * (m + 1))
                for k in range(KD):
                    for t in range(TILES):
                        mm = pe.transpose(bank_[:, k * SEQ + t * P:k * SEQ + (t + 1) * P],
                                          ycur[:, t, k * P:(k + 1) * P], ident[:])
                mm.then_inc(xt_done, 1)
            elif use == "qk":
                c, t = idx // 2, idx % 2
                if idx == QA:
                    pe.wait_ge(xtl_ready, m + 1)
                if t == 0:
                    weights(m, U_QKV + 2 * c + 1)
                project(m, bank_, c, t, qk_done)
            elif use == "v":
                c, t = 4 + idx // 2, idx % 2
                if t == 0:
                    weights(m, U_QKV + 2 * c + 1)
                project(m, bank_, c, t, v_done)
            elif use == "tr":
                which, t = (idx % 4) // 2, idx % 2
                if which == 0:
                    pe.wait_ge(qk_rotated, 8 * m + (QA if idx < 4 else QB) + t + 1)
                else:
                    pe.wait_ge(kn_ready, 4 * m + 2 * (idx // 4) + t + 1)
                for j in range(4):
                    mm = pe.transpose(bank_[:, j * P:(j + 1) * P], qk_tok[:, which, t, j * P:(j + 1) * P], ident[:])
                mm.then_inc(tr_done, 1)
            elif use == "xnt":
                pe.wait_ge(xn_ready, m + 1)
                for k in range(KD):
                    for t in range(TILES):
                        mm = pe.transpose(bank_[:, k * SEQ + t * P:k * SEQ + (t + 1) * P],
                                          xn[:, t, k * P:(k + 1) * P], ident[:])
                mm.then_inc(xnt_done, 1)
            elif use in ("gate", "up"):
                u = (U_GATE if use == "gate" else U_UP) + idx
                weights(m, u)
                if (use, idx) == ("gate", 0):
                    pe.wait_ge(xnl_ready, m + 1)
                for i in range(2):
                    for k in range(KD):
                        at = OFFS[u] + k * 2 * FP + i * FP
                        mm = split3(bank_[0:FP, i * SEQ:(i + 1) * SEQ], wh[:, at:at + FP], wl[:, at:at + FP],
                                    xnh[:, k, :], xnl[:, k, :], k == 0, k == KD - 1)
                mm.then_inc(gate_done if use == "gate" else up_done, 1)

        def w2_part(m, i):
            bank_ = bank("w2", 0)
            pe.wait_ge(hl_ready, 3 * m + i + 1)
            weights(m, U_W2 + i)
            for j in range(2):
                for t in range(TILES):
                    u = U_W2 + i
                    first = i == 0 and j == 0 and t == 0
                    last = i == 2 and j == 1
                    a = hh[0:FP, i % 2, j, t * P:(t + 1) * P], hl[0:FP, i % 2, j, t * P:(t + 1) * P]
                    b = wh[0:FP, OFFS[u] + j * DIM:OFFS[u] + (j + 1) * DIM], wl[0:FP, OFFS[u] + j * DIM:OFFS[u] + (j + 1) * DIM]
                    mm = split3(bank_[:, t * DIM:(t + 1) * DIM], a[0], a[1], b[0], b[1], first, last, skip_group_check=True)
            mm.then_inc(w2_done, 1)

        def weigh_values(g, p, m):
            pe.wait_ge(pt_moved, 2 * g + 2)
            if later(g):
                pe.wait_ge(otl_ready, g)
            pe.wait_ge(v_moved, 4 * m + (2 if p < 4 else 4))
            for h in range(2):
                cols = slice((2 * p + h) * DH, (2 * p + h + 1) * DH)
                o = [ps_o[:, t * P + h * DH:t * P + (h + 1) * DH] for t in range(TILES)]
                pe.matmul(o[0], probsT[:, h, 0:P], v[:, 0, cols], start=True, stop=True)
                pe.matmul(o[1], probsT[:, h, P:2 * P], v[:, 0, cols], start=True, stop=False)
                mm = pe.matmul(o[1], probsT[:, h, 2 * P:3 * P], v[:, 1, cols], start=False, stop=True)
            mm.then_inc(pv_done, 1)

        def turn_probs(g):
            pe.wait_ge(exp_done, g + 1)
            for h in range(2):
                if later(g):
                    pe.wait_ge(pt_moved, 2 * (g - 1) + h + 1)
                for b in range(3):
                    mm = pe.transpose(ps_pt[h][:, b * P:(b + 1) * P], probs[:, h, b * P:(b + 1) * P], ident[:])
                mm.then_inc(pt_done, 1)

        def scores(g, p, m):
            pe.wait_ge(tr_moved, 8 * m + (4 if p < 4 else 8))
            for h in range(2):
                if later(g):
                    pe.wait_ge(sim_masked, 2 * (g - 1) + h + 1)
                rows = slice(h * DH, (h + 1) * DH)
                pe.matmul(ps_sim[h][:, 0:P], qkT[rows, 0, p, 0:P], qkT[rows, 1, p, 0:P], start=True, stop=True)
                mm = pe.matmul(ps_sim[h][:, P:SPANS], qkT[rows, 0, p, P:2 * P], qkT[rows, 1, p, WINDOW:SEQ],
                               start=True, stop=True)
                mm.then_inc(sim_done, 1)

        def turn_outputs(g):
            pe.wait_ge(o_ready, g + 1)
            for t in range(TILES):
                mm = pe.transpose(ps_o[:, t * P:(t + 1) * P], o_tok[:, t, :], ident[:])
            mm.then_inc(ot_done, 1)

        def step(n):
            for j in range(PAIRS):
                g = PAIRS * (n - 1) + j
                if pair_on(g - 2):
                    weigh_values(g - 2, (j - 2) % PAIRS, n - 1 if j >= 2 else n - 2)
                if j == 1 and on(n - 3):
                    w2_part(n - 3, 2)
                if pair_on(g - 1):
                    turn_probs(g - 1)
                if pair_on(g):
                    scores(g, j, n - 1)
                uses = USES[j]
                dense(n, *uses[0])
                dense(n, *uses[1])
                if pair_on(g - 2):
                    turn_outputs(g - 2)
                for u in uses[2:]:
                    dense(n, *u)

        pe.wait_ge(const_in, 16 * CONSTS)
        for n in EDGES[0]:
            step(n)
        with pe.Fori(*FULL) as n:
            step(n)
        for n in EDGES[1]:
            step(n)

    @block.vector
    def _(dve):
        ve = nc.vector

        def outputs(g, r):
            dve.wait_ge(pv_done, g + 1)
            dve.wait_ge(rinv_ready, g + 1)
            if later(g):
                dve.wait_ge(ot_done, g)
            ve.tensor_tensor(o_tok[:].rearrange("p t (h d) -> p (t h) d", h=2),
                             ps_o[:, 0:2 * P].rearrange("p (a d) -> p a d", a=4),
                             rinv[:, r, :].unsqueeze(2).broadcast_to([P, 4, DH]), ALU.mult).then_inc(o_ready, 1)

        def invert_sums(g, r):
            dve.wait_ge(exp_done, g + 1)
            ve.reciprocal(rinv[:, r, :], rsum[:, r, :]).then_inc(rinv_ready, 1)

        def mask_and_max(g, p, r):
            for h in range(2):
                dve.wait_ge(sim_done, 2 * g + h + 1)
                if later(g):
                    dve.wait_ge(pt_done, 2 * (g - 1) + h + 1)
                settle(dve)
                ve.tensor_tensor_reduce(out=probs[:, h, 0:P], in0=ps_sim[h][:, 0:P], in1=mask[:, 0:P], scale=1.0,
                                        scalar=-1.0e30, op0=ALU.add, op1=ALU.max, accum_out=mx[:, r, h:h + 1])
                ve.tensor_tensor_reduce(out=probs[:, h, P + WINDOW:PCOLS], in0=ps_sim[h][:, P:SPANS],
                                        in1=mask[:, P:SPANS], scale=1.0, scalar=-1.0e30, op0=ALU.add, op1=ALU.max,
                                        accum_out=mx[:, r, 2 + h:3 + h]).then_inc(sim_masked, 1)
            dve.wait_ge(sim_masked, 2 * g + 2)
            ve.scalar_tensor_tensor(out=nbias[:, r, :], in0=mx[:, r, :], scalar=-1.0, in1=qsc[:, p, :],
                                    op0=ALU.mult, op1=ALU.mult).then_inc(bias_ready, 1)

        def low_outputs(g, r):
            dve.wait_ge(oth_ready, g + 1)
            ve.tensor_tensor(otl[:, r, :], ps_o[:, 0:SEQ], oth[:, r, :].bitcast(F32), ALU.subtract).then_inc(otl_ready, 1)

        def y_of(m):
            return y[:, bass.ds(sample(m) * TILES * DIM, TILES * DIM)]

        def evacuate(n, use, idx, lag):
            m = n - lag
            if not on(m):
                return
            bank_ = bank(use, idx)
            if use == "wo":
                dve.wait_ge(wo_done, 4 * m + idx + 1)
                dve.wait_ge(y_ready, m + 1)
                if idx:
                    dve.wait_ge(y_added, 4 * m + idx)
                ve.tensor_tensor(y_of(m), bank_[:], y_of(m), ALU.add).then_inc(y_added, 1)
            elif use == "xt":
                dve.wait_ge(xth_ready, m + 1)
                ve.tensor_tensor(xtl[:, 0, 0:SEQ], bank_[:, 0:SEQ], xth[:, 0, 0:SEQ].bitcast(F32), ALU.subtract)
                ve.tensor_tensor(xtl[:, 1, 1:SEQ + 1], bank_[:, SEQ:2 * SEQ], xth[:, 1, 1:SEQ + 1].bitcast(F32),
                                 ALU.subtract).then_inc(xtl_ready, 1)
            elif use == "qk":
                which, t = (idx % 4) // 2, idx % 2
                i = 8 * m + idx
                ps4 = bank_[:].rearrange("p (e s d) -> p e s d", s=2, d=32)
                tmp4 = rot_tmp[:].rearrange("p (e s d) -> p e s d", s=2, d=32)
                if idx == QA:
                    dve.wait_ge(rope_ready, layer(m) + 1)
                dve.wait_ge(sq_ready, i + 1)
                if idx < 4 and later(m):
                    dve.wait_ge(tr_done, 8 * m - (2 if which == 0 else 0))
                if idx >= 4:
                    dve.wait_ge(tr_done, 8 * m + (2 if which == 0 else 4))
                ve.tensor_tensor(qk_tok[:, which, t, :].rearrange("p (e d) -> p e d", d=DH),
                                 bank_[:].rearrange("p (e d) -> p e d", d=DH),
                                 rope[:, which, 0, t, :].unsqueeze(1).broadcast_to([P, 8, DH]), ALU.mult)
                if later(i):
                    dve.wait_ge(qk_rotated, i)
                for s in range(2):
                    mm = ve.tensor_tensor(tmp4[:, :, s, :], ps4[:, :, 1 - s, :],
                                          rope[:, which, 1, t, 32 * s:32 * s + 32].unsqueeze(1).broadcast_to([P, 8, 32]),
                                          ALU.mult)
                mm.then_inc(rot_part, 1)
                if t == 0 and which == 0 and (idx >= 4 or later(m)):
                    dve.wait_ge(rn_ready, 2 * m + (1 if idx >= 4 else 0))
                ve.tensor_reduce(ss[:, which, :].rearrange("p (a b c) -> p a b c", a=4, b=2)[:, :, t, :],
                                 squares[:].rearrange("p (a c d) -> p a c d", a=4, c=2), AX.X, ALU.add).then_inc(qk_free, 1)
                dve.wait_ge(rot_part, i + 1)
                ve.tensor_tensor(qk_tok[:, which, t, :], qk_tok[:, which, t, :], rot_tmp[:], ALU.add).then_inc(qk_rotated, 1)
            elif use == "xnt":
                lp = layer(m) * NPRM
                dve.wait_ge(xnt_done, m + 1)
                pf = prm[:].rearrange("p l c -> p (l c)")
                for k in range(KD):
                    mm = ve.tensor_scalar(xn[:, k, :], bank_[:, k * SEQ:(k + 1) * SEQ], pf[:, bass.ds(lp + k, 1)],
                                          pf[:, bass.ds(lp + KD + k, 1)], ALU.mult, ALU.add)
                mm.then_inc(xnf_ready, 1)
            elif use in ("gate", "up"):
                pf = prm[:].rearrange("p l c -> p (l c)")
                b = layer(m) * NPRM + 2 * KD + (FT if use == "up" else 0)
                dve.wait_ge(gate_done if use == "gate" else up_done, 3 * m + idx + 1)
                if (use, idx) == ("gate", 0) and later(m):
                    dve.wait_ge(hl_ready, 3 * m)
                if (use, idx) == ("up", 0):
                    dve.wait_ge(gelu_done, m + 1)
                for i in range(2):
                    f = 2 * idx + i
                    src = bank_[0:FP, i * SEQ:(i + 1) * SEQ]
                    bias = pf[0:FP, bass.ds(b + f, 1)]
                    if use == "gate":
                        mm = ve.tensor_scalar(hid[0:FP, f, :], src, bias, None, ALU.add)
                    else:
                        mm = ve.scalar_tensor_tensor(out=hid[0:FP, f, :], in0=src, scalar=bias, in1=hid[0:FP, f, :],
                                                     op0=ALU.add, op1=ALU.mult)
                mm.then_inc(gate_ready if use == "gate" else h_ready, 1)

        def low_hidden(m, i):
            dve.wait_ge(hh_ready, 3 * m + i + 1)
            ve.tensor_tensor(hl[0:FP, i % 2], hid[0:FP, 2 * i:2 * i + 2, :], hh[0:FP, i % 2].bitcast(F32),
                             ALU.subtract).then_inc(hl_ready, 1)

        def low_rows(m):
            dve.wait_ge(xnh_ready, m + 1)
            ve.tensor_tensor(xnl[:], xn[:], xnh[:].bitcast(F32), ALU.subtract).then_inc(xnl_ready, 1)
            dve.wait_ge(xnl_ready, m + 1)
            ve.memset(xn[0:1, 0, P:2 * P], 0.0).then_inc(xn_free, 1)

        def norm_keys(m, c):
            dve.wait_ge(rn_ready, 2 * m + c + 1)
            dve.wait_ge(qk_rotated, 8 * m + 4 * c + 4)
            for t in range(TILES):
                kt = qk_tok[:, 1, t, :].rearrange("p (a c d) -> p a c d", a=4, c=2)
                ve.tensor_tensor(kt, kt, rn[:, 1, :].rearrange("p (a b c) -> p a b c", a=4, b=2)[:, :, t, :]
                                 .unsqueeze(3).broadcast_to([P, 4, 2, DH]), ALU.mult).then_inc(kn_ready, 1)
            if later(m):
                dve.wait_ge(exp_done, PAIRS * (m - 1) + 4 * (c + 1))
            ve.tensor_scalar(qsc[:, 4 * c:4 * c + 4, :], rn[:, 0, :].rearrange("p (a b) -> p a b", a=4), QKS, None,
                             ALU.mult).then_inc(qsc_ready, 1)

        def row_stats(m):
            dve.wait_ge(y_added, 4 * m + 4)
            dve.wait_ge(shift_in, 48 * (m + 1))
            settle(dve)
            for t in range(TILES):
                ve.bn_stats(bst[:, t, 0, :], y[:, bass.ds(sample(m) * TILES * DIM + t * DIM, P)])
                mm = ve.bn_stats(bst[:, t, 1, :], xn[:, t, P:2 * P])
            mm.then_inc(stats_ready, 1)
            dve.wait_ge(stats_ready, m + 1)
            settle(dve)
            for t in range(TILES):
                mm = ve.bn_aggr(mv[:, t, :], bst[:, t].rearrange("p a b -> p (a b)"))
            mm.then_inc(mv_ready, 1)

        def norm_rows(m):
            dve.wait_ge(rstd_ready, m + 1)
            for t in range(TILES):
                ve.tensor_scalar(xn[:, t, 0:P], y[:, bass.ds(sample(m) * TILES * DIM + t * DIM, P)], mv[:, t, 0:1],
                                 rstd[:, t:t + 1], ALU.subtract, ALU.mult)
                mm = ve.tensor_scalar(xn[:, t, P:2 * P], xn[:, t, P:2 * P], mv[:, t, 0:1],
                                      rstd[:, t:t + 1], ALU.subtract, ALU.mult)
            mm.then_inc(xn_ready, 1)

        def add_ffn(m):
            dve.wait_ge(w2_done, 3 * m + 3)
            ve.tensor_tensor(y_of(m), bank("w2", 0)[:], y_of(m), ALU.add).then_inc(y_summed, 1)
            dve.wait_ge(y_summed, m + 1)
            dve.wait_ge(b2_in, 16 * (layer(m) + 1))
            y3 = y_of(m).rearrange("p (t d) -> p t d", t=TILES)
            ve.tensor_tensor(y3, y3, b2[:].unsqueeze(1).broadcast_to([P, TILES, DIM]), ALU.add).then_inc(y_ready, 1)

        def step(n):
            for j in range(PAIRS):
                g = PAIRS * (n - 1) + j
                if j == 0 and on(n - 3):
                    low_hidden(n - 3, 1)
                if pair_on(g - 2):
                    outputs(g - 2, (j - 2) % 4)
                if j == 1 and on(n - 3):
                    add_ffn(n - 3)
                if j == 4 and on(n - 2):
                    norm_rows(n - 2)
                if pair_on(g - 1):
                    invert_sums(g - 1, (j - 1) % 4)
                if pair_on(g):
                    mask_and_max(g, j, j % 4)
                uses = USES[j]
                for u in uses[:2]:
                    evacuate(n, *u)
                if pair_on(g - 2):
                    low_outputs(g - 2, (j - 2) % 4)
                if j == 3 and on(n - 2):
                    row_stats(n - 2)
                if j == 4 and on(n - 2):
                    low_rows(n - 2)
                if j == 6 and on(n):
                    norm_keys(n, 0)
                if j == 7 and on(n - 2):
                    low_hidden(n - 2, 0)
                for u in uses[2:]:
                    evacuate(n, *u)
                if j == 0 and on(n - 3):
                    low_hidden(n - 3, 2)
                if j == 2 and on(n - 1):
                    norm_keys(n - 1, 1)

        for h in range(2):
            ve.memset(probs[:, h, P:P + WINDOW], 0.0).then_inc(zeroed, 1)
        ve.memset(xth[:, 1, 0:1].bitcast(F32), 0.0).then_inc(zeroed, 1)
        ve.memset(xtl[:, 1, 0:1].bitcast(F32), 0.0).then_inc(zeroed, 1)
        ve.memset(xn[0:1, 0, P:2 * P], 0.0).then_inc(xn_free, 1)
        ve.memset(mx[:], 0.0).then_inc(y_ready, BATCH)
        dve.wait_ge(const_in, 16 * CONSTS)
        for n in EDGES[0]:
            step(n)
        with dve.Fori(*FULL) as n:
            step(n)
        for n in EDGES[1]:
            step(n)

    @block.scalar
    def _(act):
        sc = nc.scalar

        def move_turned(g):
            for h in range(2):
                act.wait_ge(pt_done, 2 * g + h + 1)
                if later(g):
                    act.wait_ge(pv_done, g)
                sc.copy(probsT[:, h, :], ps_pt[h][:, 0:PCOLS]).then_inc(pt_moved, 1)

        def exponentials(g, p, r):
            act.wait_ge(bias_ready, g + 1)
            for t in range(TILES):
                for h in range(2):
                    part = probs[:, h, 0:P] if t == 0 else probs[:, h, P + WINDOW:PCOLS]
                    c = 2 * t + h
                    mm = sc.activation(part, part, ACT.Exp, bias=nbias[:, r, c:c + 1], scale=qsc[:, p, c:c + 1],
                                       accum_out=rsum[:, r, c:c + 1])
            mm.then_inc(exp_done, 1)

        def high_outputs(g, r, m, p):
            act.wait_ge(ot_done, g + 1)
            if later(g, 3):
                act.wait_ge(wo_done, 4 * m + p // 2 - 1)
            sc.copy(oth[:, r, :], ps_o[:, 0:SEQ]).then_inc(oth_ready, 1)

        def evacuate(n, use, idx, lag):
            m = n - lag
            if not on(m):
                return
            bank_ = bank(use, idx)
            if use == "qk":
                i = 8 * m + idx
                act.wait_ge(qk_done, i + 1)
                if later(i):
                    act.wait_ge(qk_free, i)
                sc.activation(squares[:], bank_[:], ACT.Square).then_inc(sq_ready, 1)
            elif use == "v":
                c, t = idx // 2, idx % 2
                act.wait_ge(v_done, 4 * m + idx + 1)
                if later(m):
                    act.wait_ge(pv_done, PAIRS * (m - 1) + 4 * (c + 1))
                sc.copy(v[:, t, c * 512:(c + 1) * 512], bank_[:]).then_inc(v_moved, 1)
            elif use == "tr":
                c, which, t = idx // 4, (idx % 4) // 2, idx % 2
                act.wait_ge(tr_done, 8 * m + idx + 1)
                if later(m):
                    act.wait_ge(sim_done, 2 * (PAIRS * (m - 1) + 4 * (c + 1)))
                sc.copy(qkT[:, which, 4 * c:4 * c + 4, t * P:(t + 1) * P],
                        bank_[:].rearrange("p (a q) -> p a q", a=4)).then_inc(tr_moved, 1)
            elif use == "xt":
                act.wait_ge(xt_done, m + 1)
                if later(m):
                    act.wait_ge(v_done, 4 * m)
                sc.copy(xth[:, 0, 0:SEQ], bank_[:, 0:SEQ])
                sc.copy(xth[:, 1, 1:SEQ + 1], bank_[:, SEQ:2 * SEQ]).then_inc(xth_ready, 1)
            elif use == "xnt":
                act.wait_ge(xnf_ready, m + 1)
                if later(m):
                    act.wait_ge(up_done, 3 * m)
                sc.copy(xnh[:], xn[:]).then_inc(xnh_ready, 1)
            elif use == "up":
                i = idx
                act.wait_ge(h_ready, 3 * m + i + 1)
                if i == 2:
                    act.wait_ge(w2_done, 3 * m + 1)
                elif later(m):
                    act.wait_ge(w2_done, 3 * m)
                sc.copy(hh[0:FP, i % 2], hid[0:FP, 2 * i:2 * i + 2, :]).then_inc(hh_ready, 1)

        def gelu(m):
            act.wait_ge(gate_ready, 3 * m + 3)
            sc.activation(hid[0:FP], hid[0:FP], ACT.Gelu).then_inc(gelu_done, 1)

        def step(n):
            for j in range(PAIRS):
                g = PAIRS * (n - 1) + j
                uses = USES[j]
                if pair_on(g - 1):
                    move_turned(g - 1)
                evacuate(n, *uses[0])
                if pair_on(g):
                    exponentials(g, j, j % 4)
                evacuate(n, *uses[1])
                if pair_on(g - 2):
                    high_outputs(g - 2, (j - 2) % 4, n - 1 if j >= 2 else n - 2, (j - 2) % PAIRS)
                for u in uses[2:]:
                    evacuate(n, *u)
                if j == 6 and on(n - 2):
                    gelu(n - 2)

        act.wait_ge(zeroed, 4)
        for n in EDGES[0]:
            step(n)
        with act.Fori(*FULL) as n:
            step(n)
        for n in EDGES[1]:
            step(n)

    @block.gpsimd
    def _(pool):
        gp = nc.gpsimd

        def load_unit(l, u):
            i = NU * l + u
            pool.wait_ge(w_ready, i - (1 if u else 0))
            src = d_w[:, bass.ds(WCOLS * l + OFFS[u], UNITS[u])]
            pool.dma_start(raw[:, u % 2, 0:UNITS[u]], src).then_inc(raw_in[u % 2], 16)

        def split_unit(l, u):
            i = NU * l + u
            part = slice(OFFS[u], OFFS[u] + UNITS[u])
            src = raw[:, u % 2, 0:UNITS[u]]
            pool.wait_ge(raw_in[u % 2], 16 * (len(range(u % 2, NU, 2)) * (l - 1) + u // 2 + 1))
            settle(pool)
            gp.tensor_copy(wh[:, part], src).then_inc(w_hi, 1)
            pool.wait_ge(w_hi, i + 1 - NU)
            gp.tensor_tensor(wl[:, part], src, wh[:, part].bitcast(F32), ALU.subtract).then_inc(w_ready, 1)

        def freed(m, u):
            if u < U_QKV + 8:
                return qk_done, 8 * m + 2 * (u // 2) + 2
            if u < U_WO:
                return v_done, 4 * m + 2 * ((u - 8) // 2) + 2
            if u < U_GATE:
                return wo_done, 4 * m + u - U_WO + 1
            if u < U_UP:
                return gate_done, 3 * m + u - U_GATE + 1
            if u < U_W2:
                return up_done, 3 * m + u - U_UP + 1
            return w2_done, 3 * m + u - U_W2 + 1

        def reload(l, units):
            for u in units:
                if u + 1 < NU:
                    load_unit(l, u + 1)
                pool.wait_ge(*freed(BATCH * l - 1, u))
                split_unit(l, u)

        def rope_tables(l):
            pool.wait_ge(qks_in, 16 * (l + 1))
            if later(l):
                pool.wait_ge(qk_rotated, 8 * BATCH * l)
            settle(pool)
            gp.tensor_scalar(qks_swapped[:, :, 0, :], qks[:, :, 1, :], -1.0, 1.0, ALU.mult, ALU.mult)
            gp.tensor_copy(qks_swapped[:, :, 1, :], qks[:, :, 0, :]).then_inc(rope_part, 1)
            pool.wait_ge(rope_part, l + 1)
            for w in range(2):
                for f, scales in enumerate((qks, qks_swapped)):
                    for t in range(TILES):
                        mm = gp.tensor_tensor(rope[:, w, f, t, :].rearrange("p (s d) -> p s d", s=2), scales[:, w],
                                              rope_base[:, 2 * w + f, t, :].unsqueeze(1).broadcast_to([P, 2, 32]),
                                              ALU.mult)
            mm.then_inc(rope_ready, 1)

        def inverse_norms(m, c):
            i = 2 * m + c
            pool.wait_ge(qk_free, 8 * m + 4 * c + 4)
            settle(pool)
            gp.tensor_scalar(ssc[:], ss[:], 1e-24, 3.0e38, ALU.max, ALU.min).then_inc(rn_part, 1)
            pool.wait_ge(rn_part, i + 1)
            if later(i):
                pool.wait_ge(qsc_ready, i)
            gp.tensor_tensor(rn[:].rearrange("p a b -> p (a b)"), ssc[:].rearrange("p a b -> p (a b)"), minus_half[:],
                             ALU.pow).then_inc(rn_ready, 1)

        def inverse_deviation(m):
            pool.wait_ge(mv_ready, m + 1)
            settle(pool)
            gp.tensor_scalar(vareps[:], mv[:, :, 1], 1.0, EPS, ALU.mult, ALU.add).then_inc(rs_part, 1)
            pool.wait_ge(rs_part, m + 1)
            gp.tensor_tensor(rstd[:], vareps[:], minus_half[:, 0:TILES], ALU.pow).then_inc(rstd_ready, 1)

        def step(n, l=None, part=None):
            if part == 1:
                reload(l, range(4, 6))
            if part == 3:
                reload(l, range(U_UP, U_W2))
            if on(n - 1):
                inverse_norms(n - 1, 1)
            if part == 1:
                rope_tables(l)
                reload(l, range(6, 8))
            if part == 2:
                reload(l, range(U_WO + 2, U_WO + 4))
            if part == 3:
                reload(l, range(U_W2, NU))
            if on(n - 2):
                inverse_deviation(n - 2)
            if part == 1:
                reload(l, range(8, U_WO))
            if on(n):
                inverse_norms(n, 0)
            if part == 0:
                load_unit(l, 0)
                reload(l, range(0, 4))
            if part == 1:
                reload(l, range(U_WO, U_WO + 2))
            if part == 2:
                reload(l, range(U_GATE, U_UP))

        gp.memset(minus_half[:], -0.5).then_inc(minus_ready, 1)
        pool.wait_ge(minus_ready, 1)
        gp.memset(ssc[:], 0.0).then_inc(w_ready, NU)
        pool.wait_ge(w_ready, NU)
        pool.wait_ge(const_in, 16 * CONSTS)
        rope_tables(0)
        for n in EDGES[0]:
            step(n)
        with pool.Fori(0, DEPTH - 1) as o:
            for s in range(BATCH):
                part = s - (BATCH - 1 - FULL[0])
                step(BATCH * o + FULL[0] + s, o + 1, part if part >= 0 else None)
        with pool.Fori(BATCH * (DEPTH - 1) + FULL[0], FULL[1]) as n:
            step(n)
        for n in EDGES[1]:
            step(n)

    @block.sync
    def _(sp):
        y5 = y[:].rearrange("p (s t d) -> p s t d", s=BATCH, t=TILES)

        def step(n):
            if on(n):
                sp.wait_ge(y_ready, n + 1)
                settle(sp)
                if later(n):
                    sp.wait_ge(xt_done, n)
                settle(sp)
                sp.dma_start(ycur[:].rearrange("p t d -> p (t d)"),
                             y[:, bass.ds(sample(n) * TILES * DIM, TILES * DIM)]).then_inc(ycur_in, 16)
            m = n - 2
            if on(m):
                sp.wait_ge(y_added, 4 * m + 4)
                settle(sp)
                sp.wait_ge(xn_free, m + 1)
                settle(sp)
                at = sample(m) * TILES * DIM
                for t in range(TILES):
                    sp.dma_start(xn[1:P, t, P:2 * P], y[0:P - 1, bass.ds(at + t * DIM + P, P)]).then_inc(shift_in, 16)
                sp.dma_start(xn[0:1, 1, P:2 * P], y[P - 1:P, bass.ds(at + P, P)]).then_inc(shift_in, 16)

        def load_scales(l):
            if later(l):
                sp.wait_ge(rope_ready, l)
                settle(sp)
            sp.dma_start(qks[:].rearrange("p a s d -> p (a s d)"), d_qks[:, bass.ds(2 * DH * l, 2 * DH)]).then_inc(qks_in, 16)

        def load_b2(l):
            if later(l):
                sp.wait_ge(y_ready, BATCH * l + BATCH)
                settle(sp)
            sp.dma_start(b2[:], d_b2[:, bass.ds(DIM * l, DIM)]).then_inc(b2_in, 16)

        sp.dma_start(rope_base[:], d_const[:, 0:4 * TILES * 32].rearrange("p (a t d) -> p a t d", a=4, t=TILES)).then_inc(const_in, 16)
        sp.dma_start(mask[:], d_const[:, 4 * TILES * 32:4 * TILES * 32 + SPANS]).then_inc(const_in, 16)
        sp.dma_start(ident[:], d_const[:, 4 * TILES * 32 + SPANS:4 * TILES * 32 + SPANS + P]).then_inc(const_in, 16)
        sp.dma_start(prm[:].rearrange("p l c -> p (l c)"), d_prm).then_inc(const_in, 16)
        load_scales(0)
        load_b2(0)
        for n in EDGES[0]:
            step(n)
        with sp.Fori(0, DEPTH - 1) as o:
            for s in range(BATCH):
                step(BATCH * o + FULL[0] + s)
                if s == 0:
                    load_scales(o + 1)
                if s == BATCH - 1:
                    load_b2(o + 1)
        with sp.Fori(BATCH * (DEPTH - 1) + FULL[0], FULL[1]) as n:
            step(n)
        for n in EDGES[1]:
            step(n)


XHEADS = 16
XDH = DIM // XHEADS
XPAIRS = XHEADS // 2
XW = 4 * DIM
HID = 768
HT = HID // P
DW_UNITS = 3 * KD * HID // 512


def attend_phase(nc, ctx, y, d_x, d_ctx, d_w, d_bias, d_ident, d_sum, first, pool_jobs):

    tag = "a_" if first else "c_"

    def sb(name, shape, dt=F32):
        return ctx.enter_context(nc.sbuf_tensor(tag + name, shape, dt))

    def sem(name):
        return nc.alloc_semaphore(tag + name)

    ident = sb("ident", [P, P])
    w_raw = sb("w_raw", [P, KD, XW])
    w_h, w_l = sb("w_h", [P, KD, XW], F32R), sb("w_l", [P, KD, XW], F32R)
    bias = sb("bias", [P, XW])
    x_in_tile = None if first else sb("x_in_tile", [P, TILES * DIM])
    c_in_tile = sb("c_in_tile", [P, TILES, DIM])
    z = sb("z", [P, TILES, DIM])
    bst = sb("bst", [P, 2, TILES, 6])
    mv = sb("mv", [P, 2, TILES, 2])
    vareps = sb("vareps", [P, 2, TILES])
    rstd = sb("rstd", [P, 2, TILES])
    minus_half = sb("minus_half", [P, TILES])
    zTh, zTl = sb("zTh", [P, KD, SEQ], F32R), sb("zTl", [P, KD, SEQ], F32R)
    cTh, cTl = sb("cTh", [P, KD, SEQ], F32R), sb("cTl", [P, KD, SEQ], F32R)
    qk = sb("qk", [P, 2, XHEADS, XDH])
    parts = sb("parts", [P, TILES, 2, XHEADS, 2, 2, XDH], F32R)
    stacked = sb("stacked", [P, XPAIRS, 2, SEQ], F32R)
    v = sb("v", [P, TILES, DIM])
    probs = sb("probs", [P, 2, TILES, SEQ])
    probsT = sb("probsT", [P, 2, 2, SEQ])
    nmax = sb("nmax", [P, 4, 2, TILES])
    rsum = sb("rsum", [P, TILES, XHEADS])
    rinv = sb("rinv", [P, TILES, XHEADS])
    o_tok = sb("o_tok", [P, KD, TILES, P])
    oth, otl = sb("oth", [P, KD, SEQ], F32R), sb("otl", [P, KD, SEQ], F32R)

    def bank(name):
        return ctx.enter_context(nc.psum_tensor(tag + name, [P, 512], F32))

    ps_sim = [bank("ps_sim0"), bank("ps_sim1")]
    ps_pt = [bank("ps_pt0"), bank("ps_pt1")]
    ps_o = [bank("ps_o0"), bank("ps_o1")]
    ps_mm = [bank("ps_mm0"), bank("ps_mm1")]

    zt_done, ct_done, proj_done, v_done = sem("zt_done"), sem("ct_done"), sem("proj_done"), sem("v_done")
    st_done, sim_done, pt_done, pv_done = sem("st_done"), sem("sim_done"), sem("pt_done"), sem("pv_done")
    ot_done, wo_done = sem("ot_done"), sem("wo_done")
    x_ready, stats_ready, mv_ready, z_ready = sem("x_ready"), sem("stats_ready"), sem("mv_ready"), sem("z_ready")
    ztl_ready, ctl_ready, qk_biased, parts_l = sem("ztl_ready"), sem("ctl_ready"), sem("qk_biased"), sem("parts_l")
    v_ready, st_moved, max_ready, pt_moved_b = sem("v_ready"), sem("st_moved"), sem("max_ready"), sem("pt_moved_b")
    rinv_ready, o_ready, otl_ready, wo_read = sem("rinv_ready"), sem("o_ready"), sem("otl_ready"), sem("wo_read")
    x_summed, stats2_ready, mv2_ready, y_normed = (sem("x_summed"), sem("stats2_ready"), sem("mv2_ready"),
                                                   sem("y_normed"))
    wl_ready, bias_scaled = sem("wl_ready"), sem("bias_scaled")
    wh_ready, zth_ready, cth_ready, parts_h = sem("wh_ready"), sem("zth_ready"), sem("cth_ready"), sem("parts_h")
    exp_done, pt_moved_a, oth_ready = sem("exp_done"), sem("pt_moved_a"), sem("oth_ready")
    minus_ready, rs_part, rstd_ready, rs2_part, rstd2_ready = (sem("minus_ready"), sem("rs_part"), sem("rstd_ready"),
                                                               sem("rs2_part"), sem("rstd2_ready"))
    const_in, x_in, c_in, sum_out = sem("const_in"), sem("x_in"), sem("c_in"), sem("sum_out")

    block = ctx.enter_context(nc.Block())
    FULL = (2, BATCH)
    EDGES = (range(0, FULL[0]), range(FULL[1], BATCH + 2))

    def on(m):
        return not isinstance(m, int) or 0 <= m < BATCH

    def later(m, first_=0):
        return not isinstance(m, int) or m > first_

    def pair_on(g):
        return not isinstance(g, int) or 0 <= g < BATCH * XPAIRS

    def settle(eng):
        eng.nop(nofuse=True)

    USES = [
        [("st", 7, 1)],
        [("v", 0, 1)],
        [("zt", 0, 0), ("ct", 0, 0)],
        [("qk", 0, 0), ("qk", 1, 0), ("ot", 1, 2)],
        [("wo", 0, 2), ("st", 0, 0)],
        [("st", 1, 0), ("st", 2, 0)],
        [("ot", 0, 1), ("st", 3, 0), ("st", 4, 0)],
        [("st", 5, 0), ("st", 6, 0)],
    ]
    ORDER = [u for slot in USES for u in slot]
    assert len(ORDER) % 2 == 0
    FREED = {"st": (st_moved, 8), "v": (v_ready, 1), "zt": (ztl_ready, 1), "ct": (ctl_ready, 1), "qk": (qk_biased, 2),
             "ot": (otl_ready, 2), "wo": (wo_read, 1)}

    def mm_bank(use, idx):
        return ps_mm[[u[:2] for u in ORDER].index((use, idx)) % 2]

    def y_of(m):
        return y[:, bass.ds(m * TILES * DIM, TILES * DIM)]

    def part_views(t, w):
        if w == 0:
            return parts[:, t, w, :, :, 0, :], parts[:, t, w, :, :, 1, :]
        return parts[:, t, w, :, 0, :, :], parts[:, t, w, :, 1, :, :]

    @block.tensor
    def _(pe):
        def split3(out, lhs_h, lhs_l, rhs_h, rhs_l, start, stop):
            pe.matmul(out, lhs_h, rhs_h, start=start, stop=False)
            pe.matmul(out, lhs_h, rhs_l, start=False, stop=False)
            return pe.matmul(out, lhs_l, rhs_h, start=False, stop=stop)

        def dense(n, use, idx, lag):
            m = n - lag
            if not on(m):
                return
            bank_ = mm_bank(use, idx)
            at = [u[:2] for u in ORDER].index((use, idx))
            before, i, blag = ORDER[at - 2]
            bm = n - blag - (1 if at < 2 else 0)
            if on(bm):
                signal, per = FREED[before]
                pe.wait_ge(signal, per * bm + i + 1)
            if use in ("zt", "ct"):
                if use == "zt":
                    pe.wait_ge(z_ready, m + 1)
                else:
                    pe.wait_ge(c_in, 16 * (m + 1))
                src = z if use == "zt" else c_in_tile
                for k in range(KD):
                    for t in range(TILES):
                        mm = pe.transpose(bank_[:, k * SEQ + t * P:k * SEQ + (t + 1) * P],
                                          src[:, t, k * P:(k + 1) * P], ident[:])
                mm.then_inc(zt_done if use == "zt" else ct_done, 1)
            elif use == "qk":
                if idx == 0:
                    pe.wait_ge(ztl_ready, m + 1)
                    pe.wait_ge(ctl_ready, m + 1)
                t = idx
                for w, (h_, l_) in enumerate(((zTh, zTl), (cTh, cTl))):
                    for k in range(KD):
                        cols = slice(w * DIM, (w + 1) * DIM)
                        mm = split3(bank_[:, cols], h_[:, k, t * P:(t + 1) * P], l_[:, k, t * P:(t + 1) * P],
                                    w_h[:, k, cols], w_l[:, k, cols], k == 0, k == KD - 1)
                mm.then_inc(proj_done, 1)
            elif use == "v":
                cols = slice(2 * DIM, 3 * DIM)
                for t in range(TILES):
                    for k in range(KD):
                        mm = split3(bank_[:, t * DIM:(t + 1) * DIM], cTh[:, k, t * P:(t + 1) * P],
                                    cTl[:, k, t * P:(t + 1) * P], w_h[:, k, cols], w_l[:, k, cols], k == 0, k == KD - 1)
                mm.then_inc(v_done, 1)
            elif use == "st":
                pe.wait_ge(parts_l, 4 * m + 4)
                for w in range(2):
                    for t in range(TILES):
                        src = parts[:, t, w, 2 * idx:2 * idx + 2].bitcast(F32).rearrange("p h a b d -> p (h a b d)")
                        mm = pe.transpose(bank_[:, w * SEQ + t * P:w * SEQ + (t + 1) * P], src, ident[:])
                mm.then_inc(st_done, 1)
            elif use == "ot":
                pe.wait_ge(o_ready, 2 * m + idx + 1)
                for t in range(TILES):
                    mm = pe.transpose(bank_[:, t * P:(t + 1) * P], o_tok[:, idx, t, :], ident[:])
                mm.then_inc(ot_done, 1)
            elif use == "wo":
                pe.wait_ge(otl_ready, 2 * m + 2)
                cols = slice(3 * DIM, 4 * DIM)
                for t in range(TILES):
                    for k in range(KD):
                        mm = split3(bank_[:, t * DIM:(t + 1) * DIM], oth[:, k, t * P:(t + 1) * P],
                                    otl[:, k, t * P:(t + 1) * P], w_h[:, k, cols], w_l[:, k, cols], k == 0, k == KD - 1)
                mm.then_inc(wo_done, 1)

        def scores(g, p, m):
            pe.wait_ge(st_moved, 8 * m + p + 1)
            for h in range(2):
                if later(g):
                    pe.wait_ge(exp_done, 2 * (g - 1) + h + 1)
                rows = slice(64 * h, 64 * h + 64)
                for t in range(TILES):
                    mm = pe.matmul(ps_sim[h][:, t * SEQ:(t + 1) * SEQ], stacked[rows, p, 0, t * P:(t + 1) * P],
                                   stacked[rows, p, 1, :], start=True, stop=True)
                mm.then_inc(sim_done, 1)

        def turn_probs(g):
            for h in range(2):
                pe.wait_ge(exp_done, 2 * g + h + 1)
                if later(g):
                    pe.wait_ge(pt_moved_b if h else pt_moved_a, g)
                for c in range(2):
                    for t in range(TILES):
                        mm = pe.transpose(ps_pt[h][:, c * SEQ + t * P:c * SEQ + (t + 1) * P],
                                          probs[:, h, t, c * P:(c + 1) * P], ident[:])
                mm.then_inc(pt_done, 1)

        def weigh_values(g, p, m):
            pe.wait_ge(pt_moved_a, g + 1)
            pe.wait_ge(pt_moved_b, g + 1)
            if p == 0:
                pe.wait_ge(v_ready, m + 1)
            if p % 4 == 0 and later(m):
                pe.wait_ge(o_ready, 2 * (m - 1) + p // 4 + 1)
            for h in range(2):
                head = 2 * p + h
                for t in range(TILES):
                    out = ps_o[p // 4][:, t * P + (head % 8) * XDH:t * P + (head % 8 + 1) * XDH]
                    for c in range(2):
                        mm = pe.matmul(out, probsT[:, h, c, t * P:(t + 1) * P], v[:, c, head * XDH:(head + 1) * XDH],
                                       start=(c == 0), stop=(c == 1))
            mm.then_inc(pv_done, 1)

        def step(n):
            for j in range(XPAIRS):
                g = XPAIRS * (n - 1) + j
                if pair_on(g - 2):
                    weigh_values(g - 2, (j - 2) % XPAIRS, n - 1 if j >= 2 else n - 2)
                if pair_on(g - 1):
                    turn_probs(g - 1)
                if pair_on(g):
                    scores(g, j, n - 1)
                for u in USES[j]:
                    dense(n, *u)

        pe.wait_ge(const_in, 16 * 3)
        pe.wait_ge(wl_ready, KD)
        for n in EDGES[0]:
            step(n)
        with pe.Fori(*FULL) as n:
            step(n)
        for n in EDGES[1]:
            step(n)

    @block.vector
    def _(dve):
        ve = nc.vector

        def stats(m, which, signal, out_signal):
            for t in range(TILES):
                mm = ve.bn_stats(bst[:, which, t, :], y[:, bass.ds(m * TILES * DIM + t * DIM, DIM)])
            mm.then_inc(signal, 1)
            dve.wait_ge(signal, m + 1)
            settle(dve)
            for t in range(TILES):
                mm = ve.bn_aggr(mv[:, which, t, :], bst[:, which, t, :])
            mm.then_inc(out_signal, 1)

        def rows_in(m):
            dve.wait_ge(x_in, 16 * (m + 1))
            if not first:
                ve.tensor_tensor(y_of(m), y_of(m), x_in_tile[:], ALU.add).then_inc(x_ready, 1)
                dve.wait_ge(x_ready, m + 1)
            settle(dve)
            stats(m, 0, stats_ready, mv_ready)

        def norm_in(m):
            dve.wait_ge(rstd_ready, m + 1)
            if later(m):
                dve.wait_ge(zt_done, m)
            for t in range(TILES):
                mm = ve.tensor_scalar(z[:, t, :], y[:, bass.ds(m * TILES * DIM + t * DIM, DIM)], mv[:, 0, t, 0:1],
                                      rstd[:, 0, t:t + 1], ALU.subtract, ALU.mult)
            mm.then_inc(z_ready, 1)

        def norm_out(m):
            dve.wait_ge(rstd2_ready, m + 1)
            dve.wait_ge(sum_out, 16 * (m + 1))
            for t in range(TILES):
                yt = y[:, bass.ds(m * TILES * DIM + t * DIM, DIM)]
                mm = ve.tensor_scalar(yt, yt, mv[:, 1, t, 0:1], rstd[:, 1, t:t + 1], ALU.subtract, ALU.mult)
            mm.then_inc(y_normed, 1)

        def evacuate(n, use, idx, lag):
            m = n - lag
            if not on(m):
                return
            bank_ = mm_bank(use, idx)
            if use in ("zt", "ct"):
                hi, lo, got, done = ((zTh, zTl, zth_ready, ztl_ready) if use == "zt" else
                                     (cTh, cTl, cth_ready, ctl_ready))
                dve.wait_ge(got, m + 1)
                ve.tensor_tensor(lo[:].rearrange("p k s -> p (k s)"), bank_[:],
                                 hi[:].bitcast(F32).rearrange("p k s -> p (k s)"), ALU.subtract).then_inc(done, 1)
            elif use == "qk":
                i = 2 * m + idx
                dve.wait_ge(proj_done, i + 1)
                if later(i):
                    dve.wait_ge(parts_l, 2 * i)
                qkf = qk[:].rearrange("p w h d -> p w (h d)")
                ve.scalar_tensor_tensor(out=qkf[:, 0], in0=bank_[:, 0:DIM], scalar=XDH ** -0.5, in1=bias[:, 0:DIM],
                                        op0=ALU.mult, op1=ALU.add)
                ve.tensor_tensor(qkf[:, 1], bank_[:, DIM:2 * DIM], bias[:, DIM:2 * DIM], ALU.add).then_inc(qk_biased, 1)
                dve.wait_ge(parts_h, 2 * i + 2)
                for w in range(2):
                    hi, lo = part_views(idx, w)
                    src = qk[:, w].unsqueeze(2).broadcast_to([P, XHEADS, 2, XDH])
                    ve.tensor_tensor(lo, src, hi.bitcast(F32), ALU.subtract).then_inc(parts_l, 1)
            elif use == "v":
                dve.wait_ge(v_done, m + 1)
                if later(m):
                    dve.wait_ge(pv_done, XPAIRS * m)
                ve.tensor_tensor(v[:], bank_[:].rearrange("p (t d) -> p t d", t=TILES),
                                 bias[:, 2 * DIM:3 * DIM].unsqueeze(1).broadcast_to([P, TILES, DIM]),
                                 ALU.add).then_inc(v_ready, 1)
            elif use == "st":
                dve.wait_ge(st_done, 8 * m + idx + 1)
                if later(m):
                    dve.wait_ge(sim_done, 2 * (XPAIRS * (m - 1) + idx + 1))
                ve.tensor_copy(stacked[:, idx].rearrange("p w s -> p (w s)"), bank_[:]).then_inc(st_moved, 1)
            elif use == "ot":
                dve.wait_ge(oth_ready, 2 * m + idx + 1)
                ve.tensor_tensor(otl[:, idx, :], bank_[:, 0:SEQ], oth[:, idx, :].bitcast(F32),
                                 ALU.subtract).then_inc(otl_ready, 1)
            elif use == "wo":
                dve.wait_ge(wo_done, m + 1)
                ve.tensor_tensor(y_of(m), bank_[:], y_of(m), ALU.add).then_inc(wo_read, 1)
                dve.wait_ge(wo_read, m + 1)
                y3 = y_of(m).rearrange("p (t d) -> p t d", t=TILES)
                ve.tensor_tensor(y3, y3, bias[:, 3 * DIM:4 * DIM].unsqueeze(1).broadcast_to([P, TILES, DIM]),
                                 ALU.add).then_inc(x_summed, 1)
                if first:
                    dve.wait_ge(x_summed, m + 1)
                    settle(dve)
                    stats(m, 1, stats2_ready, mv2_ready)

        def maxima(g, r):
            for h in range(2):
                dve.wait_ge(sim_done, 2 * g + h + 1)
                ve.tensor_reduce(nmax[:, r, h, :], ps_sim[h][:].rearrange("p (t s) -> p t s", t=TILES), AX.X, ALU.max,
                                 negate=True).then_inc(max_ready, 1)

        def move_turned(g):
            dve.wait_ge(pt_done, 2 * g + 2)
            if later(g):
                dve.wait_ge(pv_done, g)
            ve.tensor_copy(probsT[:, 1].rearrange("p c s -> p (c s)"), ps_pt[1][:]).then_inc(pt_moved_b, 1)

        def outputs(m, k):
            heads = slice(8 * k, 8 * k + 8)
            ve.reciprocal(rinv[:, :, heads], rsum[:, :, heads]).then_inc(rinv_ready, 1)
            dve.wait_ge(rinv_ready, 2 * m + k + 1)
            if later(m):
                dve.wait_ge(ot_done, 2 * (m - 1) + k + 1)
            for t in range(TILES):
                mm = ve.tensor_tensor(o_tok[:, k, t, :].rearrange("p (h d) -> p h d", d=XDH),
                                      ps_o[k][:, t * P:(t + 1) * P].rearrange("p (h d) -> p h d", d=XDH),
                                      rinv[:, t, heads].unsqueeze(2).broadcast_to([P, 8, XDH]), ALU.mult)
            mm.then_inc(o_ready, 1)

        def step(n):
            for j in range(XPAIRS):
                g = XPAIRS * (n - 1) + j
                if j == 0 and on(n):
                    rows_in(n)
                if j == 1 and on(n):
                    norm_in(n)
                if j == 7 and first and on(n - 2):
                    norm_out(n - 2)
                if j == 2 and on(n - 2):
                    dve.wait_ge(pv_done, XPAIRS * (n - 1))
                    outputs(n - 2, 1)
                if j == 6 and on(n - 1):
                    dve.wait_ge(pv_done, XPAIRS * (n - 1) + 4)
                    outputs(n - 1, 0)
                if pair_on(g - 1):
                    move_turned(g - 1)
                if pair_on(g):
                    maxima(g, j % 4)
                for u in USES[j]:
                    evacuate(n, *u)

        dve.wait_ge(const_in, 16 * 3)
        ve.tensor_scalar(bias[:, 0:DIM], bias[:, 0:DIM], XDH ** -0.5, None, ALU.mult).then_inc(bias_scaled, 1)
        dve.wait_ge(bias_scaled, 1)
        for k in range(KD):
            dve.wait_ge(wh_ready, k + 1)
            ve.tensor_tensor(w_l[:, k, :], w_raw[:, k, :], w_h[:, k, :].bitcast(F32), ALU.subtract).then_inc(wl_ready, 1)
        for n in EDGES[0]:
            step(n)
        with dve.Fori(*FULL) as n:
            step(n)
        for n in EDGES[1]:
            step(n)

    @block.scalar
    def _(act):
        sc = nc.scalar

        def exponentials(g, p, r):
            for h in range(2):
                act.wait_ge(max_ready, 2 * g + h + 1)
                if later(g):
                    act.wait_ge(pt_done, 2 * (g - 1) + h + 1)
                for t in range(TILES):
                    head = 2 * p + h
                    mm = sc.activation(probs[:, h, t, :], ps_sim[h][:, t * SEQ:(t + 1) * SEQ], ACT.Exp,
                                       bias=nmax[:, r, h, t:t + 1], accum_out=rsum[:, t, head:head + 1])
                mm.then_inc(exp_done, 1)

        def move_turned(g):
            act.wait_ge(pt_done, 2 * g + 1)
            if later(g):
                act.wait_ge(pv_done, g)
            sc.copy(probsT[:, 0].rearrange("p c s -> p (c s)"), ps_pt[0][:]).then_inc(pt_moved_a, 1)

        def evacuate(n, use, idx, lag):
            m = n - lag
            if not on(m):
                return
            bank_ = mm_bank(use, idx)
            if use in ("zt", "ct"):
                hi, done, ready = (zTh, zt_done, zth_ready) if use == "zt" else (cTh, ct_done, cth_ready)
                act.wait_ge(done, m + 1)
                if later(m):
                    act.wait_ge(v_done, m)
                sc.copy(hi[:].rearrange("p k s -> p (k s)"), bank_[:]).then_inc(ready, 1)
            elif use == "qk":
                i = 2 * m + idx
                act.wait_ge(qk_biased, i + 1)
                if later(m):
                    act.wait_ge(st_done, 8 * m)
                for w in range(2):
                    sc.copy(part_views(idx, w)[0], qk[:, w].unsqueeze(2).broadcast_to([P, XHEADS, 2, XDH])).then_inc(parts_h, 1)
            elif use == "ot":
                act.wait_ge(ot_done, 2 * m + idx + 1)
                if later(m):
                    act.wait_ge(wo_done, m)
                sc.copy(oth[:, idx, :], bank_[:, 0:SEQ]).then_inc(oth_ready, 1)

        def step(n):
            for j in range(XPAIRS):
                g = XPAIRS * (n - 1) + j
                if pair_on(g - 1):
                    move_turned(g - 1)
                if pair_on(g):
                    exponentials(g, j, j % 4)
                for u in USES[j]:
                    evacuate(n, *u)

        act.wait_ge(const_in, 16 * 3)
        for k in range(KD):
            sc.copy(w_h[:, k, :], w_raw[:, k, :]).then_inc(wh_ready, 1)
        for n in EDGES[0]:
            step(n)
        with act.Fori(*FULL) as n:
            step(n)
        for n in EDGES[1]:
            step(n)

    @block.gpsimd
    def _(pool):
        gp = nc.gpsimd

        def inverse_deviation(m, which, got, part_signal, signal):
            pool.wait_ge(got, m + 1)
            gp.tensor_scalar(vareps[:, which, :], mv[:, which, :, 1], 1.0, EPS, ALU.mult, ALU.add).then_inc(part_signal, 1)
            pool.wait_ge(part_signal, m + 1)
            gp.tensor_tensor(rstd[:, which, :], vareps[:, which, :], minus_half[:], ALU.pow).then_inc(signal, 1)

        gp.memset(minus_half[:], -0.5).then_inc(minus_ready, 1)
        pool.wait_ge(minus_ready, 1)
        jobs = pool_jobs(pool)
        for n in range(BATCH + 2):
            if on(n):
                inverse_deviation(n, 0, mv_ready, rs_part, rstd_ready)
            for _ in range(2 if n else 1):
                next(jobs, None)
            if first and on(n - 2):
                inverse_deviation(n - 2, 1, mv2_ready, rs2_part, rstd2_ready)
            for _ in range(2):
                next(jobs, None)
        for _ in jobs:
            pass

    @block.sync
    def _(sp):
        x_rows = d_x.rearrange("(s t p) d -> s p t d", t=TILES, p=P)
        c_rows = d_ctx.rearrange("(s t p) d -> s p t d", t=TILES, p=P)
        sum_rows = d_sum.rearrange("(s t p) d -> s p t d", t=TILES, p=P) if first else None

        def step(n):
            if on(n):
                if later(n) and not first:
                    sp.wait_ge(x_ready, n)
                if later(n) and first:
                    sp.wait_ge(x_in, 16 * n)
                settle(sp)
                dst = y_of(n) if first else x_in_tile[:]
                sp.dma_start(dst.rearrange("p (t d) -> p t d", t=TILES), x_rows[n]).then_inc(x_in, 16)
                if later(n):
                    sp.wait_ge(ct_done, n)
                settle(sp)
                sp.dma_start(c_in_tile[:], c_rows[n]).then_inc(c_in, 16)
            if first and on(n - 2):
                sp.wait_ge(x_summed, n - 1)
                settle(sp)
                sp.dma_start(sum_rows[n - 2], y_of(n - 2).rearrange("p (t d) -> p t d", t=TILES)).then_inc(sum_out, 16)

        sp.dma_start(ident[:], d_ident).then_inc(const_in, 16)
        sp.dma_start(w_raw[:], d_w.rearrange("(k p) c -> p k c", p=P)).then_inc(const_in, 16)
        sp.dma_start(bias[:], d_bias).then_inc(const_in, 16)
        for n in range(BATCH + 2):
            step(n)
        if first:
            sp.wait_ge(sum_out, 16 * BATCH)


def ffn_phase(nc, ctx, y, d_ident, d_out, wd_h, wd_l):

    def sb(name, shape, dt=F32):
        return ctx.enter_context(nc.sbuf_tensor(name, shape, dt))

    def sem(name):
        return nc.alloc_semaphore(name)

    def bank(name):
        return ctx.enter_context(nc.psum_tensor(name, [P, 512], F32))

    ident = sb("f_ident", [P, P])
    minus_half = sb("f_minus_half", [P, TILES])
    z = sb("f_z", [P, TILES, DIM])
    bst, mv = sb("f_bst", [P, TILES, 6]), sb("f_mv", [P, TILES, 2])
    vareps, rstd = sb("f_vareps", [P, TILES]), sb("f_rstd", [P, TILES])
    zTh, zTl = sb("f_zTh", [P, KD, SEQ], F32R), sb("f_zTl", [P, KD, SEQ], F32R)
    hid = sb("f_hid", [P, HT, SEQ])
    hh, hl = sb("f_hh", [P, HT, SEQ], F32R), sb("f_hl", [P, HT, SEQ], F32R)
    out_tile = sb("f_out", [P, TILES, DIM])
    GROUPS = HT // 2
    ps_gate = [bank(f"f_ps_gate{i}") for i in range(GROUPS)]
    ps_up = [bank(f"f_ps_up{i}") for i in range(GROUPS)]
    ps_turn, ps_down = bank("f_ps_turn"), bank("f_ps_down")

    zt_done, gate_done, up_done, down_done = sem("f_zt_done"), sem("f_gate_done"), sem("f_up_done"), sem("f_down_done")
    stats_ready, mv_ready, z_ready, ztl_ready = (sem("f_stats_ready"), sem("f_mv_ready"), sem("f_z_ready"),
                                                 sem("f_ztl_ready"))
    h_ready, hl_ready, out_ready = sem("f_h_ready"), sem("f_hl_ready"), sem("f_out_ready")
    zth_ready, silu_done, hh_ready = sem("f_zth_ready"), sem("f_silu_done"), sem("f_hh_ready")
    minus_ready, rs_part, rstd_ready = sem("f_minus_ready"), sem("f_rs_part"), sem("f_rstd_ready")
    const_in, out_stored = sem("f_const_in"), sem("f_out_stored")

    block = ctx.enter_context(nc.Block())
    FULL = (2, BATCH)

    def on(m):
        return not isinstance(m, int) or 0 <= m < BATCH

    def later(m):
        return not isinstance(m, int) or m > 0

    def steps(eng, step):
        for n in range(FULL[0]):
            step(n)
        with eng.Fori(*FULL) as n:
            step(n)
        step(BATCH)

    def y_tile(m, t):
        return y[:, bass.ds(m * TILES * DIM + t * DIM, DIM)]

    def wcols(w, at, k, f):
        return w[:, (at * KD + k) * HID + f * P:(at * KD + k) * HID + (f + 1) * P]

    @block.tensor
    def _(pe):
        def split3(out, lhs_h, lhs_l, rhs_h, rhs_l, start, stop, **kw):
            pe.matmul(out, lhs_h, rhs_h, start=start, stop=False, **kw)
            pe.matmul(out, lhs_h, rhs_l, start=False, stop=False, **kw)
            return pe.matmul(out, lhs_l, rhs_h, start=False, stop=stop, **kw)

        def step(n):
            m = n - 1
            if on(m):
                pe.wait_ge(ztl_ready, m + 1)
                for i in range(GROUPS):
                    for at, ps, read, done in ((0, ps_gate, silu_done, gate_done), (1, ps_up, h_ready, up_done)):
                        if later(m):
                            pe.wait_ge(read, GROUPS * (m - 1) + i + 1)
                        for j in range(2):
                            for k in range(KD):
                                mm = split3(ps[i][:, j * SEQ:(j + 1) * SEQ], wcols(wd_h, at, k, 2 * i + j),
                                            wcols(wd_l, at, k, 2 * i + j), zTh[:, k, :], zTl[:, k, :],
                                            k == 0, k == KD - 1)
                        mm.then_inc(done, 1)
            if on(n):
                pe.wait_ge(z_ready, n + 1)
                if later(n):
                    pe.wait_ge(ztl_ready, n)
                for k in range(KD):
                    for t in range(TILES):
                        mm = pe.transpose(ps_turn[:, k * SEQ + t * P:k * SEQ + (t + 1) * P], z[:, t, k * P:(k + 1) * P],
                                          ident[:])
                mm.then_inc(zt_done, 1)
            if on(m):
                if later(m):
                    pe.wait_ge(out_ready, m)
                for f in range(HT):
                    if f % 2 == 0:
                        pe.wait_ge(hl_ready, GROUPS * m + f // 2 + 1)
                    cols = slice((2 * KD * HID) + f * DIM, (2 * KD * HID) + (f + 1) * DIM)
                    for t in range(TILES):
                        mm = split3(ps_down[:, t * DIM:(t + 1) * DIM], hh[:, f, t * P:(t + 1) * P],
                                    hl[:, f, t * P:(t + 1) * P], wd_h[:, cols], wd_l[:, cols],
                                    f == 0 and t == 0, f == HT - 1, skip_group_check=True)
                mm.then_inc(down_done, 1)

        pe.wait_ge(const_in, 16)
        steps(pe, step)

    @block.vector
    def _(dve):
        ve = nc.vector

        def step(n):
            m = n - 1
            if on(n):
                for t in range(TILES):
                    mm = ve.bn_stats(bst[:, t, :], y_tile(n, t))
                mm.then_inc(stats_ready, 1)
                dve.wait_ge(stats_ready, n + 1)
                dve.nop(nofuse=True)
                for t in range(TILES):
                    mm = ve.bn_aggr(mv[:, t, :], bst[:, t, :])
                mm.then_inc(mv_ready, 1)
            if on(m):
                for i in range(GROUPS):
                    dve.wait_ge(up_done, GROUPS * m + i + 1)
                    dve.wait_ge(silu_done, GROUPS * m + i + 1)
                    rows = hid[:, 2 * i:2 * i + 2, :].rearrange("p f s -> p (f s)")
                    ve.tensor_tensor(rows, ps_up[i][:], rows, ALU.mult).then_inc(h_ready, 1)
            if on(n):
                dve.wait_ge(rstd_ready, n + 1)
                if later(n):
                    dve.wait_ge(zt_done, n)
                for t in range(TILES):
                    mm = ve.tensor_scalar(z[:, t, :], y_tile(n, t), mv[:, t, 0:1], rstd[:, t:t + 1],
                                          ALU.subtract, ALU.mult)
                mm.then_inc(z_ready, 1)
            if on(m):
                for i in range(GROUPS):
                    dve.wait_ge(hh_ready, GROUPS * m + i + 1)
                    part = slice(2 * i, 2 * i + 2)
                    ve.tensor_tensor(hl[:, part, :], hid[:, part, :], hh[:, part, :].bitcast(F32),
                                     ALU.subtract).then_inc(hl_ready, 1)
            if on(n):
                dve.wait_ge(zth_ready, n + 1)
                ve.tensor_tensor(zTl[:].rearrange("p k s -> p (k s)"), ps_turn[:],
                                 zTh[:].bitcast(F32).rearrange("p k s -> p (k s)"), ALU.subtract).then_inc(ztl_ready, 1)
            if on(m):
                dve.wait_ge(down_done, m + 1)
                if later(m):
                    dve.wait_ge(out_stored, 16 * m)
                ve.tensor_tensor(out_tile[:].rearrange("p t d -> p (t d)"), ps_down[:],
                                 y[:, bass.ds(m * TILES * DIM, TILES * DIM)], ALU.add).then_inc(out_ready, 1)

        steps(dve, step)

    @block.scalar
    def _(act):
        sc = nc.scalar

        def step(n):
            m = n - 1
            if on(m):
                for i in range(GROUPS):
                    act.wait_ge(gate_done, GROUPS * m + i + 1)
                    if later(m):
                        act.wait_ge(hl_ready, GROUPS * m)
                    sc.activation(hid[:, 2 * i:2 * i + 2, :].rearrange("p f s -> p (f s)"), ps_gate[i][:],
                                  ACT.Silu).then_inc(silu_done, 1)
                for i in range(GROUPS):
                    act.wait_ge(h_ready, GROUPS * m + i + 1)
                    if later(m):
                        act.wait_ge(down_done, m)
                    part = slice(2 * i, 2 * i + 2)
                    sc.copy(hh[:, part, :], hid[:, part, :]).then_inc(hh_ready, 1)
            if on(n):
                act.wait_ge(zt_done, n + 1)
                if later(n):
                    act.wait_ge(up_done, GROUPS * n)
                sc.copy(zTh[:].rearrange("p k s -> p (k s)"), ps_turn[:]).then_inc(zth_ready, 1)

        steps(act, step)

    @block.gpsimd
    def _(pool):
        gp = nc.gpsimd

        def step(n):
            if not on(n):
                return
            pool.wait_ge(mv_ready, n + 1)
            pool.nop(nofuse=True)
            gp.tensor_scalar(vareps[:], mv[:, :, 1], 1.0, EPS, ALU.mult, ALU.add).then_inc(rs_part, 1)
            pool.wait_ge(rs_part, n + 1)
            gp.tensor_tensor(rstd[:], vareps[:], minus_half[:], ALU.pow).then_inc(rstd_ready, 1)

        gp.memset(minus_half[:], -0.5).then_inc(minus_ready, 1)
        pool.wait_ge(minus_ready, 1)
        steps(pool, step)

    @block.sync
    def _(sp):
        out_rows = d_out.rearrange("(s t p) d -> s p t d", t=TILES, p=P)
        sp.dma_start(ident[:], d_ident).then_inc(const_in, 16)
        for m in range(BATCH):
            sp.wait_ge(out_ready, m + 1)
            sp.dma_start(out_rows[m], out_tile[:]).then_inc(out_stored, 16)
        sp.wait_ge(out_stored, 16 * BATCH)


def split_ffn_weights(nc, pool, raw_int, raw, d_w, wd_h, wd_l, sems):
    gp = nc.gpsimd
    int_in, scaled, w_hi, w_done = sems
    for u in range(DW_UNITS):
        cols = slice(512 * u, 512 * (u + 1))
        if u:
            pool.wait_ge(w_done, u)
        pool.dma_start(raw_int[:], d_w[:, cols]).then_inc(int_in, 16)
        yield
        pool.wait_ge(int_in, 16 * (u + 1))
        gp.tensor_scalar(raw[:], raw_int[:], 1.0, 1.0 / 127.0, ALU.mult, ALU.mult).then_inc(scaled, 1)
        pool.wait_ge(scaled, u + 1)
        gp.tensor_copy(wd_h[:, cols], raw[:]).then_inc(w_hi, 1)
        pool.wait_ge(w_hi, u + 1)
        gp.tensor_tensor(wd_l[:, cols], raw[:], wd_h[:, cols].bitcast(F32), ALU.subtract).then_inc(w_done, 1)
        yield


def split_stack_weights(nc, pool, raw, d_w, wh, wl, sems):
    gp = nc.gpsimd
    raw_in, w_hi, w_done = sems
    for u in range(NU):
        part = slice(OFFS[u], OFFS[u] + UNITS[u])
        if u:
            pool.wait_ge(w_done, u)
        pool.dma_start(raw[:, 0:UNITS[u]], d_w[:, part]).then_inc(raw_in, 16)
        yield
        pool.wait_ge(raw_in, 16 * (u + 1))
        gp.tensor_copy(wh[:, part], raw[:, 0:UNITS[u]]).then_inc(w_hi, 1)
        pool.wait_ge(w_hi, u + 1)
        gp.tensor_tensor(wl[:, part], raw[:, 0:UNITS[u]], wh[:, part].bitcast(F32), ALU.subtract).then_inc(w_done, 1)
        yield


def transformer_kernel(nc, d_x, d_ctx, d_a_w, d_a_bias, d_stack_w, d_prm, d_qks, d_b2, d_const, d_c_w, d_c_bias,
                       d_ffn_w, d_ident, d_out):
    d_sum = nc.dram_tensor("x_after_attention", [BATCH * SEQ, DIM], F32).ap()
    with ExitStack() as whole:
        y = whole.enter_context(nc.sbuf_tensor("y", [P, BATCH * TILES * DIM], F32))
        with ExitStack() as weights:
            wh = weights.enter_context(nc.sbuf_tensor("wh", [P, WCOLS], F32R))
            wl = weights.enter_context(nc.sbuf_tensor("wl", [P, WCOLS], F32R))
            with nc.cleanup_on_exit(), ExitStack() as ctx:
                raw = ctx.enter_context(nc.sbuf_tensor("a_raw", [P, 512], F32))
                sems = [nc.alloc_semaphore(s) for s in ("a_raw_in", "a_raw_hi", "a_raw_done")]
                attend_phase(nc, ctx, y, d_x, d_ctx, d_a_w, d_a_bias, d_ident, d_sum, True,
                             lambda pool: split_stack_weights(nc, pool, raw, d_stack_w, wh, wl, sems))
            with nc.cleanup_on_exit(), ExitStack() as ctx:
                stack_phase(nc, ctx, y, wh, wl, d_stack_w, d_prm, d_qks, d_b2, d_const)
        wd_h = whole.enter_context(nc.sbuf_tensor("wd_h", [P, 512 * DW_UNITS], F32R))
        wd_l = whole.enter_context(nc.sbuf_tensor("wd_l", [P, 512 * DW_UNITS], F32R))
        with nc.cleanup_on_exit(), ExitStack() as ctx:
            raw = ctx.enter_context(nc.sbuf_tensor("c_raw", [P, 512], F32))
            raw_int = ctx.enter_context(nc.sbuf_tensor("c_raw_int", [P, 512], mybir.dt.int32))
            sems = [nc.alloc_semaphore(s) for s in ("c_int_in", "c_scaled", "c_raw_hi", "c_raw_done")]
            attend_phase(nc, ctx, y, d_sum, d_ctx, d_c_w, d_c_bias, d_ident, None, False,
                         lambda pool: split_ffn_weights(nc, pool, raw_int, raw, d_ffn_w, wd_h, wd_l, sems))
        with nc.cleanup_on_exit(), ExitStack() as ctx:
            ffn_phase(nc, ctx, y, d_ident, d_out, wd_h, wd_l)


def shape_constants():
    half = np.arange(0, DH, 2, dtype=np.float32)
    inv_freq = (np.float32(1.0) / np.float32(10000.0) ** (half / np.float32(DH))).astype(np.float32)
    t = np.arange(SEQ, dtype=np.float32)
    freqs = (t[:, None] * inv_freq[None, :]).astype(np.float32)
    base = ((half + np.float32(0.4 * DH)) / np.float32(1.4 * DH)).astype(np.float32)
    power = ((t - SEQ // 2) / np.float32(WINDOW // 2)).astype(np.float32)
    scale = (base[None, :] ** power[:, None]).astype(np.float32)
    cos, sin = np.cos(freqs), np.sin(freqs)
    inv = (np.float32(1.0) / scale).astype(np.float32)
    tables = np.stack([cos * scale, sin * scale, cos * inv, sin * inv]).astype(np.float32)
    tables = tables.reshape(4, TILES, P, 32).transpose(2, 0, 1, 3).reshape(P, -1)
    r = np.arange(P)[:, None]
    masks = []
    for q0, k0, w in ((0, 0, P), (P, P - WINDOW, P + WINDOW)):
        d = (r + q0) - (np.arange(w)[None, :] + k0)
        masks.append(np.where((d >= 0) & (d <= WINDOW), 0.0, -1.0e30).astype(np.float32))
    return np.ascontiguousarray(np.concatenate([tables] + masks + [np.eye(P, dtype=np.float32)], axis=1))


def pack_stack_weights(Wqkv, Wo, W1, W2):
    out = np.zeros((DEPTH, P, WCOLS), Wqkv.dtype)
    kt = Wqkv.reshape(DEPTH, KD, P, 3 * INNER)
    for c, at in enumerate((0, INNER, 512, INNER + 512, 2 * INNER, 2 * INNER + 512)):
        for k in range(KD):
            o = OFFS[U_QKV + 2 * c + k]
            out[:, :, o:o + 512] = kt[:, k, :, at:at + 512]
    wo = Wo.reshape(DEPTH, PAIRS, P, DIM)
    for i in range(4):
        for q in range(2):
            o = OFFS[U_WO + i] + q * DIM
            out[:, :, o:o + DIM] = wo[:, 2 * i + q]
    w1 = np.zeros((DEPTH, KD, P, 2, FT * FP), W1.dtype)
    w1[..., :FF] = W1.reshape(DEPTH, KD, P, 2, FF)
    for i in range(3):
        for k in range(KD):
            for which, u in ((1, U_GATE), (0, U_UP)):
                o = OFFS[u + i] + k * 2 * FP
                out[:, :, o:o + 2 * FP] = w1[:, k, :, which, 2 * FP * i:2 * FP * (i + 1)]
    w2 = np.zeros((DEPTH, FT * FP, DIM), W2.dtype)
    w2[:, :FF] = W2
    w2 = w2.reshape(DEPTH, FT, FP, DIM)
    for i in range(3):
        for j in range(2):
            o = OFFS[U_W2 + i] + j * DIM
            out[:, :FP, o:o + DIM] = w2[:, 2 * i + j]
    return np.ascontiguousarray(out.transpose(1, 0, 2).reshape(P, DEPTH * WCOLS))


def pack_stack_params(ln_g, ln_b, b1):
    out = np.zeros((P, DEPTH, NPRM), ln_g.dtype)
    out[:, :, 0:KD] = ln_g.reshape(DEPTH, KD, P).transpose(2, 0, 1)
    out[:, :, KD:2 * KD] = ln_b.reshape(DEPTH, KD, P).transpose(2, 0, 1)
    for which, at in ((1, 2 * KD), (0, 2 * KD + FT)):
        b = np.zeros((DEPTH, FT * FP), b1.dtype)
        b[:, :FF] = b1[:, which * FF:(which + 1) * FF]
        out[:FP, :, at:at + FT] = b.reshape(DEPTH, FT, FP).transpose(2, 0, 1)
    return np.ascontiguousarray(out.reshape(P, -1))


def kernel(**inputs):
    import concourse.bacc as bacc
    from concourse.bass_utils import run_bass_kernel_spmd

    a = {k: np.asarray(x) for k, x in inputs.items()}

    def rows(vectors):
        return np.ascontiguousarray(np.broadcast_to(np.concatenate([x.reshape(-1) for x in vectors]), (P, sum(x.size for x in vectors))))

    def hidden_major(w):
        return w.T.reshape(KD, P, HID).transpose(1, 0, 2).reshape(P, KD * HID)

    f = {k[len("L0_ffn_"):]: x for k, x in a.items() if k.startswith("L0_ffn_")}
    p, q = "L0_xattn_", "L1_xattn_"
    arrays = {
        "x": a["x"].reshape(BATCH * SEQ, DIM),
        "ctx": a["ctx_1024"].reshape(BATCH * SEQ, DIM),
        "a_w": np.concatenate([a[p + s].T for s in ("wq_w", "wk_w", "wv_w", "wo_w")], axis=1),
        "a_bias": rows([a[p + s] for s in ("wq_b", "wk_b", "wv_b", "wo_b")]),
        "stack_w": pack_stack_weights(f["Wqkv"], f["Wo"], f["W1"], f["W2"]),
        "prm": pack_stack_params(f["ln_g"], f["ln_b"], f["b1"]),
        "qks": rows([x[i] for i in range(DEPTH) for x in (f["q_scale"], f["k_scale"])]),
        "b2": rows([f["b2"]]),
        "const": shape_constants(),
        "c_w": np.concatenate([a[q + s] for s in ("Wq", "Wk", "Wv", "Wo")], axis=1),
        "c_bias": rows([a[q + s] for s in ("bq", "bk", "bv", "bo")]),
        "ffn_w": np.concatenate([hidden_major(a["L1_ffn_w_gate"]), hidden_major(a["L1_ffn_w_up"]),
                                 a["L1_ffn_w_down"].T.reshape(HT, P, DIM).transpose(1, 0, 2).reshape(P, HT * DIM)],
                                axis=1),
        "ident": np.eye(P, dtype=np.float32),
    }
    nc = bacc.Bacc("TRN2", target_bir_lowering=False, num_devices=1)
    feeds, args = {}, []
    for name, x in arrays.items():
        x = np.ascontiguousarray(x)
        feeds[f"in_{name}"] = x
        args.append(nc.dram_tensor(f"in_{name}", x.shape, mybir.dt.from_np(x.dtype), kind="ExternalInput").ap())
    args.append(nc.dram_tensor("out_x", [BATCH * SEQ, DIM], F32, kind="ExternalOutput").ap())
    transformer_kernel(nc, *args)
    r = run_bass_kernel_spmd(nc, [feeds], core_ids=[0])
    return r.results[0]["out_x"].reshape(BATCH, SEQ, DIM)
```

```python
from contextlib import ExitStack

import numpy as np

import concourse.bass as bass
from concourse import mybir

F32 = mybir.dt.float32
F32R = mybir.dt.float32r
BF16 = mybir.dt.bfloat16
ALU = mybir.AluOpType
ACT = mybir.ActivationFunctionType
AX = mybir.AxisListType

P = 128
BATCH, SEQ, DIM = 8, 256, 256
TILES = SEQ // P
KD = DIM // P
DEPTH, HEADS, DH = 6, 16, 64
PAIRS = HEADS // 2
INNER = HEADS * DH
FF = 682
FT = 6
FP = 114
WINDOW = 64
QKS = 8.0
SPANS = P + (P + WINDOW)
PCOLS = 3 * P

UNITS = [512] * 16 + [KD * 2 * FP] * 6 + [512] * 3
OFFS = [sum(UNITS[:u]) for u in range(len(UNITS))]
NU = len(UNITS)
WCOLS = sum(UNITS)
U_QKV, U_WO, U_GATE, U_UP, U_W2 = 0, 12, 16, 19, 22
NPRM = 2 * KD + 2 * FT
CONSTS = 4

EPS = 1e-5
STEPS = DEPTH * BATCH

BANK_USES = ("wo", "w2", "up", "qk", "v", "tr", "xt", "xnt", "gate")
PAIR_WORK = ("mask", "invert", "outputs", "low outputs", "exponentials", "move turned", "high outputs")
PE_SLOTS = [
    [("weigh values", 0, 2), ("scores", 0, 0), ("up", 2, 3), ("turn probs", 0, 1), ("turn outputs", 0, 2),
     ("qk", 6, 1), ("w2", 0, 3)],
    [("weigh values", 0, 2), ("turn probs", 0, 1), ("scores", 0, 0), ("w2_last", 0, 3), ("qk", 7, 1),
     ("turn outputs", 0, 2), ("v", 0, 1), ("v", 1, 1), ("wo", 2, 2)],
    [("weigh values", 0, 2), ("turn probs", 0, 1), ("scores", 0, 0), ("wo", 3, 2), ("turn outputs", 0, 2),
     ("tr", 4, 1), ("tr", 5, 1), ("v", 2, 1)],
    [("xt", 0, 0), ("v", 3, 1), ("weigh values", 0, 2), ("turn probs", 0, 1), ("scores", 0, 0), ("tr", 6, 1),
     ("tr", 7, 1), ("turn outputs", 0, 2), ("qk", 0, 0)],
    [("weigh values", 0, 2), ("turn probs", 0, 1), ("scores", 0, 0), ("wo", 0, 1), ("xnt", 0, 2),
     ("turn outputs", 0, 2), ("qk", 1, 0), ("qk", 2, 0)],
    [("weigh values", 0, 2), ("turn probs", 0, 1), ("scores", 0, 0), ("gate", 0, 2), ("turn outputs", 0, 2),
     ("qk", 3, 0)],
    [("weigh values", 0, 2), ("turn probs", 0, 1), ("scores", 0, 0), ("gate", 1, 2), ("gate", 2, 2),
     ("turn outputs", 0, 2), ("tr", 0, 0), ("tr", 1, 0), ("qk", 4, 0)],
    [("up", 0, 2), ("weigh values", 0, 2), ("turn probs", 0, 1), ("scores", 0, 0), ("wo", 1, 1),
     ("turn outputs", 0, 2), ("tr", 2, 0), ("tr", 3, 0), ("qk", 5, 0), ("up", 1, 2)],
]
DVE_SLOTS = [
    [("outputs", 0, 2), ("mask", 0, 0), ("low hidden", 1, 3), ("low outputs", 0, 2), ("invert", 0, 1), ("up", 2, 3),
     ("low hidden", 2, 3), ("qk", 6, 1)],
    [("outputs", 0, 2), ("mask", 0, 0), ("add ffn", 0, 3), ("invert", 0, 1), ("qk", 7, 1), ("low outputs", 0, 2)],
    [("outputs", 0, 2), ("mask", 0, 0), ("invert", 0, 1), ("wo", 2, 2), ("wo", 3, 2), ("low outputs", 0, 2),
     ("norm keys", 1, 1)],
    [("row stats", 0, 2), ("outputs", 0, 2), ("xt", 0, 0), ("mask", 0, 0), ("invert", 0, 1), ("low outputs", 0, 2)],
    [("qk", 0, 0), ("outputs", 0, 2), ("mask", 0, 0), ("norm rows", 0, 2), ("invert", 0, 1), ("wo", 0, 1),
     ("xnt", 0, 2), ("low outputs", 0, 2), ("qk", 1, 0), ("low rows", 0, 2), ("qk", 2, 0)],
    [("outputs", 0, 2), ("mask", 0, 0), ("invert", 0, 1), ("low outputs", 0, 2), ("gate", 0, 2)],
    [("qk", 3, 0), ("outputs", 0, 2), ("invert", 0, 1), ("mask", 0, 0), ("gate", 1, 2), ("gate", 2, 2),
     ("low outputs", 0, 2), ("qk", 4, 0), ("up", 0, 2)],
    [("outputs", 0, 2), ("norm keys", 0, 0), ("mask", 0, 0), ("invert", 0, 1), ("wo", 1, 1), ("low outputs", 0, 2),
     ("low hidden", 0, 2), ("up", 1, 2), ("qk", 5, 0)],
]
ACT_SLOTS = [
    [("move turned", 0, 1), ("high outputs", 0, 2), ("exponentials", 0, 0), ("up", 2, 3)],
    [("qk", 6, 1), ("move turned", 0, 1), ("qk", 7, 1), ("exponentials", 0, 0), ("high outputs", 0, 2), ("v", 0, 1),
     ("v", 1, 1)],
    [("move turned", 0, 1), ("exponentials", 0, 0), ("tr", 4, 1), ("high outputs", 0, 2), ("tr", 5, 1), ("v", 2, 1),
     ("xt", 0, 0), ("v", 3, 1)],
    [("move turned", 0, 1), ("tr", 6, 1), ("tr", 7, 1), ("high outputs", 0, 2), ("exponentials", 0, 0)],
    [("qk", 0, 0), ("move turned", 0, 1), ("exponentials", 0, 0), ("high outputs", 0, 2), ("xnt", 0, 2), ("qk", 1, 0),
     ("qk", 2, 0)],
    [("move turned", 0, 1), ("high outputs", 0, 2), ("exponentials", 0, 0)],
    [("qk", 3, 0), ("move turned", 0, 1), ("high outputs", 0, 2), ("exponentials", 0, 0), ("tr", 0, 0), ("qk", 4, 0),
     ("tr", 1, 0), ("gelu", 0, 2)],
    [("up", 0, 2), ("move turned", 0, 1), ("high outputs", 0, 2), ("tr", 2, 0), ("exponentials", 0, 0), ("tr", 3, 0),
     ("qk", 5, 0), ("up", 1, 2)],
]


def stack_phase(nc, ctx, y, wh, wl, d_w, d_prm, d_qks, d_b2, d_const):

    def sb(name, shape, dt=F32):
        return ctx.enter_context(nc.sbuf_tensor(name, shape, dt))

    def sem(name):
        return nc.alloc_semaphore(name)

    raw = sb("raw", [P, 2, 512])
    rope_base = sb("rope_base", [P, 4, TILES, 32])
    mask = sb("mask", [P, SPANS])
    ident = sb("ident", [P, P])
    qks = sb("qks", [P, 2, 2, 32])
    qks_swapped = sb("qks_swapped", [P, 2, 2, 32])
    rope = sb("rope", [P, 2, 2, TILES, 64])
    prm = sb("prm", [P, DEPTH, NPRM])
    b2 = sb("b2", [P, DIM])
    ycur = sb("ycur", [P, TILES, DIM])
    xth = sb("xth", [P, KD, SEQ + 1], F32R)
    xtl = sb("xtl", [P, KD, SEQ + 1], F32R)
    qk_tok = sb("qk_tok", [P, 2, TILES, 512])
    rot_tmp = sb("rot_tmp", [P, 512])
    squares = sb("squares", [P, 512])
    ss = sb("ss", [P, 2, 16])
    ssc = sb("ssc", [P, 2, 16])
    rn = sb("rn", [P, 2, 16])
    minus_half = sb("minus_half", [P, 32])
    qsc = sb("qsc", [P, PAIRS, 4])
    qkT = sb("qkT", [P, 2, PAIRS, SEQ])
    v = sb("v", [P, TILES, INNER])
    probs = sb("probs", [P, 2, PCOLS])
    probsT = sb("probsT", [P, 2, PCOLS])
    mx = sb("mx", [P, 4, 4])
    nbias = sb("nbias", [P, 4, 4])
    rsum = sb("rsum", [P, 4, 4])
    rinv = sb("rinv", [P, 4, 4])
    o_tok = sb("o_tok", [P, TILES, P])
    oth = sb("oth", [P, 4, SEQ], F32R)
    otl = sb("otl", [P, 4, SEQ], F32R)
    xn = sb("xn", [P, 2, DIM])
    bst = sb("bst", [P, TILES, 2, 6])
    mv = sb("mv", [P, TILES, 2])
    rstd = sb("rstd", [P, TILES])
    vareps = sb("vareps", [P, TILES])
    xnh = sb("xnh", [P, KD, SEQ], F32R)
    xnl = sb("xnl", [P, KD, SEQ], F32R)
    hid = sb("hid", [P, FT, SEQ])
    hh = sb("hh", [P, 2, 2, SEQ], F32R)
    hl = sb("hl", [P, 2, 2, SEQ], F32R)

    ps_sim = [ctx.enter_context(nc.psum_tensor(f"ps_sim{h}", [P, 512], F32)) for h in range(2)]
    ps_pt = [ctx.enter_context(nc.psum_tensor(f"ps_pt{h}", [P, 512], F32)) for h in range(2)]
    ps_o = ctx.enter_context(nc.psum_tensor("ps_o", [P, 512], F32))
    ps_mm = [ctx.enter_context(nc.psum_tensor(f"ps_mm{b}", [P, 512], F32)) for b in range(3)]

    sim_done, pt_done, pv_done, ot_done = sem("sim_done"), sem("pt_done"), sem("pv_done"), sem("ot_done")
    qk_done, v_done, tr_done, wo_done = sem("qk_done"), sem("v_done"), sem("tr_done"), sem("wo_done")
    xt_done, xnt_done, gate_done, up_done, w2_done = (sem("xt_done"), sem("xnt_done"), sem("gate_done"),
                                                      sem("up_done"), sem("w2_done"))
    sim_masked, bias_ready, rinv_ready, o_ready = sem("sim_masked"), sem("bias_ready"), sem("rinv_ready"), sem("o_ready")
    otl_ready, rot_part, squares_summed, qk_rotated = sem("otl_ready"), sem("rot_part"), sem("squares_summed"), sem("qk_rotated")
    kn_ready, qsc_ready, xtl_ready, y_added = sem("kn_ready"), sem("qsc_ready"), sem("xtl_ready"), sem("y_added")
    stats_ready, mv_ready, xn_ready, xnf_ready, xnl_ready = (sem("stats_ready"), sem("mv_ready"), sem("xn_ready"),
                                                             sem("xnf_ready"), sem("xnl_ready"))
    gate_ready, h_ready, hl_ready, y_summed, y_ready = (sem("gate_ready"), sem("h_ready"), sem("hl_ready"),
                                                        sem("y_summed"), sem("y_ready"))
    zeroed, xn_free, minus_ready = sem("zeroed"), sem("xn_free"), sem("minus_ready")
    exp_done, pt_moved, oth_ready, sq_ready = sem("exp_done"), sem("pt_moved"), sem("oth_ready"), sem("sq_ready")
    v_moved, tr_moved, xth_ready, xnh_ready = sem("v_moved"), sem("tr_moved"), sem("xth_ready"), sem("xnh_ready")
    gelu_done, hh_ready = sem("gelu_done"), sem("hh_ready")
    w_hi, w_ready, rope_part, rope_ready = sem("w_hi"), sem("w_ready"), sem("rope_part"), sem("rope_ready")
    rn_part, rn_ready, rs_part, rstd_ready = sem("rn_part"), sem("rn_ready"), sem("rs_part"), sem("rstd_ready")
    raw_in = [sem("raw_in0"), sem("raw_in1")]
    const_in, qks_in, b2_in, ycur_in, shift_in = (sem("const_in"), sem("qks_in"), sem("b2_in"),
                                                          sem("ycur_in"), sem("shift_in"))

    block = ctx.enter_context(nc.Block())

    def on(m):
        return not isinstance(m, int) or 0 <= m < STEPS

    def later(m, first=0):
        return not isinstance(m, int) or m > first

    def settle(eng):
        eng.nop(nofuse=True)

    def sample(m):
        return m % BATCH

    def layer(m):
        return m // BATCH

    FULL = (4, STEPS)
    EDGES = (range(0, FULL[0]), range(FULL[1], STEPS + 3))

    QA, KA, QB, KB = 0, 2, 4, 6
    ORDER = [u for slot in PE_SLOTS for u in slot if u[0] in BANK_USES]
    assert len(ORDER) % 3 == 0
    FREED = {"wo": (y_added, 4), "w2": (y_summed, 1), "up": (h_ready, 3), "qk": (rot_part, 8), "v": (v_moved, 4),
             "tr": (tr_moved, 8), "xt": (xtl_ready, 1), "xnt": (xnf_ready, 1), "gate": (gate_ready, 3)}

    def bank(use, idx):
        return ps_mm[[u[:2] for u in ORDER].index((use, idx)) % 3]

    def pair_on(g):
        return not isinstance(g, int) or 0 <= g < STEPS * PAIRS

    @block.tensor
    def _(pe):
        def split3(out, lhs_h, lhs_l, rhs_h, rhs_l, start, stop, **kw):
            pe.matmul(out, lhs_h, rhs_h, start=start, stop=False, **kw)
            pe.matmul(out, lhs_h, rhs_l, start=False, stop=False, **kw)
            return pe.matmul(out, lhs_l, rhs_h, start=False, stop=stop, **kw)

        def wait_bank(n, use, idx):
            at = [u[:2] for u in ORDER].index((use, idx)) - 3
            while at > -4 * len(ORDER):
                before, i, lag = ORDER[at % len(ORDER)]
                m = n - lag + at // len(ORDER)
                if on(m):
                    signal, per = FREED[before]
                    pe.wait_ge(signal, per * m + i + 1)
                    return
                at -= 3

        def weights(m, u):
            pe.wait_ge(w_ready, NU * layer(m) + u + 1)

        def wcols(w, u, k, width):
            return w[:, OFFS[u] + k * width:OFFS[u] + (k + 1) * width]

        def project(m, bank_, c, t, signal):
            for k in range(KD):
                u = U_QKV + 2 * c + k
                mm = split3(bank_[:], xth[:, k, t * P:(t + 1) * P], xtl[:, k, t * P:(t + 1) * P],
                            wcols(wh, u, 0, 512), wcols(wl, u, 0, 512), k == 0, k == KD - 1)
            mm.then_inc(signal, 1)

        def dense(n, use, idx, lag):
            m = n - lag
            if not on(m):
                return
            if use == "w2_last":
                w2_part(m, 2)
                return
            bank_ = bank(use, idx)
            wait_bank(n, use, idx)
            if use == "w2":
                for i in range(2):
                    w2_part(m, i)
            elif use == "wo":
                pe.wait_ge(otl_ready, PAIRS * m + 2 * idx + 2)
                weights(m, U_WO + idx)
                for t in range(TILES):
                    for q in range(2):
                        r = (2 * idx + q) % 4
                        mm = split3(bank_[:, t * DIM:(t + 1) * DIM], oth[:, r, t * P:(t + 1) * P],
                                    otl[:, r, t * P:(t + 1) * P], wcols(wh, U_WO + idx, q, DIM),
                                    wcols(wl, U_WO + idx, q, DIM), q == 0, q == 1)
                mm.then_inc(wo_done, 1)
            elif use == "xt":
                pe.wait_ge(ycur_in, 16 * (m + 1))
                for k in range(KD):
                    for t in range(TILES):
                        mm = pe.transpose(bank_[:, k * SEQ + t * P:k * SEQ + (t + 1) * P],
                                          ycur[:, t, k * P:(k + 1) * P], ident[:])
                mm.then_inc(xt_done, 1)
            elif use == "qk":
                c, t = idx // 2, idx % 2
                if idx == QA:
                    pe.wait_ge(xtl_ready, m + 1)
                if t == 0:
                    weights(m, U_QKV + 2 * c + 1)
                project(m, bank_, c, t, qk_done)
            elif use == "v":
                c, t = 4 + idx // 2, idx % 2
                if t == 0:
                    weights(m, U_QKV + 2 * c + 1)
                project(m, bank_, c, t, v_done)
            elif use == "tr":
                which, t = (idx % 4) // 2, idx % 2
                if which == 0:
                    pe.wait_ge(qk_rotated, 8 * m + (QA if idx < 4 else QB) + t + 1)
                else:
                    pe.wait_ge(kn_ready, 4 * m + 2 * (idx // 4) + t + 1)
                for j in range(4):
                    mm = pe.transpose(bank_[:, j * P:(j + 1) * P], qk_tok[:, which, t, j * P:(j + 1) * P], ident[:])
                mm.then_inc(tr_done, 1)
            elif use == "xnt":
                pe.wait_ge(xn_ready, m + 1)
                for k in range(KD):
                    for t in range(TILES):
                        mm = pe.transpose(bank_[:, k * SEQ + t * P:k * SEQ + (t + 1) * P],
                                          xn[:, t, k * P:(k + 1) * P], ident[:])
                mm.then_inc(xnt_done, 1)
            elif use in ("gate", "up"):
                u = (U_GATE if use == "gate" else U_UP) + idx
                weights(m, u)
                if (use, idx) == ("gate", 0):
                    pe.wait_ge(xnl_ready, m + 1)
                for i in range(2):
                    for k in range(KD):
                        at = OFFS[u] + k * 2 * FP + i * FP
                        mm = split3(bank_[0:FP, i * SEQ:(i + 1) * SEQ], wh[:, at:at + FP], wl[:, at:at + FP],
                                    xnh[:, k, :], xnl[:, k, :], k == 0, k == KD - 1)
                mm.then_inc(gate_done if use == "gate" else up_done, 1)

        def w2_part(m, i):
            bank_ = bank("w2", 0)
            pe.wait_ge(hl_ready, 3 * m + i + 1)
            weights(m, U_W2 + i)
            for j in range(2):
                for t in range(TILES):
                    u = U_W2 + i
                    first = i == 0 and j == 0 and t == 0
                    last = i == 2 and j == 1
                    a = hh[0:FP, i % 2, j, t * P:(t + 1) * P], hl[0:FP, i % 2, j, t * P:(t + 1) * P]
                    b = wh[0:FP, OFFS[u] + j * DIM:OFFS[u] + (j + 1) * DIM], wl[0:FP, OFFS[u] + j * DIM:OFFS[u] + (j + 1) * DIM]
                    mm = split3(bank_[:, t * DIM:(t + 1) * DIM], a[0], a[1], b[0], b[1], first, last, skip_group_check=True)
            mm.then_inc(w2_done, 1)

        def weigh_values(g, p, m):
            pe.wait_ge(pt_moved, 2 * g + 2)
            if later(g):
                pe.wait_ge(otl_ready, g)
            pe.wait_ge(v_moved, 4 * m + (2 if p < 4 else 4))
            for h in range(2):
                cols = slice((2 * p + h) * DH, (2 * p + h + 1) * DH)
                o = [ps_o[:, t * P + h * DH:t * P + (h + 1) * DH] for t in range(TILES)]
                pe.matmul(o[0], probsT[:, h, 0:P], v[:, 0, cols], start=True, stop=True)
                pe.matmul(o[1], probsT[:, h, P:2 * P], v[:, 0, cols], start=True, stop=False)
                mm = pe.matmul(o[1], probsT[:, h, 2 * P:3 * P], v[:, 1, cols], start=False, stop=True)
            mm.then_inc(pv_done, 1)

        def turn_probs(g):
            pe.wait_ge(exp_done, g + 1)
            for h in range(2):
                if later(g):
                    pe.wait_ge(pt_moved, 2 * (g - 1) + h + 1)
                for b in range(3):
                    mm = pe.transpose(ps_pt[h][:, b * P:(b + 1) * P], probs[:, h, b * P:(b + 1) * P], ident[:])
                mm.then_inc(pt_done, 1)

        def scores(g, p, m):
            pe.wait_ge(tr_moved, 8 * m + (4 if p < 4 else 8))
            for h in range(2):
                if later(g):
                    pe.wait_ge(sim_masked, 2 * (g - 1) + h + 1)
                rows = slice(h * DH, (h + 1) * DH)
                pe.matmul(ps_sim[h][:, 0:P], qkT[rows, 0, p, 0:P], qkT[rows, 1, p, 0:P], start=True, stop=True)
                mm = pe.matmul(ps_sim[h][:, P:SPANS], qkT[rows, 0, p, P:2 * P], qkT[rows, 1, p, WINDOW:SEQ],
                               start=True, stop=True)
                mm.then_inc(sim_done, 1)

        def turn_outputs(g):
            pe.wait_ge(o_ready, g + 1)
            for t in range(TILES):
                mm = pe.transpose(ps_o[:, t * P:(t + 1) * P], o_tok[:, t, :], ident[:])
            mm.then_inc(ot_done, 1)

        def step(n):
            for j, slot in enumerate(PE_SLOTS):
                for what, idx, lag in slot:
                    if what in BANK_USES or what == "w2_last":
                        dense(n, what, idx, lag)
                        continue
                    g, p, m = PAIRS * (n - 1) + j - lag, (j - lag) % PAIRS, n - 1 - (lag > j)
                    if not pair_on(g):
                        continue
                    if what == "scores":
                        scores(g, p, m)
                    elif what == "turn probs":
                        turn_probs(g)
                    elif what == "weigh values":
                        weigh_values(g, p, m)
                    elif what == "turn outputs":
                        turn_outputs(g)

        pe.wait_ge(const_in, 16 * CONSTS)
        for n in EDGES[0]:
            step(n)
        with pe.Fori(*FULL) as n:
            step(n)
        for n in EDGES[1]:
            step(n)

    @block.vector
    def _(dve):
        ve = nc.vector

        def outputs(g, r):
            dve.wait_ge(pv_done, g + 1)
            dve.wait_ge(rinv_ready, g + 1)
            if later(g):
                dve.wait_ge(ot_done, g)
            ve.tensor_tensor(o_tok[:].rearrange("p t (h d) -> p (t h) d", h=2),
                             ps_o[:, 0:2 * P].rearrange("p (a d) -> p a d", a=4),
                             rinv[:, r, :].unsqueeze(2).broadcast_to([P, 4, DH]), ALU.mult).then_inc(o_ready, 1)

        def invert_sums(g, r):
            dve.wait_ge(exp_done, g + 1)
            ve.reciprocal(rinv[:, r, :], rsum[:, r, :]).then_inc(rinv_ready, 1)

        def mask_and_max(g, p, r):
            for h in range(2):
                dve.wait_ge(sim_done, 2 * g + h + 1)
                if later(g):
                    dve.wait_ge(pt_done, 2 * (g - 1) + h + 1)
                settle(dve)
                ve.tensor_tensor_reduce(out=probs[:, h, 0:P], in0=ps_sim[h][:, 0:P], in1=mask[:, 0:P], scale=1.0,
                                        scalar=-1.0e30, op0=ALU.add, op1=ALU.max, accum_out=mx[:, r, h:h + 1])
                ve.tensor_tensor_reduce(out=probs[:, h, P + WINDOW:PCOLS], in0=ps_sim[h][:, P:SPANS],
                                        in1=mask[:, P:SPANS], scale=1.0, scalar=-1.0e30, op0=ALU.add, op1=ALU.max,
                                        accum_out=mx[:, r, 2 + h:3 + h]).then_inc(sim_masked, 1)
            dve.wait_ge(sim_masked, 2 * g + 2)
            ve.scalar_tensor_tensor(out=nbias[:, r, :], in0=mx[:, r, :], scalar=-1.0, in1=qsc[:, p, :],
                                    op0=ALU.mult, op1=ALU.mult).then_inc(bias_ready, 1)

        def low_outputs(g, r):
            dve.wait_ge(oth_ready, g + 1)
            ve.tensor_tensor(otl[:, r, :], ps_o[:, 0:SEQ], oth[:, r, :].bitcast(F32), ALU.subtract).then_inc(otl_ready, 1)

        def y_of(m):
            return y[:, bass.ds(sample(m) * TILES * DIM, TILES * DIM)]

        def evacuate(n, use, idx, lag):
            m = n - lag
            if not on(m):
                return
            bank_ = bank(use, idx)
            if use == "wo":
                dve.wait_ge(wo_done, 4 * m + idx + 1)
                dve.wait_ge(y_ready, m + 1)
                if idx:
                    dve.wait_ge(y_added, 4 * m + idx)
                ve.tensor_tensor(y_of(m), bank_[:], y_of(m), ALU.add).then_inc(y_added, 1)
            elif use == "xt":
                dve.wait_ge(xth_ready, m + 1)
                ve.tensor_tensor(xtl[:, 0, 0:SEQ], bank_[:, 0:SEQ], xth[:, 0, 0:SEQ].bitcast(F32), ALU.subtract)
                ve.tensor_tensor(xtl[:, 1, 1:SEQ + 1], bank_[:, SEQ:2 * SEQ], xth[:, 1, 1:SEQ + 1].bitcast(F32),
                                 ALU.subtract).then_inc(xtl_ready, 1)
            elif use == "qk":
                which, t = (idx % 4) // 2, idx % 2
                i = 8 * m + idx
                ps4 = bank_[:].rearrange("p (e s d) -> p e s d", s=2, d=32)
                tmp4 = rot_tmp[:].rearrange("p (e s d) -> p e s d", s=2, d=32)
                if idx == QA:
                    dve.wait_ge(rope_ready, layer(m) + 1)
                dve.wait_ge(sq_ready, i + 1)
                if idx < 4 and later(m):
                    dve.wait_ge(tr_done, 8 * m - (2 if which == 0 else 0))
                if idx >= 4:
                    dve.wait_ge(tr_done, 8 * m + (2 if which == 0 else 4))
                ve.tensor_tensor(qk_tok[:, which, t, :].rearrange("p (e d) -> p e d", d=DH),
                                 bank_[:].rearrange("p (e d) -> p e d", d=DH),
                                 rope[:, which, 0, t, :].unsqueeze(1).broadcast_to([P, 8, DH]), ALU.mult)
                if later(i):
                    dve.wait_ge(qk_rotated, i)
                for s in range(2):
                    mm = ve.tensor_tensor(tmp4[:, :, s, :], ps4[:, :, 1 - s, :],
                                          rope[:, which, 1, t, 32 * s:32 * s + 32].unsqueeze(1).broadcast_to([P, 8, 32]),
                                          ALU.mult)
                mm.then_inc(rot_part, 1)
                dve.wait_ge(rot_part, i + 1)
                ve.tensor_tensor(qk_tok[:, which, t, :], qk_tok[:, which, t, :], rot_tmp[:], ALU.add).then_inc(qk_rotated, 1)
                if t == 0 and which == 0 and (idx >= 4 or later(m)):
                    dve.wait_ge(rn_ready, 2 * m + (1 if idx >= 4 else 0))
                ve.tensor_reduce(ss[:, which, :].rearrange("p (a b c) -> p a b c", a=4, b=2)[:, :, t, :],
                                 squares[:].rearrange("p (a c d) -> p a c d", a=4, c=2), AX.X, ALU.add).then_inc(squares_summed, 1)
            elif use == "xnt":
                lp = layer(m) * NPRM
                dve.wait_ge(xnt_done, m + 1)
                pf = prm[:].rearrange("p l c -> p (l c)")
                for k in range(KD):
                    mm = ve.tensor_scalar(xn[:, k, :], bank_[:, k * SEQ:(k + 1) * SEQ], pf[:, bass.ds(lp + k, 1)],
                                          pf[:, bass.ds(lp + KD + k, 1)], ALU.mult, ALU.add)
                mm.then_inc(xnf_ready, 1)
            elif use in ("gate", "up"):
                pf = prm[:].rearrange("p l c -> p (l c)")
                b = layer(m) * NPRM + 2 * KD + (FT if use == "up" else 0)
                dve.wait_ge(gate_done if use == "gate" else up_done, 3 * m + idx + 1)
                if (use, idx) == ("gate", 0) and later(m):
                    dve.wait_ge(hl_ready, 3 * m)
                if (use, idx) == ("up", 0):
                    dve.wait_ge(gelu_done, m + 1)
                for i in range(2):
                    f = 2 * idx + i
                    src = bank_[0:FP, i * SEQ:(i + 1) * SEQ]
                    bias = pf[0:FP, bass.ds(b + f, 1)]
                    if use == "gate":
                        mm = ve.tensor_scalar(hid[0:FP, f, :], src, bias, None, ALU.add)
                    else:
                        mm = ve.scalar_tensor_tensor(out=hid[0:FP, f, :], in0=src, scalar=bias, in1=hid[0:FP, f, :],
                                                     op0=ALU.add, op1=ALU.mult)
                mm.then_inc(gate_ready if use == "gate" else h_ready, 1)

        def low_hidden(m, i):
            dve.wait_ge(hh_ready, 3 * m + i + 1)
            ve.tensor_tensor(hl[0:FP, i % 2], hid[0:FP, 2 * i:2 * i + 2, :], hh[0:FP, i % 2].bitcast(F32),
                             ALU.subtract).then_inc(hl_ready, 1)

        def low_rows(m):
            dve.wait_ge(xnh_ready, m + 1)
            ve.tensor_tensor(xnl[:], xn[:], xnh[:].bitcast(F32), ALU.subtract).then_inc(xnl_ready, 1)
            dve.wait_ge(xnl_ready, m + 1)
            ve.memset(xn[0:1, 0, P:2 * P], 0.0).then_inc(xn_free, 1)

        def norm_keys(m, c):
            dve.wait_ge(rn_ready, 2 * m + c + 1)
            dve.wait_ge(qk_rotated, 8 * m + 4 * c + 4)
            for t in range(TILES):
                kt = qk_tok[:, 1, t, :].rearrange("p (a c d) -> p a c d", a=4, c=2)
                ve.tensor_tensor(kt, kt, rn[:, 1, :].rearrange("p (a b c) -> p a b c", a=4, b=2)[:, :, t, :]
                                 .unsqueeze(3).broadcast_to([P, 4, 2, DH]), ALU.mult).then_inc(kn_ready, 1)
            if later(m):
                dve.wait_ge(exp_done, PAIRS * (m - 1) + 4 * (c + 1))
            ve.tensor_scalar(qsc[:, 4 * c:4 * c + 4, :], rn[:, 0, :].rearrange("p (a b) -> p a b", a=4), QKS, None,
                             ALU.mult).then_inc(qsc_ready, 1)

        def row_stats(m):
            dve.wait_ge(y_added, 4 * m + 4)
            dve.wait_ge(shift_in, 48 * (m + 1))
            settle(dve)
            for t in range(TILES):
                ve.bn_stats(bst[:, t, 0, :], y[:, bass.ds(sample(m) * TILES * DIM + t * DIM, P)])
                mm = ve.bn_stats(bst[:, t, 1, :], xn[:, t, P:2 * P])
            mm.then_inc(stats_ready, 1)
            dve.wait_ge(stats_ready, m + 1)
            settle(dve)
            for t in range(TILES):
                mm = ve.bn_aggr(mv[:, t, :], bst[:, t].rearrange("p a b -> p (a b)"))
            mm.then_inc(mv_ready, 1)

        def norm_rows(m):
            dve.wait_ge(rstd_ready, m + 1)
            for t in range(TILES):
                ve.tensor_scalar(xn[:, t, 0:P], y[:, bass.ds(sample(m) * TILES * DIM + t * DIM, P)], mv[:, t, 0:1],
                                 rstd[:, t:t + 1], ALU.subtract, ALU.mult)
                mm = ve.tensor_scalar(xn[:, t, P:2 * P], xn[:, t, P:2 * P], mv[:, t, 0:1],
                                      rstd[:, t:t + 1], ALU.subtract, ALU.mult)
            mm.then_inc(xn_ready, 1)

        def add_ffn(m):
            dve.wait_ge(w2_done, 3 * m + 3)
            ve.tensor_tensor(y_of(m), bank("w2", 0)[:], y_of(m), ALU.add).then_inc(y_summed, 1)
            dve.wait_ge(y_summed, m + 1)
            dve.wait_ge(b2_in, 16 * (layer(m) + 1))
            y3 = y_of(m).rearrange("p (t d) -> p t d", t=TILES)
            ve.tensor_tensor(y3, y3, b2[:].unsqueeze(1).broadcast_to([P, TILES, DIM]), ALU.add).then_inc(y_ready, 1)

        def step(n):
            for j, slot in enumerate(DVE_SLOTS):
                for what, idx, lag in slot:
                    m = n - lag
                    if what in BANK_USES:
                        evacuate(n, what, idx, lag)
                    elif what in PAIR_WORK:
                        g, p, r = PAIRS * (n - 1) + j - lag, (j - lag) % PAIRS, (j - lag) % 4
                        if not pair_on(g):
                            continue
                        if what == "mask":
                            mask_and_max(g, p, r)
                        elif what == "invert":
                            invert_sums(g, r)
                        elif what == "outputs":
                            outputs(g, r)
                        elif what == "low outputs":
                            low_outputs(g, r)
                    elif not on(m):
                        continue
                    elif what == "row stats":
                        row_stats(m)
                    elif what == "norm rows":
                        norm_rows(m)
                    elif what == "low rows":
                        low_rows(m)
                    elif what == "norm keys":
                        norm_keys(m, idx)
                    elif what == "low hidden":
                        low_hidden(m, idx)
                    elif what == "add ffn":
                        add_ffn(m)

        for h in range(2):
            ve.memset(probs[:, h, P:P + WINDOW], 0.0).then_inc(zeroed, 1)
        ve.memset(xth[:, 1, 0:1].bitcast(F32), 0.0).then_inc(zeroed, 1)
        ve.memset(xtl[:, 1, 0:1].bitcast(F32), 0.0).then_inc(zeroed, 1)
        ve.memset(xn[0:1, 0, P:2 * P], 0.0).then_inc(xn_free, 1)
        ve.memset(mx[:], 0.0).then_inc(y_ready, BATCH)
        dve.wait_ge(const_in, 16 * CONSTS)
        for n in EDGES[0]:
            step(n)
        with dve.Fori(*FULL) as n:
            step(n)
        for n in EDGES[1]:
            step(n)

    @block.scalar
    def _(act):
        sc = nc.scalar

        def move_turned(g):
            for h in range(2):
                act.wait_ge(pt_done, 2 * g + h + 1)
                if later(g):
                    act.wait_ge(pv_done, g)
                sc.copy(probsT[:, h, :], ps_pt[h][:, 0:PCOLS]).then_inc(pt_moved, 1)

        def exponentials(g, p, r):
            act.wait_ge(bias_ready, g + 1)
            for t in range(TILES):
                for h in range(2):
                    part = probs[:, h, 0:P] if t == 0 else probs[:, h, P + WINDOW:PCOLS]
                    c = 2 * t + h
                    mm = sc.activation(part, part, ACT.Exp, bias=nbias[:, r, c:c + 1], scale=qsc[:, p, c:c + 1],
                                       accum_out=rsum[:, r, c:c + 1])
            mm.then_inc(exp_done, 1)

        def high_outputs(g, r, m, p):
            act.wait_ge(ot_done, g + 1)
            if later(g, 3):
                act.wait_ge(wo_done, 4 * m + p // 2 - 1)
            sc.copy(oth[:, r, :], ps_o[:, 0:SEQ]).then_inc(oth_ready, 1)

        def evacuate(n, use, idx, lag):
            m = n - lag
            if not on(m):
                return
            bank_ = bank(use, idx)
            if use == "qk":
                i = 8 * m + idx
                act.wait_ge(qk_done, i + 1)
                if later(i):
                    act.wait_ge(squares_summed, i)
                sc.activation(squares[:], bank_[:], ACT.Square).then_inc(sq_ready, 1)
            elif use == "v":
                c, t = idx // 2, idx % 2
                act.wait_ge(v_done, 4 * m + idx + 1)
                if later(m):
                    act.wait_ge(pv_done, PAIRS * (m - 1) + 4 * (c + 1))
                sc.copy(v[:, t, c * 512:(c + 1) * 512], bank_[:]).then_inc(v_moved, 1)
            elif use == "tr":
                c, which, t = idx // 4, (idx % 4) // 2, idx % 2
                act.wait_ge(tr_done, 8 * m + idx + 1)
                if later(m):
                    act.wait_ge(sim_done, 2 * (PAIRS * (m - 1) + 4 * (c + 1)))
                sc.copy(qkT[:, which, 4 * c:4 * c + 4, t * P:(t + 1) * P],
                        bank_[:].rearrange("p (a q) -> p a q", a=4)).then_inc(tr_moved, 1)
            elif use == "xt":
                act.wait_ge(xt_done, m + 1)
                if later(m):
                    act.wait_ge(v_done, 4 * m)
                sc.copy(xth[:, 0, 0:SEQ], bank_[:, 0:SEQ])
                sc.copy(xth[:, 1, 1:SEQ + 1], bank_[:, SEQ:2 * SEQ]).then_inc(xth_ready, 1)
            elif use == "xnt":
                act.wait_ge(xnf_ready, m + 1)
                if later(m):
                    act.wait_ge(up_done, 3 * m)
                sc.copy(xnh[:], xn[:]).then_inc(xnh_ready, 1)
            elif use == "up":
                i = idx
                act.wait_ge(h_ready, 3 * m + i + 1)
                if i == 2:
                    act.wait_ge(w2_done, 3 * m + 1)
                elif later(m):
                    act.wait_ge(w2_done, 3 * m)
                sc.copy(hh[0:FP, i % 2], hid[0:FP, 2 * i:2 * i + 2, :]).then_inc(hh_ready, 1)

        def gelu(m):
            act.wait_ge(gate_ready, 3 * m + 3)
            sc.activation(hid[0:FP], hid[0:FP], ACT.Gelu).then_inc(gelu_done, 1)

        def step(n):
            for j, slot in enumerate(ACT_SLOTS):
                for what, idx, lag in slot:
                    if what in PAIR_WORK:
                        g, p, r = PAIRS * (n - 1) + j - lag, (j - lag) % PAIRS, (j - lag) % 4
                        if not pair_on(g):
                            continue
                        if what == "exponentials":
                            exponentials(g, p, r)
                        elif what == "move turned":
                            move_turned(g)
                        elif what == "high outputs":
                            high_outputs(g, r, n - 1 - (lag > j), p)
                    elif what == "gelu":
                        if on(n - lag):
                            gelu(n - lag)
                    elif what in BANK_USES:
                        evacuate(n, what, idx, lag)

        act.wait_ge(zeroed, 4)
        for n in EDGES[0]:
            step(n)
        with act.Fori(*FULL) as n:
            step(n)
        for n in EDGES[1]:
            step(n)

    @block.gpsimd
    def _(pool):
        gp = nc.gpsimd

        def load_unit(l, u):
            i = NU * l + u
            pool.wait_ge(w_ready, i - (1 if u else 0))
            src = d_w[:, bass.ds(WCOLS * l + OFFS[u], UNITS[u])]
            pool.dma_start(raw[:, u % 2, 0:UNITS[u]], src).then_inc(raw_in[u % 2], 16)

        def split_unit(l, u):
            i = NU * l + u
            part = slice(OFFS[u], OFFS[u] + UNITS[u])
            src = raw[:, u % 2, 0:UNITS[u]]
            pool.wait_ge(raw_in[u % 2], 16 * (len(range(u % 2, NU, 2)) * (l - 1) + u // 2 + 1))
            settle(pool)
            gp.tensor_copy(wh[:, part], src).then_inc(w_hi, 1)
            pool.wait_ge(w_hi, i + 1 - NU)
            gp.tensor_tensor(wl[:, part], src, wh[:, part].bitcast(F32), ALU.subtract).then_inc(w_ready, 1)

        def freed(m, u):
            if u < U_QKV + 8:
                return qk_done, 8 * m + 2 * (u // 2) + 2
            if u < U_WO:
                return v_done, 4 * m + 2 * ((u - 8) // 2) + 2
            if u < U_GATE:
                return wo_done, 4 * m + u - U_WO + 1
            if u < U_UP:
                return gate_done, 3 * m + u - U_GATE + 1
            if u < U_W2:
                return up_done, 3 * m + u - U_UP + 1
            return w2_done, 3 * m + u - U_W2 + 1

        def reload(l, units):
            for u in units:
                if u + 1 < NU:
                    load_unit(l, u + 1)
                pool.wait_ge(*freed(BATCH * l - 1, u))
                split_unit(l, u)

        def rope_tables(l):
            pool.wait_ge(qks_in, 16 * (l + 1))
            if later(l):
                pool.wait_ge(qk_rotated, 8 * BATCH * l)
            settle(pool)
            gp.tensor_scalar(qks_swapped[:, :, 0, :], qks[:, :, 1, :], -1.0, 1.0, ALU.mult, ALU.mult)
            gp.tensor_copy(qks_swapped[:, :, 1, :], qks[:, :, 0, :]).then_inc(rope_part, 1)
            pool.wait_ge(rope_part, l + 1)
            for w in range(2):
                for f, scales in enumerate((qks, qks_swapped)):
                    for t in range(TILES):
                        mm = gp.tensor_tensor(rope[:, w, f, t, :].rearrange("p (s d) -> p s d", s=2), scales[:, w],
                                              rope_base[:, 2 * w + f, t, :].unsqueeze(1).broadcast_to([P, 2, 32]),
                                              ALU.mult)
            mm.then_inc(rope_ready, 1)

        def inverse_norms(m, c):
            i = 2 * m + c
            pool.wait_ge(squares_summed, 8 * m + 4 * c + 4)
            settle(pool)
            gp.tensor_scalar(ssc[:], ss[:], 1e-24, 3.0e38, ALU.max, ALU.min).then_inc(rn_part, 1)
            pool.wait_ge(rn_part, i + 1)
            if later(i):
                pool.wait_ge(qsc_ready, i)
            gp.tensor_tensor(rn[:].rearrange("p a b -> p (a b)"), ssc[:].rearrange("p a b -> p (a b)"), minus_half[:],
                             ALU.pow).then_inc(rn_ready, 1)

        def inverse_deviation(m):
            pool.wait_ge(mv_ready, m + 1)
            settle(pool)
            gp.tensor_scalar(vareps[:], mv[:, :, 1], 1.0, EPS, ALU.mult, ALU.add).then_inc(rs_part, 1)
            pool.wait_ge(rs_part, m + 1)
            gp.tensor_tensor(rstd[:], vareps[:], minus_half[:, 0:TILES], ALU.pow).then_inc(rstd_ready, 1)

        def step(n, l=None, part=None):
            if part == 1:
                reload(l, range(4, 6))
            if part == 3:
                reload(l, range(U_UP, U_W2))
            if on(n - 1):
                inverse_norms(n - 1, 1)
            if part == 1:
                rope_tables(l)
                reload(l, range(6, 8))
            if part == 2:
                reload(l, range(U_WO + 2, U_WO + 4))
            if part == 3:
                reload(l, range(U_W2, NU))
            if on(n - 2):
                inverse_deviation(n - 2)
            if part == 1:
                reload(l, range(8, U_WO))
            if on(n):
                inverse_norms(n, 0)
            if part == 0:
                load_unit(l, 0)
                reload(l, range(0, 4))
            if part == 1:
                reload(l, range(U_WO, U_WO + 2))
            if part == 2:
                reload(l, range(U_GATE, U_UP))

        gp.memset(minus_half[:], -0.5).then_inc(minus_ready, 1)
        pool.wait_ge(minus_ready, 1)
        gp.memset(ssc[:], 0.0).then_inc(w_ready, NU)
        pool.wait_ge(w_ready, NU)
        pool.wait_ge(const_in, 16 * CONSTS)
        rope_tables(0)
        for n in EDGES[0]:
            step(n)
        with pool.Fori(0, DEPTH - 1) as o:
            for s in range(BATCH):
                part = s - (BATCH - 1 - FULL[0])
                step(BATCH * o + FULL[0] + s, o + 1, part if part >= 0 else None)
        with pool.Fori(BATCH * (DEPTH - 1) + FULL[0], FULL[1]) as n:
            step(n)
        for n in EDGES[1]:
            step(n)

    @block.sync
    def _(sp):
        y5 = y[:].rearrange("p (s t d) -> p s t d", s=BATCH, t=TILES)

        def step(n):
            if on(n):
                sp.wait_ge(y_ready, n + 1)
                settle(sp)
                if later(n):
                    sp.wait_ge(xt_done, n)
                settle(sp)
                sp.dma_start(ycur[:].rearrange("p t d -> p (t d)"),
                             y[:, bass.ds(sample(n) * TILES * DIM, TILES * DIM)]).then_inc(ycur_in, 16)
            m = n - 2
            if on(m):
                sp.wait_ge(y_added, 4 * m + 4)
                settle(sp)
                sp.wait_ge(xn_free, m + 1)
                settle(sp)
                at = sample(m) * TILES * DIM
                for t in range(TILES):
                    sp.dma_start(xn[1:P, t, P:2 * P], y[0:P - 1, bass.ds(at + t * DIM + P, P)]).then_inc(shift_in, 16)
                sp.dma_start(xn[0:1, 1, P:2 * P], y[P - 1:P, bass.ds(at + P, P)]).then_inc(shift_in, 16)

        def load_scales(l):
            if later(l):
                sp.wait_ge(rope_ready, l)
                settle(sp)
            sp.dma_start(qks[:].rearrange("p a s d -> p (a s d)"), d_qks[:, bass.ds(2 * DH * l, 2 * DH)]).then_inc(qks_in, 16)

        def load_b2(l):
            if later(l):
                sp.wait_ge(y_ready, BATCH * l + BATCH)
                settle(sp)
            sp.dma_start(b2[:], d_b2[:, bass.ds(DIM * l, DIM)]).then_inc(b2_in, 16)

        sp.dma_start(rope_base[:], d_const[:, 0:4 * TILES * 32].rearrange("p (a t d) -> p a t d", a=4, t=TILES)).then_inc(const_in, 16)
        sp.dma_start(mask[:], d_const[:, 4 * TILES * 32:4 * TILES * 32 + SPANS]).then_inc(const_in, 16)
        sp.dma_start(ident[:], d_const[:, 4 * TILES * 32 + SPANS:4 * TILES * 32 + SPANS + P]).then_inc(const_in, 16)
        sp.dma_start(prm[:].rearrange("p l c -> p (l c)"), d_prm).then_inc(const_in, 16)
        load_scales(0)
        load_b2(0)
        for n in EDGES[0]:
            step(n)
        with sp.Fori(0, DEPTH - 1) as o:
            for s in range(BATCH):
                step(BATCH * o + FULL[0] + s)
                if s == 0:
                    load_scales(o + 1)
                if s == BATCH + 2 - FULL[0]:
                    load_b2(o + 1)
        with sp.Fori(BATCH * (DEPTH - 1) + FULL[0], FULL[1]) as n:
            step(n)
        for n in EDGES[1]:
            step(n)


XHEADS = 16
XDH = DIM // XHEADS
XPAIRS = XHEADS // 2
XW = 4 * DIM
HID = 768
HT = HID // P
DW_UNITS = 3 * KD * HID // 512

X_BANK_USES = ("st", "v", "zt", "ct", "qk", "ot", "wo")
X_PAIR_WORK = ("move turned", "maxima")
X_PE_SLOTS = [
    [("weigh values", 0, 2), ("turn probs", 0, 1), ("scores", 0, 0), ("st", 7, 1)],
    [("weigh values", 0, 2), ("turn probs", 0, 1), ("scores", 0, 0), ("v", 0, 1)],
    [("weigh values", 0, 2), ("turn probs", 0, 1), ("scores", 0, 0), ("zt", 0, 0)],
    [("weigh values", 0, 2), ("turn probs", 0, 1), ("scores", 0, 0), ("ct", 0, 0), ("qk", 0, 0), ("ot", 1, 2),
     ("qk", 1, 0)],
    [("weigh values", 0, 2), ("turn probs", 0, 1), ("scores", 0, 0), ("wo", 0, 2), ("st", 0, 0)],
    [("weigh values", 0, 2), ("st", 1, 0), ("turn probs", 0, 1), ("scores", 0, 0)],
    [("st", 2, 0), ("weigh values", 0, 2), ("turn probs", 0, 1), ("scores", 0, 0), ("st", 3, 0)],
    [("st", 4, 0), ("weigh values", 0, 2), ("ot", 0, 1), ("turn probs", 0, 1), ("scores", 0, 0), ("st", 5, 0),
     ("st", 6, 0)],
]
X_DVE_SLOTS = [
    [("move turned", 0, 1), ("maxima", 0, 0)],
    [("rows in", 0, 0), ("move turned", 0, 1), ("maxima", 0, 0), ("v", 0, 1), ("st", 7, 1), ("norm in", 0, 0)],
    [("move turned", 0, 1), ("maxima", 0, 0), ("outputs", 1, 2)],
    [("zt", 0, 0), ("ct", 0, 0), ("move turned", 0, 1), ("maxima", 0, 0), ("qk", 0, 0), ("qk", 1, 0)],
    [("ot", 1, 2), ("move turned", 0, 1), ("maxima", 0, 0)],
    [("wo", 0, 2), ("st", 0, 0), ("move turned", 0, 1), ("maxima", 0, 0), ("outputs", 0, 1), ("st", 1, 0),
     ("st", 2, 0)],
    [("move turned", 0, 1), ("maxima", 0, 0), ("st", 3, 0), ("st", 4, 0), ("norm out", 0, 2)],
    [("move turned", 0, 1), ("maxima", 0, 0), ("ot", 0, 1), ("st", 5, 0), ("st", 6, 0)],
]
X_ACT_SLOTS = [
    [("move turned", 0, 1), ("exponentials", 0, 0)],
    [("move turned", 0, 1), ("exponentials", 0, 0)],
    [("move turned", 0, 1), ("exponentials", 0, 0)],
    [("move turned", 0, 1), ("zt", 0, 0), ("ct", 0, 0), ("qk", 0, 0), ("ot", 1, 2), ("exponentials", 0, 0),
     ("qk", 1, 0)],
    [("move turned", 0, 1), ("exponentials", 0, 0)],
    [("move turned", 0, 1), ("exponentials", 0, 0)],
    [("move turned", 0, 1), ("exponentials", 0, 0)],
    [("ot", 0, 1), ("move turned", 0, 1), ("exponentials", 0, 0)],
]


def attend_phase(nc, ctx, y, d_x, d_ctx, d_w, d_bias, d_ident, d_sum, first, pool_jobs):

    tag = "a_" if first else "c_"

    def sb(name, shape, dt=F32):
        return ctx.enter_context(nc.sbuf_tensor(tag + name, shape, dt))

    def sem(name):
        return nc.alloc_semaphore(tag + name)

    ident = sb("ident", [P, P])
    w_raw = sb("w_raw", [P, KD, XW])
    w_h, w_l = sb("w_h", [P, KD, XW], F32R), sb("w_l", [P, KD, XW], F32R)
    bias = sb("bias", [P, XW])
    x_in_tile = None if first else sb("x_in_tile", [P, TILES * DIM])
    c_in_tile = sb("c_in_tile", [P, TILES, DIM])
    z = sb("z", [P, TILES, DIM])
    bst = sb("bst", [P, 2, TILES, 6])
    mv = sb("mv", [P, 2, TILES, 2])
    vareps = sb("vareps", [P, 2, TILES])
    rstd = sb("rstd", [P, 2, TILES])
    minus_half = sb("minus_half", [P, TILES])
    zTh, zTl = sb("zTh", [P, KD, SEQ], F32R), sb("zTl", [P, KD, SEQ], F32R)
    cTh, cTl = sb("cTh", [P, KD, SEQ], F32R), sb("cTl", [P, KD, SEQ], F32R)
    qk = sb("qk", [P, 2, XHEADS, XDH])
    parts = sb("parts", [P, TILES, 2, XHEADS, 2, 2, XDH], F32R)
    stacked = sb("stacked", [P, XPAIRS, 2, SEQ], F32R)
    v = sb("v", [P, TILES, DIM])
    probs = sb("probs", [P, 2, TILES, SEQ])
    probsT = sb("probsT", [P, 2, 2, SEQ])
    nmax = sb("nmax", [P, 4, 2, TILES])
    rsum = sb("rsum", [P, TILES, XHEADS])
    rinv = sb("rinv", [P, TILES, XHEADS])
    o_tok = sb("o_tok", [P, KD, TILES, P])
    oth, otl = sb("oth", [P, KD, SEQ], F32R), sb("otl", [P, KD, SEQ], F32R)

    def bank(name):
        return ctx.enter_context(nc.psum_tensor(tag + name, [P, 512], F32))

    ps_sim = [bank("ps_sim0"), bank("ps_sim1")]
    ps_pt = [bank("ps_pt0"), bank("ps_pt1")]
    ps_o = [bank("ps_o0"), bank("ps_o1")]
    ps_mm = [bank("ps_mm0"), bank("ps_mm1")]

    zt_done, ct_done, proj_done, v_done = sem("zt_done"), sem("ct_done"), sem("proj_done"), sem("v_done")
    st_done, sim_done, pt_done, pv_done = sem("st_done"), sem("sim_done"), sem("pt_done"), sem("pv_done")
    ot_done, wo_done = sem("ot_done"), sem("wo_done")
    x_ready, stats_ready, mv_ready, z_ready = sem("x_ready"), sem("stats_ready"), sem("mv_ready"), sem("z_ready")
    ztl_ready, ctl_ready, qk_biased, parts_l = sem("ztl_ready"), sem("ctl_ready"), sem("qk_biased"), sem("parts_l")
    v_ready, st_moved, max_ready, pt_moved_b = sem("v_ready"), sem("st_moved"), sem("max_ready"), sem("pt_moved_b")
    rinv_ready, o_ready, otl_ready, wo_read = sem("rinv_ready"), sem("o_ready"), sem("otl_ready"), sem("wo_read")
    x_summed, stats2_ready, mv2_ready, y_normed = (sem("x_summed"), sem("stats2_ready"), sem("mv2_ready"),
                                                   sem("y_normed"))
    wl_ready, bias_scaled = sem("wl_ready"), sem("bias_scaled")
    wh_ready, zth_ready, cth_ready, parts_h = sem("wh_ready"), sem("zth_ready"), sem("cth_ready"), sem("parts_h")
    exp_done, pt_moved_a, oth_ready = sem("exp_done"), sem("pt_moved_a"), sem("oth_ready")
    minus_ready, rs_part, rstd_ready, rs2_part, rstd2_ready = (sem("minus_ready"), sem("rs_part"), sem("rstd_ready"),
                                                               sem("rs2_part"), sem("rstd2_ready"))
    const_in, x_in, c_in, sum_out = sem("const_in"), sem("x_in"), sem("c_in"), sem("sum_out")

    block = ctx.enter_context(nc.Block())
    FULL = (3, BATCH)
    EDGES = (range(0, FULL[0]), range(FULL[1], BATCH + 2))

    def on(m):
        return not isinstance(m, int) or 0 <= m < BATCH

    def later(m, first_=0):
        return not isinstance(m, int) or m > first_

    def pair_on(g):
        return not isinstance(g, int) or 0 <= g < BATCH * XPAIRS

    def settle(eng):
        eng.nop(nofuse=True)

    ORDER = [u for slot in X_PE_SLOTS for u in slot if u[0] in X_BANK_USES]
    assert len(ORDER) % 2 == 0
    FREED = {"st": (st_moved, 8), "v": (v_ready, 1), "zt": (ztl_ready, 1), "ct": (ctl_ready, 1), "qk": (qk_biased, 2),
             "ot": (otl_ready, 2), "wo": (wo_read, 1)}

    def mm_bank(use, idx):
        return ps_mm[[u[:2] for u in ORDER].index((use, idx)) % 2]

    def y_of(m):
        return y[:, bass.ds(m * TILES * DIM, TILES * DIM)]

    def part_views(t, w):
        if w == 0:
            return parts[:, t, w, :, :, 0, :], parts[:, t, w, :, :, 1, :]
        return parts[:, t, w, :, 0, :, :], parts[:, t, w, :, 1, :, :]

    @block.tensor
    def _(pe):
        def split3(out, lhs_h, lhs_l, rhs_h, rhs_l, start, stop):
            pe.matmul(out, lhs_h, rhs_h, start=start, stop=False)
            pe.matmul(out, lhs_h, rhs_l, start=False, stop=False)
            return pe.matmul(out, lhs_l, rhs_h, start=False, stop=stop)

        def dense(n, use, idx, lag):
            m = n - lag
            if not on(m):
                return
            bank_ = mm_bank(use, idx)
            at = [u[:2] for u in ORDER].index((use, idx)) - 2
            while at > -4 * len(ORDER):
                before, i, blag = ORDER[at % len(ORDER)]
                bm = n - blag + at // len(ORDER)
                if on(bm):
                    signal, per = FREED[before]
                    pe.wait_ge(signal, per * bm + i + 1)
                    break
                at -= 2
            if use in ("zt", "ct"):
                if use == "zt":
                    pe.wait_ge(z_ready, m + 1)
                else:
                    pe.wait_ge(c_in, 16 * (m + 1))
                src = z if use == "zt" else c_in_tile
                for k in range(KD):
                    for t in range(TILES):
                        mm = pe.transpose(bank_[:, k * SEQ + t * P:k * SEQ + (t + 1) * P],
                                          src[:, t, k * P:(k + 1) * P], ident[:])
                mm.then_inc(zt_done if use == "zt" else ct_done, 1)
            elif use == "qk":
                if idx == 0:
                    pe.wait_ge(ztl_ready, m + 1)
                    pe.wait_ge(ctl_ready, m + 1)
                t = idx
                for w, (h_, l_) in enumerate(((zTh, zTl), (cTh, cTl))):
                    for k in range(KD):
                        cols = slice(w * DIM, (w + 1) * DIM)
                        mm = split3(bank_[:, cols], h_[:, k, t * P:(t + 1) * P], l_[:, k, t * P:(t + 1) * P],
                                    w_h[:, k, cols], w_l[:, k, cols], k == 0, k == KD - 1)
                mm.then_inc(proj_done, 1)
            elif use == "v":
                cols = slice(2 * DIM, 3 * DIM)
                for t in range(TILES):
                    for k in range(KD):
                        mm = split3(bank_[:, t * DIM:(t + 1) * DIM], cTh[:, k, t * P:(t + 1) * P],
                                    cTl[:, k, t * P:(t + 1) * P], w_h[:, k, cols], w_l[:, k, cols], k == 0, k == KD - 1)
                mm.then_inc(v_done, 1)
            elif use == "st":
                pe.wait_ge(parts_l, 4 * m + 4)
                for w in range(2):
                    for t in range(TILES):
                        src = parts[:, t, w, 2 * idx:2 * idx + 2].bitcast(F32).rearrange("p h a b d -> p (h a b d)")
                        mm = pe.transpose(bank_[:, w * SEQ + t * P:w * SEQ + (t + 1) * P], src, ident[:])
                mm.then_inc(st_done, 1)
            elif use == "ot":
                pe.wait_ge(o_ready, 2 * m + idx + 1)
                for t in range(TILES):
                    mm = pe.transpose(bank_[:, t * P:(t + 1) * P], o_tok[:, idx, t, :], ident[:])
                mm.then_inc(ot_done, 1)
            elif use == "wo":
                pe.wait_ge(otl_ready, 2 * m + 2)
                cols = slice(3 * DIM, 4 * DIM)
                for t in range(TILES):
                    for k in range(KD):
                        mm = split3(bank_[:, t * DIM:(t + 1) * DIM], oth[:, k, t * P:(t + 1) * P],
                                    otl[:, k, t * P:(t + 1) * P], w_h[:, k, cols], w_l[:, k, cols], k == 0, k == KD - 1)
                mm.then_inc(wo_done, 1)

        def scores(g, p, m):
            pe.wait_ge(st_moved, 8 * m + p + 1)
            for h in range(2):
                if later(g):
                    pe.wait_ge(exp_done, 2 * (g - 1) + h + 1)
                rows = slice(64 * h, 64 * h + 64)
                for t in range(TILES):
                    mm = pe.matmul(ps_sim[h][:, t * SEQ:(t + 1) * SEQ], stacked[rows, p, 0, t * P:(t + 1) * P],
                                   stacked[rows, p, 1, :], start=True, stop=True)
                mm.then_inc(sim_done, 1)

        def turn_probs(g):
            for h in range(2):
                pe.wait_ge(exp_done, 2 * g + h + 1)
                if later(g):
                    pe.wait_ge(pt_moved_b if h else pt_moved_a, g)
                for c in range(2):
                    for t in range(TILES):
                        mm = pe.transpose(ps_pt[h][:, c * SEQ + t * P:c * SEQ + (t + 1) * P],
                                          probs[:, h, t, c * P:(c + 1) * P], ident[:])
                mm.then_inc(pt_done, 1)

        def weigh_values(g, p, m):
            pe.wait_ge(pt_moved_a, g + 1)
            pe.wait_ge(pt_moved_b, g + 1)
            if p == 0:
                pe.wait_ge(v_ready, m + 1)
            if p % 4 == 0 and later(m):
                pe.wait_ge(o_ready, 2 * (m - 1) + p // 4 + 1)
            for h in range(2):
                head = 2 * p + h
                for t in range(TILES):
                    out = ps_o[p // 4][:, t * P + (head % 8) * XDH:t * P + (head % 8 + 1) * XDH]
                    for c in range(2):
                        mm = pe.matmul(out, probsT[:, h, c, t * P:(t + 1) * P], v[:, c, head * XDH:(head + 1) * XDH],
                                       start=(c == 0), stop=(c == 1))
            mm.then_inc(pv_done, 1)

        def step(n):
            for j, slot in enumerate(X_PE_SLOTS):
                for what, idx, lag in slot:
                    if what in X_BANK_USES:
                        dense(n, what, idx, lag)
                        continue
                    g, p, m = XPAIRS * (n - 1) + j - lag, (j - lag) % XPAIRS, n - 1 - (lag > j)
                    if not pair_on(g):
                        continue
                    if what == "scores":
                        scores(g, p, m)
                    elif what == "turn probs":
                        turn_probs(g)
                    elif what == "weigh values":
                        weigh_values(g, p, m)

        pe.wait_ge(const_in, 16 * 3)
        pe.wait_ge(wl_ready, KD)
        for n in EDGES[0]:
            step(n)
        with pe.Fori(*FULL) as n:
            step(n)
        for n in EDGES[1]:
            step(n)

    @block.vector
    def _(dve):
        ve = nc.vector

        def stats(m, which, signal, out_signal):
            for t in range(TILES):
                mm = ve.bn_stats(bst[:, which, t, :], y[:, bass.ds(m * TILES * DIM + t * DIM, DIM)])
            mm.then_inc(signal, 1)
            dve.wait_ge(signal, m + 1)
            settle(dve)
            for t in range(TILES):
                mm = ve.bn_aggr(mv[:, which, t, :], bst[:, which, t, :])
            mm.then_inc(out_signal, 1)

        def rows_in(m):
            dve.wait_ge(x_in, 16 * (m + 1))
            if not first:
                ve.tensor_tensor(y_of(m), y_of(m), x_in_tile[:], ALU.add).then_inc(x_ready, 1)
                dve.wait_ge(x_ready, m + 1)
            settle(dve)
            stats(m, 0, stats_ready, mv_ready)

        def norm_in(m):
            dve.wait_ge(rstd_ready, m + 1)
            if later(m):
                dve.wait_ge(zt_done, m)
            for t in range(TILES):
                mm = ve.tensor_scalar(z[:, t, :], y[:, bass.ds(m * TILES * DIM + t * DIM, DIM)], mv[:, 0, t, 0:1],
                                      rstd[:, 0, t:t + 1], ALU.subtract, ALU.mult)
            mm.then_inc(z_ready, 1)

        def norm_out(m):
            dve.wait_ge(rstd2_ready, m + 1)
            dve.wait_ge(sum_out, 16 * (m + 1))
            for t in range(TILES):
                yt = y[:, bass.ds(m * TILES * DIM + t * DIM, DIM)]
                mm = ve.tensor_scalar(yt, yt, mv[:, 1, t, 0:1], rstd[:, 1, t:t + 1], ALU.subtract, ALU.mult)
            mm.then_inc(y_normed, 1)

        def evacuate(n, use, idx, lag):
            m = n - lag
            if not on(m):
                return
            bank_ = mm_bank(use, idx)
            if use in ("zt", "ct"):
                hi, lo, got, done = ((zTh, zTl, zth_ready, ztl_ready) if use == "zt" else
                                     (cTh, cTl, cth_ready, ctl_ready))
                dve.wait_ge(got, m + 1)
                ve.tensor_tensor(lo[:].rearrange("p k s -> p (k s)"), bank_[:],
                                 hi[:].bitcast(F32).rearrange("p k s -> p (k s)"), ALU.subtract).then_inc(done, 1)
            elif use == "qk":
                i = 2 * m + idx
                dve.wait_ge(proj_done, i + 1)
                if later(i):
                    dve.wait_ge(parts_l, 2 * i)
                qkf = qk[:].rearrange("p w h d -> p w (h d)")
                ve.scalar_tensor_tensor(out=qkf[:, 0], in0=bank_[:, 0:DIM], scalar=XDH ** -0.5, in1=bias[:, 0:DIM],
                                        op0=ALU.mult, op1=ALU.add)
                ve.tensor_tensor(qkf[:, 1], bank_[:, DIM:2 * DIM], bias[:, DIM:2 * DIM], ALU.add).then_inc(qk_biased, 1)
                dve.wait_ge(parts_h, 2 * i + 2)
                for w in range(2):
                    hi, lo = part_views(idx, w)
                    src = qk[:, w].unsqueeze(2).broadcast_to([P, XHEADS, 2, XDH])
                    ve.tensor_tensor(lo, src, hi.bitcast(F32), ALU.subtract).then_inc(parts_l, 1)
            elif use == "v":
                dve.wait_ge(v_done, m + 1)
                if later(m):
                    dve.wait_ge(pv_done, XPAIRS * m)
                ve.tensor_tensor(v[:], bank_[:].rearrange("p (t d) -> p t d", t=TILES),
                                 bias[:, 2 * DIM:3 * DIM].unsqueeze(1).broadcast_to([P, TILES, DIM]),
                                 ALU.add).then_inc(v_ready, 1)
            elif use == "st":
                dve.wait_ge(st_done, 8 * m + idx + 1)
                if later(m):
                    dve.wait_ge(sim_done, 2 * (XPAIRS * (m - 1) + idx + 1))
                ve.tensor_copy(stacked[:, idx].rearrange("p w s -> p (w s)"), bank_[:]).then_inc(st_moved, 1)
            elif use == "ot":
                dve.wait_ge(oth_ready, 2 * m + idx + 1)
                ve.tensor_tensor(otl[:, idx, :], bank_[:, 0:SEQ], oth[:, idx, :].bitcast(F32),
                                 ALU.subtract).then_inc(otl_ready, 1)
            elif use == "wo":
                dve.wait_ge(wo_done, m + 1)
                ve.tensor_tensor(y_of(m), bank_[:], y_of(m), ALU.add).then_inc(wo_read, 1)
                dve.wait_ge(wo_read, m + 1)
                y3 = y_of(m).rearrange("p (t d) -> p t d", t=TILES)
                ve.tensor_tensor(y3, y3, bias[:, 3 * DIM:4 * DIM].unsqueeze(1).broadcast_to([P, TILES, DIM]),
                                 ALU.add).then_inc(x_summed, 1)
                if first:
                    dve.wait_ge(x_summed, m + 1)
                    settle(dve)
                    stats(m, 1, stats2_ready, mv2_ready)

        def maxima(g, r):
            for h in range(2):
                dve.wait_ge(sim_done, 2 * g + h + 1)
                ve.tensor_reduce(nmax[:, r, h, :], ps_sim[h][:].rearrange("p (t s) -> p t s", t=TILES), AX.X, ALU.max,
                                 negate=True).then_inc(max_ready, 1)

        def move_turned(g):
            dve.wait_ge(pt_done, 2 * g + 2)
            if later(g):
                dve.wait_ge(pv_done, g)
            ve.tensor_copy(probsT[:, 1].rearrange("p c s -> p (c s)"), ps_pt[1][:]).then_inc(pt_moved_b, 1)

        def outputs(m, k):
            heads = slice(8 * k, 8 * k + 8)
            dve.wait_ge(pv_done, XPAIRS * m + 4 * k + 4)
            ve.reciprocal(rinv[:, :, heads], rsum[:, :, heads]).then_inc(rinv_ready, 1)
            dve.wait_ge(rinv_ready, 2 * m + k + 1)
            if later(m):
                dve.wait_ge(ot_done, 2 * (m - 1) + k + 1)
            for t in range(TILES):
                mm = ve.tensor_tensor(o_tok[:, k, t, :].rearrange("p (h d) -> p h d", d=XDH),
                                      ps_o[k][:, t * P:(t + 1) * P].rearrange("p (h d) -> p h d", d=XDH),
                                      rinv[:, t, heads].unsqueeze(2).broadcast_to([P, 8, XDH]), ALU.mult)
            mm.then_inc(o_ready, 1)

        def step(n):
            for j, slot in enumerate(X_DVE_SLOTS):
                for what, idx, lag in slot:
                    m = n - lag
                    if what in X_BANK_USES:
                        evacuate(n, what, idx, lag)
                    elif what in X_PAIR_WORK:
                        g = XPAIRS * (n - 1) + j - lag
                        if not pair_on(g):
                            continue
                        if what == "move turned":
                            move_turned(g)
                        elif what == "maxima":
                            maxima(g, (j - lag) % 4)
                    elif not on(m):
                        continue
                    elif what == "rows in":
                        rows_in(m)
                    elif what == "norm in":
                        norm_in(m)
                    elif what == "norm out":
                        if first:
                            norm_out(m)
                    elif what == "outputs":
                        outputs(m, idx)

        dve.wait_ge(const_in, 16 * 3)
        ve.tensor_scalar(bias[:, 0:DIM], bias[:, 0:DIM], XDH ** -0.5, None, ALU.mult).then_inc(bias_scaled, 1)
        dve.wait_ge(bias_scaled, 1)
        for k in range(KD):
            dve.wait_ge(wh_ready, k + 1)
            ve.tensor_tensor(w_l[:, k, :], w_raw[:, k, :], w_h[:, k, :].bitcast(F32), ALU.subtract).then_inc(wl_ready, 1)
        for n in EDGES[0]:
            step(n)
        with dve.Fori(*FULL) as n:
            step(n)
        for n in EDGES[1]:
            step(n)

    @block.scalar
    def _(act):
        sc = nc.scalar

        def exponentials(g, p, r):
            for h in range(2):
                act.wait_ge(max_ready, 2 * g + h + 1)
                if later(g):
                    act.wait_ge(pt_done, 2 * (g - 1) + h + 1)
                for t in range(TILES):
                    head = 2 * p + h
                    mm = sc.activation(probs[:, h, t, :], ps_sim[h][:, t * SEQ:(t + 1) * SEQ], ACT.Exp,
                                       bias=nmax[:, r, h, t:t + 1], accum_out=rsum[:, t, head:head + 1])
                mm.then_inc(exp_done, 1)

        def move_turned(g):
            act.wait_ge(pt_done, 2 * g + 1)
            if later(g):
                act.wait_ge(pv_done, g)
            sc.copy(probsT[:, 0].rearrange("p c s -> p (c s)"), ps_pt[0][:]).then_inc(pt_moved_a, 1)

        def evacuate(n, use, idx, lag):
            m = n - lag
            if not on(m):
                return
            bank_ = mm_bank(use, idx)
            if use in ("zt", "ct"):
                hi, done, ready = (zTh, zt_done, zth_ready) if use == "zt" else (cTh, ct_done, cth_ready)
                act.wait_ge(done, m + 1)
                if later(m):
                    act.wait_ge(v_done, m)
                sc.copy(hi[:].rearrange("p k s -> p (k s)"), bank_[:]).then_inc(ready, 1)
            elif use == "qk":
                i = 2 * m + idx
                act.wait_ge(qk_biased, i + 1)
                if later(m):
                    act.wait_ge(st_done, 8 * m)
                for w in range(2):
                    sc.copy(part_views(idx, w)[0], qk[:, w].unsqueeze(2).broadcast_to([P, XHEADS, 2, XDH])).then_inc(parts_h, 1)
            elif use == "ot":
                act.wait_ge(ot_done, 2 * m + idx + 1)
                if later(m):
                    act.wait_ge(wo_done, m)
                sc.copy(oth[:, idx, :], bank_[:, 0:SEQ]).then_inc(oth_ready, 1)

        def step(n):
            for j, slot in enumerate(X_ACT_SLOTS):
                for what, idx, lag in slot:
                    if what in X_BANK_USES:
                        evacuate(n, what, idx, lag)
                        continue
                    g = XPAIRS * (n - 1) + j - lag
                    if not pair_on(g):
                        continue
                    if what == "move turned":
                        move_turned(g)
                    elif what == "exponentials":
                        exponentials(g, (j - lag) % XPAIRS, (j - lag) % 4)

        act.wait_ge(const_in, 16 * 3)
        for k in range(KD):
            sc.copy(w_h[:, k, :], w_raw[:, k, :]).then_inc(wh_ready, 1)
        for n in EDGES[0]:
            step(n)
        with act.Fori(*FULL) as n:
            step(n)
        for n in EDGES[1]:
            step(n)

    @block.gpsimd
    def _(pool):
        gp = nc.gpsimd

        def inverse_deviation(m, which, got, part_signal, signal):
            pool.wait_ge(got, m + 1)
            gp.tensor_scalar(vareps[:, which, :], mv[:, which, :, 1], 1.0, EPS, ALU.mult, ALU.add).then_inc(part_signal, 1)
            pool.wait_ge(part_signal, m + 1)
            gp.tensor_tensor(rstd[:, which, :], vareps[:, which, :], minus_half[:], ALU.pow).then_inc(signal, 1)

        gp.memset(minus_half[:], -0.5).then_inc(minus_ready, 1)
        pool.wait_ge(minus_ready, 1)
        jobs = pool_jobs(pool)
        for n in range(BATCH + 2):
            if on(n):
                inverse_deviation(n, 0, mv_ready, rs_part, rstd_ready)
            for _ in range(2 if n else 1):
                next(jobs, None)
            if first and on(n - 2):
                inverse_deviation(n - 2, 1, mv2_ready, rs2_part, rstd2_ready)
            for _ in range(2):
                next(jobs, None)
        for _ in jobs:
            pass

    @block.sync
    def _(sp):
        x_rows = d_x.rearrange("(s t p) d -> s p t d", t=TILES, p=P)
        c_rows = d_ctx.rearrange("(s t p) d -> s p t d", t=TILES, p=P)
        sum_rows = d_sum.rearrange("(s t p) d -> s p t d", t=TILES, p=P) if first else None

        def step(n):
            if on(n):
                if later(n) and not first:
                    sp.wait_ge(x_ready, n)
                if later(n) and first:
                    sp.wait_ge(x_in, 16 * n)
                settle(sp)
                dst = y_of(n) if first else x_in_tile[:]
                sp.dma_start(dst.rearrange("p (t d) -> p t d", t=TILES), x_rows[n]).then_inc(x_in, 16)
                if later(n):
                    sp.wait_ge(ct_done, n)
                settle(sp)
                sp.dma_start(c_in_tile[:], c_rows[n]).then_inc(c_in, 16)
            if first and on(n - 2):
                sp.wait_ge(x_summed, n - 1)
                settle(sp)
                sp.dma_start(sum_rows[n - 2], y_of(n - 2).rearrange("p (t d) -> p t d", t=TILES)).then_inc(sum_out, 16)

        sp.dma_start(ident[:], d_ident).then_inc(const_in, 16)
        sp.dma_start(w_raw[:], d_w.rearrange("(k p) c -> p k c", p=P)).then_inc(const_in, 16)
        sp.dma_start(bias[:], d_bias).then_inc(const_in, 16)
        for n in range(BATCH + 2):
            step(n)
        if first:
            sp.wait_ge(sum_out, 16 * BATCH)


def ffn_phase(nc, ctx, y, d_ident, d_out, wd_h, wd_l):

    def sb(name, shape, dt=F32):
        return ctx.enter_context(nc.sbuf_tensor(name, shape, dt))

    def sem(name):
        return nc.alloc_semaphore(name)

    def bank(name):
        return ctx.enter_context(nc.psum_tensor(name, [P, 512], F32))

    ident = sb("f_ident", [P, P])
    minus_half = sb("f_minus_half", [P, TILES])
    z = sb("f_z", [P, TILES, DIM])
    bst, mv = sb("f_bst", [P, TILES, 6]), sb("f_mv", [P, TILES, 2])
    vareps, rstd = sb("f_vareps", [P, TILES]), sb("f_rstd", [P, TILES])
    zTh, zTl = sb("f_zTh", [P, KD, SEQ], F32R), sb("f_zTl", [P, KD, SEQ], F32R)
    hid = sb("f_hid", [P, HT, SEQ])
    hh, hl = sb("f_hh", [P, HT, SEQ], F32R), sb("f_hl", [P, HT, SEQ], F32R)
    out_tile = sb("f_out", [P, TILES, DIM])
    GROUPS = HT // 2
    ps_gate = [bank(f"f_ps_gate{i}") for i in range(GROUPS)]
    ps_up = [bank(f"f_ps_up{i}") for i in range(GROUPS)]
    ps_turn, ps_down = bank("f_ps_turn"), bank("f_ps_down")

    zt_done, gate_done, up_done, down_done = sem("f_zt_done"), sem("f_gate_done"), sem("f_up_done"), sem("f_down_done")
    stats_ready, mv_ready, z_ready, ztl_ready = (sem("f_stats_ready"), sem("f_mv_ready"), sem("f_z_ready"),
                                                 sem("f_ztl_ready"))
    h_ready, hl_ready, out_ready = sem("f_h_ready"), sem("f_hl_ready"), sem("f_out_ready")
    zth_ready, silu_done, hh_ready = sem("f_zth_ready"), sem("f_silu_done"), sem("f_hh_ready")
    minus_ready, rs_part, rstd_ready = sem("f_minus_ready"), sem("f_rs_part"), sem("f_rstd_ready")
    const_in, out_stored = sem("f_const_in"), sem("f_out_stored")

    block = ctx.enter_context(nc.Block())
    FULL = (2, BATCH)

    def on(m):
        return not isinstance(m, int) or 0 <= m < BATCH

    def later(m):
        return not isinstance(m, int) or m > 0

    def steps(eng, step):
        for n in range(FULL[0]):
            step(n)
        with eng.Fori(*FULL) as n:
            step(n)
        step(BATCH)

    def y_tile(m, t):
        return y[:, bass.ds(m * TILES * DIM + t * DIM, DIM)]

    def wcols(w, at, k, f):
        return w[:, (at * KD + k) * HID + f * P:(at * KD + k) * HID + (f + 1) * P]

    @block.tensor
    def _(pe):
        def split3(out, lhs_h, lhs_l, rhs_h, rhs_l, start, stop, **kw):
            pe.matmul(out, lhs_h, rhs_h, start=start, stop=False, **kw)
            pe.matmul(out, lhs_h, rhs_l, start=False, stop=False, **kw)
            return pe.matmul(out, lhs_l, rhs_h, start=False, stop=stop, **kw)

        def step(n):
            m = n - 1
            if on(m):
                pe.wait_ge(ztl_ready, m + 1)
                for i in range(GROUPS):
                    for at, ps, read, done in ((0, ps_gate, silu_done, gate_done), (1, ps_up, h_ready, up_done)):
                        if later(m):
                            pe.wait_ge(read, GROUPS * (m - 1) + i + 1)
                        for j in range(2):
                            for k in range(KD):
                                mm = split3(ps[i][:, j * SEQ:(j + 1) * SEQ], wcols(wd_h, at, k, 2 * i + j),
                                            wcols(wd_l, at, k, 2 * i + j), zTh[:, k, :], zTl[:, k, :],
                                            k == 0, k == KD - 1)
                        mm.then_inc(done, 1)
            if on(n):
                pe.wait_ge(z_ready, n + 1)
                if later(n):
                    pe.wait_ge(ztl_ready, n)
                for k in range(KD):
                    for t in range(TILES):
                        mm = pe.transpose(ps_turn[:, k * SEQ + t * P:k * SEQ + (t + 1) * P], z[:, t, k * P:(k + 1) * P],
                                          ident[:])
                mm.then_inc(zt_done, 1)
            if on(m):
                if later(m):
                    pe.wait_ge(out_ready, m)
                for f in range(HT):
                    if f % 2 == 0:
                        pe.wait_ge(hl_ready, GROUPS * m + f // 2 + 1)
                    cols = slice((2 * KD * HID) + f * DIM, (2 * KD * HID) + (f + 1) * DIM)
                    for t in range(TILES):
                        mm = split3(ps_down[:, t * DIM:(t + 1) * DIM], hh[:, f, t * P:(t + 1) * P],
                                    hl[:, f, t * P:(t + 1) * P], wd_h[:, cols], wd_l[:, cols],
                                    f == 0 and t == 0, f == HT - 1, skip_group_check=True)
                mm.then_inc(down_done, 1)

        pe.wait_ge(const_in, 16)
        steps(pe, step)

    @block.vector
    def _(dve):
        ve = nc.vector

        def step(n):
            m = n - 1
            if on(n):
                for t in range(TILES):
                    mm = ve.bn_stats(bst[:, t, :], y_tile(n, t))
                mm.then_inc(stats_ready, 1)
                dve.wait_ge(stats_ready, n + 1)
                dve.nop(nofuse=True)
                for t in range(TILES):
                    mm = ve.bn_aggr(mv[:, t, :], bst[:, t, :])
                mm.then_inc(mv_ready, 1)
            if on(m):
                for i in range(GROUPS):
                    dve.wait_ge(up_done, GROUPS * m + i + 1)
                    dve.wait_ge(silu_done, GROUPS * m + i + 1)
                    rows = hid[:, 2 * i:2 * i + 2, :].rearrange("p f s -> p (f s)")
                    ve.tensor_tensor(rows, ps_up[i][:], rows, ALU.mult).then_inc(h_ready, 1)
            if on(n):
                dve.wait_ge(rstd_ready, n + 1)
                if later(n):
                    dve.wait_ge(zt_done, n)
                for t in range(TILES):
                    mm = ve.tensor_scalar(z[:, t, :], y_tile(n, t), mv[:, t, 0:1], rstd[:, t:t + 1],
                                          ALU.subtract, ALU.mult)
                mm.then_inc(z_ready, 1)
            if on(m):
                for i in range(GROUPS):
                    dve.wait_ge(hh_ready, GROUPS * m + i + 1)
                    part = slice(2 * i, 2 * i + 2)
                    ve.tensor_tensor(hl[:, part, :], hid[:, part, :], hh[:, part, :].bitcast(F32),
                                     ALU.subtract).then_inc(hl_ready, 1)
            if on(n):
                dve.wait_ge(zth_ready, n + 1)
                ve.tensor_tensor(zTl[:].rearrange("p k s -> p (k s)"), ps_turn[:],
                                 zTh[:].bitcast(F32).rearrange("p k s -> p (k s)"), ALU.subtract).then_inc(ztl_ready, 1)
            if on(m):
                dve.wait_ge(down_done, m + 1)
                if later(m):
                    dve.wait_ge(out_stored, 16 * m)
                ve.tensor_tensor(out_tile[:].rearrange("p t d -> p (t d)"), ps_down[:],
                                 y[:, bass.ds(m * TILES * DIM, TILES * DIM)], ALU.add).then_inc(out_ready, 1)

        steps(dve, step)

    @block.scalar
    def _(act):
        sc = nc.scalar

        def step(n):
            m = n - 1
            if on(m):
                for i in range(GROUPS):
                    act.wait_ge(gate_done, GROUPS * m + i + 1)
                    if later(m):
                        act.wait_ge(hl_ready, GROUPS * m)
                    sc.activation(hid[:, 2 * i:2 * i + 2, :].rearrange("p f s -> p (f s)"), ps_gate[i][:],
                                  ACT.Silu).then_inc(silu_done, 1)
                for i in range(GROUPS):
                    act.wait_ge(h_ready, GROUPS * m + i + 1)
                    if later(m):
                        act.wait_ge(down_done, m)
                    part = slice(2 * i, 2 * i + 2)
                    sc.copy(hh[:, part, :], hid[:, part, :]).then_inc(hh_ready, 1)
            if on(n):
                act.wait_ge(zt_done, n + 1)
                if later(n):
                    act.wait_ge(up_done, GROUPS * n)
                sc.copy(zTh[:].rearrange("p k s -> p (k s)"), ps_turn[:]).then_inc(zth_ready, 1)

        steps(act, step)

    @block.gpsimd
    def _(pool):
        gp = nc.gpsimd

        def step(n):
            if not on(n):
                return
            pool.wait_ge(mv_ready, n + 1)
            pool.nop(nofuse=True)
            gp.tensor_scalar(vareps[:], mv[:, :, 1], 1.0, EPS, ALU.mult, ALU.add).then_inc(rs_part, 1)
            pool.wait_ge(rs_part, n + 1)
            gp.tensor_tensor(rstd[:], vareps[:], minus_half[:], ALU.pow).then_inc(rstd_ready, 1)

        gp.memset(minus_half[:], -0.5).then_inc(minus_ready, 1)
        pool.wait_ge(minus_ready, 1)
        steps(pool, step)

    @block.sync
    def _(sp):
        out_rows = d_out.rearrange("(s t p) d -> s p t d", t=TILES, p=P)
        sp.dma_start(ident[:], d_ident).then_inc(const_in, 16)
        for m in range(BATCH):
            sp.wait_ge(out_ready, m + 1)
            sp.dma_start(out_rows[m], out_tile[:]).then_inc(out_stored, 16)
        sp.wait_ge(out_stored, 16 * BATCH)


def split_ffn_weights(nc, pool, raw_int, raw, d_w, wd_h, wd_l, sems):
    gp = nc.gpsimd
    int_in, scaled, w_hi, w_done = sems
    for u in range(DW_UNITS):
        cols = slice(512 * u, 512 * (u + 1))
        if u:
            pool.wait_ge(w_done, u)
        pool.dma_start(raw_int[:], d_w[:, cols]).then_inc(int_in, 16)
        yield
        pool.wait_ge(int_in, 16 * (u + 1))
        gp.tensor_scalar(raw[:], raw_int[:], 1.0, 1.0 / 127.0, ALU.mult, ALU.mult).then_inc(scaled, 1)
        pool.wait_ge(scaled, u + 1)
        gp.tensor_copy(wd_h[:, cols], raw[:]).then_inc(w_hi, 1)
        pool.wait_ge(w_hi, u + 1)
        gp.tensor_tensor(wd_l[:, cols], raw[:], wd_h[:, cols].bitcast(F32), ALU.subtract).then_inc(w_done, 1)
        yield


def split_stack_weights(nc, pool, raw, d_w, wh, wl, sems):
    gp = nc.gpsimd
    raw_in, w_hi, w_done = sems
    for u in range(NU):
        part = slice(OFFS[u], OFFS[u] + UNITS[u])
        if u:
            pool.wait_ge(w_done, u)
        pool.dma_start(raw[:, 0:UNITS[u]], d_w[:, part]).then_inc(raw_in, 16)
        yield
        pool.wait_ge(raw_in, 16 * (u + 1))
        gp.tensor_copy(wh[:, part], raw[:, 0:UNITS[u]]).then_inc(w_hi, 1)
        pool.wait_ge(w_hi, u + 1)
        gp.tensor_tensor(wl[:, part], raw[:, 0:UNITS[u]], wh[:, part].bitcast(F32), ALU.subtract).then_inc(w_done, 1)
        yield


def transformer_kernel(nc, d_x, d_ctx, d_a_w, d_a_bias, d_stack_w, d_prm, d_qks, d_b2, d_const, d_c_w, d_c_bias,
                       d_ffn_w, d_ident, d_out):
    d_sum = nc.dram_tensor("x_after_attention", [BATCH * SEQ, DIM], F32).ap()
    with ExitStack() as whole:
        y = whole.enter_context(nc.sbuf_tensor("y", [P, BATCH * TILES * DIM], F32))
        with ExitStack() as weights:
            wh = weights.enter_context(nc.sbuf_tensor("wh", [P, WCOLS], F32R))
            wl = weights.enter_context(nc.sbuf_tensor("wl", [P, WCOLS], F32R))
            with nc.cleanup_on_exit(), ExitStack() as ctx:
                raw = ctx.enter_context(nc.sbuf_tensor("a_raw", [P, 512], F32))
                sems = [nc.alloc_semaphore(s) for s in ("a_raw_in", "a_raw_hi", "a_raw_done")]
                attend_phase(nc, ctx, y, d_x, d_ctx, d_a_w, d_a_bias, d_ident, d_sum, True,
                             lambda pool: split_stack_weights(nc, pool, raw, d_stack_w, wh, wl, sems))
            with nc.cleanup_on_exit(), ExitStack() as ctx:
                stack_phase(nc, ctx, y, wh, wl, d_stack_w, d_prm, d_qks, d_b2, d_const)
        wd_h = whole.enter_context(nc.sbuf_tensor("wd_h", [P, 512 * DW_UNITS], F32R))
        wd_l = whole.enter_context(nc.sbuf_tensor("wd_l", [P, 512 * DW_UNITS], F32R))
        with nc.cleanup_on_exit(), ExitStack() as ctx:
            raw = ctx.enter_context(nc.sbuf_tensor("c_raw", [P, 512], F32))
            raw_int = ctx.enter_context(nc.sbuf_tensor("c_raw_int", [P, 512], mybir.dt.int32))
            sems = [nc.alloc_semaphore(s) for s in ("c_int_in", "c_scaled", "c_raw_hi", "c_raw_done")]
            attend_phase(nc, ctx, y, d_sum, d_ctx, d_c_w, d_c_bias, d_ident, None, False,
                         lambda pool: split_ffn_weights(nc, pool, raw_int, raw, d_ffn_w, wd_h, wd_l, sems))
        with nc.cleanup_on_exit(), ExitStack() as ctx:
            ffn_phase(nc, ctx, y, d_ident, d_out, wd_h, wd_l)


def shape_constants():
    half = np.arange(0, DH, 2, dtype=np.float32)
    inv_freq = (np.float32(1.0) / np.float32(10000.0) ** (half / np.float32(DH))).astype(np.float32)
    t = np.arange(SEQ, dtype=np.float32)
    freqs = (t[:, None] * inv_freq[None, :]).astype(np.float32)
    base = ((half + np.float32(0.4 * DH)) / np.float32(1.4 * DH)).astype(np.float32)
    power = ((t - SEQ // 2) / np.float32(WINDOW // 2)).astype(np.float32)
    scale = (base[None, :] ** power[:, None]).astype(np.float32)
    cos, sin = np.cos(freqs), np.sin(freqs)
    inv = (np.float32(1.0) / scale).astype(np.float32)
    tables = np.stack([cos * scale, sin * scale, cos * inv, sin * inv]).astype(np.float32)
    tables = tables.reshape(4, TILES, P, 32).transpose(2, 0, 1, 3).reshape(P, -1)
    r = np.arange(P)[:, None]
    masks = []
    for q0, k0, w in ((0, 0, P), (P, P - WINDOW, P + WINDOW)):
        d = (r + q0) - (np.arange(w)[None, :] + k0)
        masks.append(np.where((d >= 0) & (d <= WINDOW), 0.0, -1.0e30).astype(np.float32))
    return np.ascontiguousarray(np.concatenate([tables] + masks + [np.eye(P, dtype=np.float32)], axis=1))


def pack_stack_weights(Wqkv, Wo, W1, W2):
    out = np.zeros((DEPTH, P, WCOLS), Wqkv.dtype)
    kt = Wqkv.reshape(DEPTH, KD, P, 3 * INNER)
    for c, at in enumerate((0, INNER, 512, INNER + 512, 2 * INNER, 2 * INNER + 512)):
        for k in range(KD):
            o = OFFS[U_QKV + 2 * c + k]
            out[:, :, o:o + 512] = kt[:, k, :, at:at + 512]
    wo = Wo.reshape(DEPTH, PAIRS, P, DIM)
    for i in range(4):
        for q in range(2):
            o = OFFS[U_WO + i] + q * DIM
            out[:, :, o:o + DIM] = wo[:, 2 * i + q]
    w1 = np.zeros((DEPTH, KD, P, 2, FT * FP), W1.dtype)
    w1[..., :FF] = W1.reshape(DEPTH, KD, P, 2, FF)
    for i in range(3):
        for k in range(KD):
            for which, u in ((1, U_GATE), (0, U_UP)):
                o = OFFS[u + i] + k * 2 * FP
                out[:, :, o:o + 2 * FP] = w1[:, k, :, which, 2 * FP * i:2 * FP * (i + 1)]
    w2 = np.zeros((DEPTH, FT * FP, DIM), W2.dtype)
    w2[:, :FF] = W2
    w2 = w2.reshape(DEPTH, FT, FP, DIM)
    for i in range(3):
        for j in range(2):
            o = OFFS[U_W2 + i] + j * DIM
            out[:, :FP, o:o + DIM] = w2[:, 2 * i + j]
    return np.ascontiguousarray(out.transpose(1, 0, 2).reshape(P, DEPTH * WCOLS))


def pack_stack_params(ln_g, ln_b, b1):
    out = np.zeros((P, DEPTH, NPRM), ln_g.dtype)
    out[:, :, 0:KD] = ln_g.reshape(DEPTH, KD, P).transpose(2, 0, 1)
    out[:, :, KD:2 * KD] = ln_b.reshape(DEPTH, KD, P).transpose(2, 0, 1)
    for which, at in ((1, 2 * KD), (0, 2 * KD + FT)):
        b = np.zeros((DEPTH, FT * FP), b1.dtype)
        b[:, :FF] = b1[:, which * FF:(which + 1) * FF]
        out[:FP, :, at:at + FT] = b.reshape(DEPTH, FT, FP).transpose(2, 0, 1)
    return np.ascontiguousarray(out.reshape(P, -1))


def kernel(**inputs):
    import concourse.bacc as bacc
    from concourse.bass_utils import run_bass_kernel_spmd

    a = {k: np.asarray(x) for k, x in inputs.items()}

    def rows(vectors):
        return np.ascontiguousarray(np.broadcast_to(np.concatenate([x.reshape(-1) for x in vectors]), (P, sum(x.size for x in vectors))))

    def hidden_major(w):
        return w.T.reshape(KD, P, HID).transpose(1, 0, 2).reshape(P, KD * HID)

    f = {k[len("L0_ffn_"):]: x for k, x in a.items() if k.startswith("L0_ffn_")}
    p, q = "L0_xattn_", "L1_xattn_"
    arrays = {
        "x": a["x"].reshape(BATCH * SEQ, DIM),
        "ctx": a["ctx_1024"].reshape(BATCH * SEQ, DIM),
        "a_w": np.concatenate([a[p + s].T for s in ("wq_w", "wk_w", "wv_w", "wo_w")], axis=1),
        "a_bias": rows([a[p + s] for s in ("wq_b", "wk_b", "wv_b", "wo_b")]),
        "stack_w": pack_stack_weights(f["Wqkv"], f["Wo"], f["W1"], f["W2"]),
        "prm": pack_stack_params(f["ln_g"], f["ln_b"], f["b1"]),
        "qks": rows([x[i] for i in range(DEPTH) for x in (f["q_scale"], f["k_scale"])]),
        "b2": rows([f["b2"]]),
        "const": shape_constants(),
        "c_w": np.concatenate([a[q + s] for s in ("Wq", "Wk", "Wv", "Wo")], axis=1),
        "c_bias": rows([a[q + s] for s in ("bq", "bk", "bv", "bo")]),
        "ffn_w": np.concatenate([hidden_major(a["L1_ffn_w_gate"]), hidden_major(a["L1_ffn_w_up"]),
                                 a["L1_ffn_w_down"].T.reshape(HT, P, DIM).transpose(1, 0, 2).reshape(P, HT * DIM)],
                                axis=1),
        "ident": np.eye(P, dtype=np.float32),
    }
    nc = bacc.Bacc("TRN2", target_bir_lowering=False, num_devices=1)
    feeds, args = {}, []
    for name, x in arrays.items():
        x = np.ascontiguousarray(x)
        feeds[f"in_{name}"] = x
        args.append(nc.dram_tensor(f"in_{name}", x.shape, mybir.dt.from_np(x.dtype), kind="ExternalInput").ap())
    args.append(nc.dram_tensor("out_x", [BATCH * SEQ, DIM], F32, kind="ExternalOutput").ap())
    transformer_kernel(nc, *args)
    r = run_bass_kernel_spmd(nc, [feeds], core_ids=[0])
    return r.results[0]["out_x"].reshape(BATCH, SEQ, DIM)
```

```python
from contextlib import ExitStack

import numpy as np

import concourse.bass as bass
from concourse import mybir

F32 = mybir.dt.float32
F32R = mybir.dt.float32r
BF16 = mybir.dt.bfloat16
ALU = mybir.AluOpType
ACT = mybir.ActivationFunctionType
AX = mybir.AxisListType

P = 128
BATCH, SEQ, DIM = 8, 256, 256
TILES = SEQ // P
KD = DIM // P
DEPTH, HEADS, DH = 6, 16, 64
PAIRS = HEADS // 2
INNER = HEADS * DH
FF = 682
FT = 6
FP = 114
WINDOW = 64
QKS = 8.0
SPANS = P + (P + WINDOW)
PCOLS = 3 * P

UNITS = [512] * 16 + [KD * 2 * FP] * 6 + [512] * 3
OFFS = [sum(UNITS[:u]) for u in range(len(UNITS))]
NU = len(UNITS)
WCOLS = sum(UNITS)
U_QKV, U_WO, U_GATE, U_UP, U_W2 = 0, 12, 16, 19, 22
U_LATE = U_UP
NPRM = 2 * KD + 2 * FT
CONSTS = 4

EPS = 1e-5
STEPS = DEPTH * BATCH

BANK_USES = ("wo", "w2", "up", "qk", "v", "tr", "xt", "xnt", "gate")
PAIR_WORK = ("mask", "invert", "outputs", "low outputs", "exponentials", "move turned", "high outputs")
PE_SLOTS = [
    [("up", 1, 3), ("weigh values", 0, 2), ("tr", 3, 1), ("turn probs", 0, 1), ("scores", 0, 0), ("up", 2, 3),
     ("qk", 6, 1), ("turn outputs", 0, 2), ("w2", 0, 3), ("tr", 4, 1)],
    [("weigh values", 0, 2), ("turn probs", 0, 1), ("scores", 0, 0), ("w2_last", 0, 3), ("qk", 7, 1),
     ("turn outputs", 0, 2), ("v", 0, 1), ("v", 1, 1), ("wo", 2, 2)],
    [("weigh values", 0, 2), ("turn probs", 0, 1), ("scores", 0, 0), ("turn outputs", 0, 2)],
    [("wo", 3, 2), ("tr", 5, 1), ("v", 2, 1), ("v", 3, 1), ("xt", 0, 0), ("weigh values", 0, 2), ("tr", 6, 1),
     ("turn probs", 0, 1), ("scores", 0, 0), ("turn outputs", 0, 2), ("tr", 7, 1), ("qk", 0, 0)],
    [("weigh values", 0, 2), ("turn probs", 0, 1), ("scores", 0, 0), ("wo", 0, 1), ("qk", 1, 0), ("xnt", 0, 2),
     ("turn outputs", 0, 2)],
    [("qk", 2, 0), ("weigh values", 0, 2), ("turn probs", 0, 1), ("scores", 0, 0), ("turn outputs", 0, 2)],
    [("qk", 3, 0), ("gate", 0, 2), ("weigh values", 0, 2), ("turn probs", 0, 1), ("scores", 0, 0), ("gate", 1, 2),
     ("turn outputs", 0, 2), ("gate", 2, 2), ("tr", 0, 0), ("qk", 4, 0), ("tr", 1, 0), ("up", 0, 2)],
    [("weigh values", 0, 2), ("turn probs", 0, 1), ("scores", 0, 0), ("wo", 1, 1), ("turn outputs", 0, 2),
     ("tr", 2, 0), ("qk", 5, 0)],
]
DVE_SLOTS = [
    [("outputs", 0, 2), ("low hidden", 1, 3), ("mask", 0, 0), ("up", 2, 3), ("low outputs", 0, 2), ("invert", 0, 1)],
    [("low hidden", 2, 3), ("qk", 6, 1), ("outputs", 0, 2), ("mask", 0, 0), ("add ffn", 0, 3), ("qk", 7, 1),
     ("invert", 0, 1), ("low outputs", 0, 2)],
    [("outputs", 0, 2), ("wo", 2, 2), ("mask", 0, 0), ("wo", 3, 2), ("invert", 0, 1), ("low outputs", 0, 2)],
    [("norm keys", 1, 1), ("xt", 0, 0), ("outputs", 0, 2), ("mask", 0, 0), ("low outputs", 0, 2), ("row stats", 0, 2),
     ("invert", 0, 1)],
    [("outputs", 0, 2), ("norm rows", 0, 2), ("mask", 0, 0), ("qk", 0, 0), ("wo", 0, 1), ("xnt", 0, 2),
     ("invert", 0, 1), ("low outputs", 0, 2)],
    [("qk", 1, 0), ("outputs", 0, 2), ("low rows", 0, 2), ("mask", 0, 0), ("low outputs", 0, 2), ("invert", 0, 1)],
    [("qk", 2, 0), ("gate", 0, 2), ("outputs", 0, 2), ("qk", 3, 0), ("mask", 0, 0), ("gate", 1, 2),
     ("low outputs", 0, 2), ("gate", 2, 2), ("invert", 0, 1), ("qk", 4, 0)],
    [("outputs", 0, 2), ("norm keys", 0, 0), ("up", 0, 2), ("mask", 0, 0), ("wo", 1, 1), ("low outputs", 0, 2),
     ("up", 1, 2), ("qk", 5, 0), ("invert", 0, 1), ("low hidden", 0, 2)],
]
ACT_SLOTS = [
    [("qk", 5, 1), ("tr", 3, 1), ("up", 1, 3), ("move turned", 0, 1), ("qk", 6, 1), ("high outputs", 0, 2),
     ("exponentials", 0, 0), ("up", 2, 3), ("tr", 4, 1)],
    [("move turned", 0, 1), ("qk", 7, 1), ("exponentials", 0, 0), ("high outputs", 0, 2), ("v", 0, 1), ("v", 1, 1)],
    [("move turned", 0, 1), ("exponentials", 0, 0), ("tr", 5, 1), ("high outputs", 0, 2), ("v", 2, 1), ("xt", 0, 0),
     ("tr", 6, 1), ("v", 3, 1)],
    [("move turned", 0, 1), ("high outputs", 0, 2), ("exponentials", 0, 0), ("tr", 7, 1), ("qk", 0, 0)],
    [("move turned", 0, 1), ("exponentials", 0, 0), ("high outputs", 0, 2)],
    [("qk", 1, 0), ("xnt", 0, 2), ("move turned", 0, 1), ("qk", 2, 0), ("high outputs", 0, 2), ("exponentials", 0, 0),
     ("qk", 3, 0)],
    [("move turned", 0, 1), ("high outputs", 0, 2), ("tr", 0, 0), ("exponentials", 0, 0), ("qk", 4, 0)],
    [("gelu", 0, 2), ("tr", 1, 0), ("move turned", 0, 1), ("up", 0, 2), ("high outputs", 0, 2), ("tr", 2, 0),
     ("exponentials", 0, 0)],
]


def stack_phase(nc, ctx, y, wh, wl, d_w, d_prm, d_qks, d_b2, d_const):

    def sb(name, shape, dt=F32):
        return ctx.enter_context(nc.sbuf_tensor(name, shape, dt))

    def sem(name):
        return nc.alloc_semaphore(name)

    raw = sb("raw", [P, 2, 512])
    rope_base = sb("rope_base", [P, 4, TILES, 32])
    mask = sb("mask", [P, SPANS])
    ident = sb("ident", [P, P])
    qks = sb("qks", [P, 2, 2, 32])
    qks_swapped = sb("qks_swapped", [P, 2, 2, 32])
    rope = sb("rope", [P, 2, 2, TILES, 64])
    prm = sb("prm", [P, DEPTH, NPRM])
    b2 = sb("b2", [P, DIM])
    ycur = sb("ycur", [P, TILES, DIM])
    xth = sb("xth", [P, KD, SEQ + 1], F32R)
    xtl = sb("xtl", [P, KD, SEQ + 1], F32R)
    qk_tok = sb("qk_tok", [P, 2, TILES, 512])
    rot_tmp = sb("rot_tmp", [P, 512])
    squares = sb("squares", [P, 512])
    ss = sb("ss", [P, 2, 16])
    ssc = sb("ssc", [P, 2, 16])
    rn = sb("rn", [P, 2, 16])
    minus_half = sb("minus_half", [P, 32])
    qsc = sb("qsc", [P, PAIRS, 4])
    qkT = sb("qkT", [P, 2, PAIRS, SEQ])
    v = sb("v", [P, TILES, INNER])
    probs = sb("probs", [P, 2, PCOLS])
    probsT = sb("probsT", [P, 2, PCOLS])
    mx = sb("mx", [P, 4, 4])
    nbias = sb("nbias", [P, 4, 4])
    rsum = sb("rsum", [P, 4, 4])
    rinv = sb("rinv", [P, 4, 4])
    o_tok = sb("o_tok", [P, TILES, P])
    oth = sb("oth", [P, 4, SEQ], F32R)
    otl = sb("otl", [P, 4, SEQ], F32R)
    xn = sb("xn", [P, 2, DIM])
    bst = sb("bst", [P, TILES, 2, 6])
    mv = sb("mv", [P, TILES, 2])
    rstd = sb("rstd", [P, TILES])
    vareps = sb("vareps", [P, TILES])
    xnh = sb("xnh", [P, KD, SEQ], F32R)
    xnl = sb("xnl", [P, KD, SEQ], F32R)
    hid = sb("hid", [P, FT, SEQ])
    hh = sb("hh", [P, 2, 2, SEQ], F32R)
    hl = sb("hl", [P, 2, 2, SEQ], F32R)

    ps_sim = [ctx.enter_context(nc.psum_tensor(f"ps_sim{h}", [P, 512], F32)) for h in range(2)]
    ps_pt = [ctx.enter_context(nc.psum_tensor(f"ps_pt{h}", [P, 512], F32)) for h in range(2)]
    ps_o = ctx.enter_context(nc.psum_tensor("ps_o", [P, 512], F32))
    ps_mm = [ctx.enter_context(nc.psum_tensor(f"ps_mm{b}", [P, 512], F32)) for b in range(3)]

    sim_done, pt_done, pv_done, ot_done = sem("sim_done"), sem("pt_done"), sem("pv_done"), sem("ot_done")
    qk_done, v_done, tr_done, wo_done = sem("qk_done"), sem("v_done"), sem("tr_done"), sem("wo_done")
    xt_done, xnt_done, gate_done, up_done, w2_done = (sem("xt_done"), sem("xnt_done"), sem("gate_done"),
                                                      sem("up_done"), sem("w2_done"))
    sim_masked, bias_ready, rinv_ready, o_ready = sem("sim_masked"), sem("bias_ready"), sem("rinv_ready"), sem("o_ready")
    otl_ready, rot_part, squares_summed, qk_rotated = sem("otl_ready"), sem("rot_part"), sem("squares_summed"), sem("qk_rotated")
    kn_ready, qsc_ready, xtl_ready, y_added = sem("kn_ready"), sem("qsc_ready"), sem("xtl_ready"), sem("y_added")
    stats_ready, mv_ready, xn_ready, xnf_ready, xnl_ready = (sem("stats_ready"), sem("mv_ready"), sem("xn_ready"),
                                                             sem("xnf_ready"), sem("xnl_ready"))
    gate_ready, h_ready, hl_ready, y_summed, y_ready = (sem("gate_ready"), sem("h_ready"), sem("hl_ready"),
                                                        sem("y_summed"), sem("y_ready"))
    zeroed, xn_free, minus_ready = sem("zeroed"), sem("xn_free"), sem("minus_ready")
    exp_done, pt_moved, oth_ready, sq_ready = sem("exp_done"), sem("pt_moved"), sem("oth_ready"), sem("sq_ready")
    v_moved, tr_moved, xth_ready, xnh_ready = sem("v_moved"), sem("tr_moved"), sem("xth_ready"), sem("xnh_ready")
    gelu_done, hh_ready = sem("gelu_done"), sem("hh_ready")
    w_hi, w_ready, rope_part, rope_ready = sem("w_hi"), sem("w_ready"), sem("rope_part"), sem("rope_ready")
    rn_part, rn_ready, rs_part, rstd_ready = sem("rn_part"), sem("rn_ready"), sem("rs_part"), sem("rstd_ready")
    raw_in = [sem("raw_in0"), sem("raw_in1")]
    const_in, qks_in, b2_in, ycur_in, shift_in = (sem("const_in"), sem("qks_in"), sem("b2_in"),
                                                          sem("ycur_in"), sem("shift_in"))

    block = ctx.enter_context(nc.Block())

    def on(m):
        return not isinstance(m, int) or 0 <= m < STEPS

    def later(m, first=0):
        return not isinstance(m, int) or m > first

    def settle(eng):
        eng.nop(nofuse=True)

    def sample(m):
        return m % BATCH

    def layer(m):
        return m // BATCH

    FULL = (4, STEPS)
    EDGES = (range(0, FULL[0]), range(FULL[1], STEPS + 3))

    QA, KA, QB, KB = 0, 2, 4, 6
    ORDER = [u for slot in PE_SLOTS for u in slot if u[0] in BANK_USES]
    assert len(ORDER) % 3 == 0
    FREED = {"wo": (y_added, 4), "w2": (y_summed, 1), "up": (h_ready, 3), "qk": (rot_part, 8), "v": (v_moved, 4),
             "tr": (tr_moved, 8), "xt": (xtl_ready, 1), "xnt": (xnf_ready, 1), "gate": (gate_ready, 3)}

    def bank(use, idx):
        return ps_mm[[u[:2] for u in ORDER].index((use, idx)) % 3]

    def pair_on(g):
        return not isinstance(g, int) or 0 <= g < STEPS * PAIRS

    @block.tensor
    def _(pe):
        def split3(out, lhs_h, lhs_l, rhs_h, rhs_l, start, stop, **kw):
            pe.matmul(out, lhs_h, rhs_h, start=start, stop=False, **kw)
            pe.matmul(out, lhs_h, rhs_l, start=False, stop=False, **kw)
            return pe.matmul(out, lhs_l, rhs_h, start=False, stop=stop, **kw)

        def wait_bank(n, use, idx):
            at = [u[:2] for u in ORDER].index((use, idx)) - 3
            while at > -4 * len(ORDER):
                before, i, lag = ORDER[at % len(ORDER)]
                m = n - lag + at // len(ORDER)
                if on(m):
                    signal, per = FREED[before]
                    pe.wait_ge(signal, per * m + i + 1)
                    return
                at -= 3

        def weights(m, u):
            pe.wait_ge(w_ready, NU * layer(m) + u + 1)

        def wcols(w, u, k, width):
            return w[:, OFFS[u] + k * width:OFFS[u] + (k + 1) * width]

        def project(m, bank_, c, t, signal):
            for k in range(KD):
                u = U_QKV + 2 * c + k
                mm = split3(bank_[:], xth[:, k, t * P:(t + 1) * P], xtl[:, k, t * P:(t + 1) * P],
                            wcols(wh, u, 0, 512), wcols(wl, u, 0, 512), k == 0, k == KD - 1)
            mm.then_inc(signal, 1)

        def dense(n, use, idx, lag):
            m = n - lag
            if not on(m):
                return
            if use == "w2_last":
                w2_part(m, 2)
                return
            bank_ = bank(use, idx)
            wait_bank(n, use, idx)
            if use == "w2":
                for i in range(2):
                    w2_part(m, i)
            elif use == "wo":
                pe.wait_ge(otl_ready, PAIRS * m + 2 * idx + 2)
                weights(m, U_WO + idx)
                for t in range(TILES):
                    for q in range(2):
                        r = (2 * idx + q) % 4
                        mm = split3(bank_[:, t * DIM:(t + 1) * DIM], oth[:, r, t * P:(t + 1) * P],
                                    otl[:, r, t * P:(t + 1) * P], wcols(wh, U_WO + idx, q, DIM),
                                    wcols(wl, U_WO + idx, q, DIM), q == 0, q == 1)
                mm.then_inc(wo_done, 1)
            elif use == "xt":
                pe.wait_ge(ycur_in, 16 * (m + 1))
                for k in range(KD):
                    for t in range(TILES):
                        mm = pe.transpose(bank_[:, k * SEQ + t * P:k * SEQ + (t + 1) * P],
                                          ycur[:, t, k * P:(k + 1) * P], ident[:])
                mm.then_inc(xt_done, 1)
            elif use == "qk":
                c, t = idx // 2, idx % 2
                if idx == QA:
                    pe.wait_ge(xtl_ready, m + 1)
                if t == 0:
                    weights(m, U_QKV + 2 * c + 1)
                project(m, bank_, c, t, qk_done)
            elif use == "v":
                c, t = 4 + idx // 2, idx % 2
                if t == 0:
                    weights(m, U_QKV + 2 * c + 1)
                project(m, bank_, c, t, v_done)
            elif use == "tr":
                which, t = (idx % 4) // 2, idx % 2
                if which == 0:
                    pe.wait_ge(qk_rotated, 8 * m + (QA if idx < 4 else QB) + t + 1)
                else:
                    pe.wait_ge(kn_ready, 4 * m + 2 * (idx // 4) + t + 1)
                for j in range(4):
                    mm = pe.transpose(bank_[:, j * P:(j + 1) * P], qk_tok[:, which, t, j * P:(j + 1) * P], ident[:])
                mm.then_inc(tr_done, 1)
            elif use == "xnt":
                pe.wait_ge(xn_ready, m + 1)
                for k in range(KD):
                    for t in range(TILES):
                        mm = pe.transpose(bank_[:, k * SEQ + t * P:k * SEQ + (t + 1) * P],
                                          xn[:, t, k * P:(k + 1) * P], ident[:])
                mm.then_inc(xnt_done, 1)
            elif use in ("gate", "up"):
                u = (U_GATE if use == "gate" else U_UP) + idx
                weights(m, u)
                if (use, idx) == ("gate", 0):
                    pe.wait_ge(xnl_ready, m + 1)
                for i in range(2):
                    for k in range(KD):
                        at = OFFS[u] + k * 2 * FP + i * FP
                        mm = split3(bank_[0:FP, i * SEQ:(i + 1) * SEQ], wh[:, at:at + FP], wl[:, at:at + FP],
                                    xnh[:, k, :], xnl[:, k, :], k == 0, k == KD - 1)
                mm.then_inc(gate_done if use == "gate" else up_done, 1)

        def w2_part(m, i):
            bank_ = bank("w2", 0)
            pe.wait_ge(hl_ready, 3 * m + i + 1)
            weights(m, U_W2 + i)
            for j in range(2):
                for t in range(TILES):
                    u = U_W2 + i
                    first = i == 0 and j == 0 and t == 0
                    last = i == 2 and j == 1
                    a = hh[0:FP, i % 2, j, t * P:(t + 1) * P], hl[0:FP, i % 2, j, t * P:(t + 1) * P]
                    b = wh[0:FP, OFFS[u] + j * DIM:OFFS[u] + (j + 1) * DIM], wl[0:FP, OFFS[u] + j * DIM:OFFS[u] + (j + 1) * DIM]
                    mm = split3(bank_[:, t * DIM:(t + 1) * DIM], a[0], a[1], b[0], b[1], first, last, skip_group_check=True)
            mm.then_inc(w2_done, 1)

        def weigh_values(g, p, m):
            pe.wait_ge(pt_moved, 2 * g + 2)
            if later(g):
                pe.wait_ge(otl_ready, g)
            pe.wait_ge(v_moved, 4 * m + (2 if p < 4 else 4))
            for h in range(2):
                cols = slice((2 * p + h) * DH, (2 * p + h + 1) * DH)
                o = [ps_o[:, t * P + h * DH:t * P + (h + 1) * DH] for t in range(TILES)]
                pe.matmul(o[0], probsT[:, h, 0:P], v[:, 0, cols], start=True, stop=True)
                pe.matmul(o[1], probsT[:, h, P:2 * P], v[:, 0, cols], start=True, stop=False)
                mm = pe.matmul(o[1], probsT[:, h, 2 * P:3 * P], v[:, 1, cols], start=False, stop=True)
            mm.then_inc(pv_done, 1)

        def turn_probs(g):
            pe.wait_ge(exp_done, g + 1)
            for h in range(2):
                if later(g):
                    pe.wait_ge(pt_moved, 2 * (g - 1) + h + 1)
                for b in range(3):
                    mm = pe.transpose(ps_pt[h][:, b * P:(b + 1) * P], probs[:, h, b * P:(b + 1) * P], ident[:])
                mm.then_inc(pt_done, 1)

        def scores(g, p, m):
            pe.wait_ge(tr_moved, 8 * m + (4 if p < 4 else 8))
            for h in range(2):
                if later(g):
                    pe.wait_ge(sim_masked, 2 * (g - 1) + h + 1)
                rows = slice(h * DH, (h + 1) * DH)
                pe.matmul(ps_sim[h][:, 0:P], qkT[rows, 0, p, 0:P], qkT[rows, 1, p, 0:P], start=True, stop=True)
                mm = pe.matmul(ps_sim[h][:, P:SPANS], qkT[rows, 0, p, P:2 * P], qkT[rows, 1, p, WINDOW:SEQ],
                               start=True, stop=True)
                mm.then_inc(sim_done, 1)

        def turn_outputs(g):
            pe.wait_ge(o_ready, g + 1)
            for t in range(TILES):
                mm = pe.transpose(ps_o[:, t * P:(t + 1) * P], o_tok[:, t, :], ident[:])
            mm.then_inc(ot_done, 1)

        def step(n):
            for j, slot in enumerate(PE_SLOTS):
                for what, idx, lag in slot:
                    if what in BANK_USES or what == "w2_last":
                        dense(n, what, idx, lag)
                        continue
                    g, p, m = PAIRS * (n - 1) + j - lag, (j - lag) % PAIRS, n - 1 - (lag > j)
                    if not pair_on(g):
                        continue
                    if what == "scores":
                        scores(g, p, m)
                    elif what == "turn probs":
                        turn_probs(g)
                    elif what == "weigh values":
                        weigh_values(g, p, m)
                    elif what == "turn outputs":
                        turn_outputs(g)

        pe.wait_ge(const_in, 16 * CONSTS)
        for n in EDGES[0]:
            step(n)
        with pe.Fori(*FULL) as n:
            step(n)
        for n in EDGES[1]:
            step(n)

    @block.vector
    def _(dve):
        ve = nc.vector

        def outputs(g, r):
            dve.wait_ge(pv_done, g + 1)
            dve.wait_ge(rinv_ready, g + 1)
            if later(g):
                dve.wait_ge(ot_done, g)
            ve.tensor_tensor(o_tok[:].rearrange("p t (h d) -> p (t h) d", h=2),
                             ps_o[:, 0:2 * P].rearrange("p (a d) -> p a d", a=4),
                             rinv[:, r, :].unsqueeze(2).broadcast_to([P, 4, DH]), ALU.mult).then_inc(o_ready, 1)

        def invert_sums(g, r):
            dve.wait_ge(exp_done, g + 1)
            ve.reciprocal(rinv[:, r, :], rsum[:, r, :]).then_inc(rinv_ready, 1)

        def mask_and_max(g, p, r):
            for h in range(2):
                dve.wait_ge(sim_done, 2 * g + h + 1)
                if later(g):
                    dve.wait_ge(pt_done, 2 * (g - 1) + h + 1)
                settle(dve)
                ve.tensor_tensor_reduce(out=probs[:, h, 0:P], in0=ps_sim[h][:, 0:P], in1=mask[:, 0:P], scale=1.0,
                                        scalar=-1.0e30, op0=ALU.add, op1=ALU.max, accum_out=mx[:, r, h:h + 1])
                ve.tensor_tensor_reduce(out=probs[:, h, P + WINDOW:PCOLS], in0=ps_sim[h][:, P:SPANS],
                                        in1=mask[:, P:SPANS], scale=1.0, scalar=-1.0e30, op0=ALU.add, op1=ALU.max,
                                        accum_out=mx[:, r, 2 + h:3 + h]).then_inc(sim_masked, 1)
            dve.wait_ge(sim_masked, 2 * g + 2)
            ve.scalar_tensor_tensor(out=nbias[:, r, :], in0=mx[:, r, :], scalar=-1.0, in1=qsc[:, p, :],
                                    op0=ALU.mult, op1=ALU.mult).then_inc(bias_ready, 1)

        def low_outputs(g, r):
            dve.wait_ge(oth_ready, g + 1)
            ve.tensor_tensor(otl[:, r, :], ps_o[:, 0:SEQ], oth[:, r, :].bitcast(F32), ALU.subtract).then_inc(otl_ready, 1)

        def y_of(m):
            return y[:, bass.ds(sample(m) * TILES * DIM, TILES * DIM)]

        def evacuate(n, use, idx, lag):
            m = n - lag
            if not on(m):
                return
            bank_ = bank(use, idx)
            if use == "wo":
                dve.wait_ge(wo_done, 4 * m + idx + 1)
                dve.wait_ge(y_ready, m + 1)
                if idx:
                    dve.wait_ge(y_added, 4 * m + idx)
                ve.tensor_tensor(y_of(m), bank_[:], y_of(m), ALU.add).then_inc(y_added, 1)
            elif use == "xt":
                dve.wait_ge(xth_ready, m + 1)
                ve.tensor_tensor(xtl[:, 0, 0:SEQ], bank_[:, 0:SEQ], xth[:, 0, 0:SEQ].bitcast(F32), ALU.subtract)
                ve.tensor_tensor(xtl[:, 1, 1:SEQ + 1], bank_[:, SEQ:2 * SEQ], xth[:, 1, 1:SEQ + 1].bitcast(F32),
                                 ALU.subtract).then_inc(xtl_ready, 1)
            elif use == "qk":
                which, t = (idx % 4) // 2, idx % 2
                i = 8 * m + idx
                ps4 = bank_[:].rearrange("p (e s d) -> p e s d", s=2, d=32)
                tmp4 = rot_tmp[:].rearrange("p (e s d) -> p e s d", s=2, d=32)
                if idx == QA:
                    dve.wait_ge(rope_ready, layer(m) + 1)
                dve.wait_ge(sq_ready, i + 1)
                if idx < 4 and later(m):
                    dve.wait_ge(tr_done, 8 * m - (2 if which == 0 else 0))
                if idx >= 4:
                    dve.wait_ge(tr_done, 8 * m + (2 if which == 0 else 4))
                ve.tensor_tensor(qk_tok[:, which, t, :].rearrange("p (e d) -> p e d", d=DH),
                                 bank_[:].rearrange("p (e d) -> p e d", d=DH),
                                 rope[:, which, 0, t, :].unsqueeze(1).broadcast_to([P, 8, DH]), ALU.mult)
                if later(i):
                    dve.wait_ge(qk_rotated, i)
                for s in range(2):
                    mm = ve.tensor_tensor(tmp4[:, :, s, :], ps4[:, :, 1 - s, :],
                                          rope[:, which, 1, t, 32 * s:32 * s + 32].unsqueeze(1).broadcast_to([P, 8, 32]),
                                          ALU.mult)
                mm.then_inc(rot_part, 1)
                dve.wait_ge(rot_part, i + 1)
                ve.tensor_tensor(qk_tok[:, which, t, :], qk_tok[:, which, t, :], rot_tmp[:], ALU.add).then_inc(qk_rotated, 1)
                if t == 0 and which == 0 and (idx >= 4 or later(m)):
                    dve.wait_ge(rn_ready, 2 * m + (1 if idx >= 4 else 0))
                ve.tensor_reduce(ss[:, which, :].rearrange("p (a b c) -> p a b c", a=4, b=2)[:, :, t, :],
                                 squares[:].rearrange("p (a c d) -> p a c d", a=4, c=2), AX.X, ALU.add).then_inc(squares_summed, 1)
            elif use == "xnt":
                lp = layer(m) * NPRM
                dve.wait_ge(xnt_done, m + 1)
                pf = prm[:].rearrange("p l c -> p (l c)")
                for k in range(KD):
                    mm = ve.tensor_scalar(xn[:, k, :], bank_[:, k * SEQ:(k + 1) * SEQ], pf[:, bass.ds(lp + k, 1)],
                                          pf[:, bass.ds(lp + KD + k, 1)], ALU.mult, ALU.add)
                mm.then_inc(xnf_ready, 1)
            elif use in ("gate", "up"):
                pf = prm[:].rearrange("p l c -> p (l c)")
                b = layer(m) * NPRM + 2 * KD + (FT if use == "up" else 0)
                dve.wait_ge(gate_done if use == "gate" else up_done, 3 * m + idx + 1)
                if (use, idx) == ("gate", 0) and later(m):
                    dve.wait_ge(hl_ready, 3 * m)
                if (use, idx) == ("up", 0):
                    dve.wait_ge(gelu_done, m + 1)
                for i in range(2):
                    f = 2 * idx + i
                    src = bank_[0:FP, i * SEQ:(i + 1) * SEQ]
                    bias = pf[0:FP, bass.ds(b + f, 1)]
                    if use == "gate":
                        mm = ve.tensor_scalar(hid[0:FP, f, :], src, bias, None, ALU.add)
                    else:
                        mm = ve.scalar_tensor_tensor(out=hid[0:FP, f, :], in0=src, scalar=bias, in1=hid[0:FP, f, :],
                                                     op0=ALU.add, op1=ALU.mult)
                mm.then_inc(gate_ready if use == "gate" else h_ready, 1)

        def low_hidden(m, i):
            dve.wait_ge(hh_ready, 3 * m + i + 1)
            ve.tensor_tensor(hl[0:FP, i % 2], hid[0:FP, 2 * i:2 * i + 2, :], hh[0:FP, i % 2].bitcast(F32),
                             ALU.subtract).then_inc(hl_ready, 1)

        def low_rows(m):
            dve.wait_ge(xnh_ready, m + 1)
            ve.tensor_tensor(xnl[:], xn[:], xnh[:].bitcast(F32), ALU.subtract).then_inc(xnl_ready, 1)
            dve.wait_ge(xnl_ready, m + 1)
            ve.memset(xn[0:1, 0, P:2 * P], 0.0).then_inc(xn_free, 1)

        def norm_keys(m, c):
            dve.wait_ge(rn_ready, 2 * m + c + 1)
            dve.wait_ge(qk_rotated, 8 * m + 4 * c + 4)
            for t in range(TILES):
                kt = qk_tok[:, 1, t, :].rearrange("p (a c d) -> p a c d", a=4, c=2)
                ve.tensor_tensor(kt, kt, rn[:, 1, :].rearrange("p (a b c) -> p a b c", a=4, b=2)[:, :, t, :]
                                 .unsqueeze(3).broadcast_to([P, 4, 2, DH]), ALU.mult).then_inc(kn_ready, 1)
            if later(m):
                dve.wait_ge(exp_done, PAIRS * (m - 1) + 4 * (c + 1))
            ve.tensor_scalar(qsc[:, 4 * c:4 * c + 4, :], rn[:, 0, :].rearrange("p (a b) -> p a b", a=4), QKS, None,
                             ALU.mult).then_inc(qsc_ready, 1)

        def row_stats(m):
            dve.wait_ge(y_added, 4 * m + 4)
            dve.wait_ge(shift_in, 48 * (m + 1))
            settle(dve)
            for t in range(TILES):
                ve.bn_stats(bst[:, t, 0, :], y[:, bass.ds(sample(m) * TILES * DIM + t * DIM, P)])
                mm = ve.bn_stats(bst[:, t, 1, :], xn[:, t, P:2 * P])
            mm.then_inc(stats_ready, 1)
            dve.wait_ge(stats_ready, m + 1)
            settle(dve)
            for t in range(TILES):
                mm = ve.bn_aggr(mv[:, t, :], bst[:, t].rearrange("p a b -> p (a b)"))
            mm.then_inc(mv_ready, 1)

        def norm_rows(m):
            dve.wait_ge(rstd_ready, m + 1)
            for t in range(TILES):
                ve.tensor_scalar(xn[:, t, 0:P], y[:, bass.ds(sample(m) * TILES * DIM + t * DIM, P)], mv[:, t, 0:1],
                                 rstd[:, t:t + 1], ALU.subtract, ALU.mult)
                mm = ve.tensor_scalar(xn[:, t, P:2 * P], xn[:, t, P:2 * P], mv[:, t, 0:1],
                                      rstd[:, t:t + 1], ALU.subtract, ALU.mult)
            mm.then_inc(xn_ready, 1)

        def add_ffn(m):
            dve.wait_ge(w2_done, 3 * m + 3)
            ve.tensor_tensor(y_of(m), bank("w2", 0)[:], y_of(m), ALU.add).then_inc(y_summed, 1)
            dve.wait_ge(y_summed, m + 1)
            dve.wait_ge(b2_in, 16 * (layer(m) + 1))
            y3 = y_of(m).rearrange("p (t d) -> p t d", t=TILES)
            ve.tensor_tensor(y3, y3, b2[:].unsqueeze(1).broadcast_to([P, TILES, DIM]), ALU.add).then_inc(y_ready, 1)

        def step(n):
            for j, slot in enumerate(DVE_SLOTS):
                for what, idx, lag in slot:
                    m = n - lag
                    if what in BANK_USES:
                        evacuate(n, what, idx, lag)
                    elif what in PAIR_WORK:
                        g, p, r = PAIRS * (n - 1) + j - lag, (j - lag) % PAIRS, (j - lag) % 4
                        if not pair_on(g):
                            continue
                        if what == "mask":
                            mask_and_max(g, p, r)
                        elif what == "invert":
                            invert_sums(g, r)
                        elif what == "outputs":
                            outputs(g, r)
                        elif what == "low outputs":
                            low_outputs(g, r)
                    elif not on(m):
                        continue
                    elif what == "row stats":
                        row_stats(m)
                    elif what == "norm rows":
                        norm_rows(m)
                    elif what == "low rows":
                        low_rows(m)
                    elif what == "norm keys":
                        norm_keys(m, idx)
                    elif what == "low hidden":
                        low_hidden(m, idx)
                    elif what == "add ffn":
                        add_ffn(m)

        for h in range(2):
            ve.memset(probs[:, h, P:P + WINDOW], 0.0).then_inc(zeroed, 1)
        ve.memset(xth[:, 1, 0:1].bitcast(F32), 0.0).then_inc(zeroed, 1)
        ve.memset(xtl[:, 1, 0:1].bitcast(F32), 0.0).then_inc(zeroed, 1)
        ve.memset(xn[0:1, 0, P:2 * P], 0.0).then_inc(xn_free, 1)
        ve.memset(mx[:], 0.0).then_inc(y_ready, BATCH)
        dve.wait_ge(const_in, 16 * CONSTS)
        for n in EDGES[0]:
            step(n)
        with dve.Fori(*FULL) as n:
            step(n)
        for n in EDGES[1]:
            step(n)

    @block.scalar
    def _(act):
        sc = nc.scalar

        def move_turned(g):
            for h in range(2):
                act.wait_ge(pt_done, 2 * g + h + 1)
                if later(g):
                    act.wait_ge(pv_done, g)
                sc.copy(probsT[:, h, :], ps_pt[h][:, 0:PCOLS]).then_inc(pt_moved, 1)

        def exponentials(g, p, r):
            act.wait_ge(bias_ready, g + 1)
            for t in range(TILES):
                for h in range(2):
                    part = probs[:, h, 0:P] if t == 0 else probs[:, h, P + WINDOW:PCOLS]
                    c = 2 * t + h
                    mm = sc.activation(part, part, ACT.Exp, bias=nbias[:, r, c:c + 1], scale=qsc[:, p, c:c + 1],
                                       accum_out=rsum[:, r, c:c + 1])
            mm.then_inc(exp_done, 1)

        def high_outputs(g, r, m, p):
            act.wait_ge(ot_done, g + 1)
            if later(g, 3):
                act.wait_ge(wo_done, 4 * m + p // 2 - 1)
            sc.copy(oth[:, r, :], ps_o[:, 0:SEQ]).then_inc(oth_ready, 1)

        def evacuate(n, use, idx, lag):
            m = n - lag
            if not on(m):
                return
            bank_ = bank(use, idx)
            if use == "qk":
                i = 8 * m + idx
                act.wait_ge(qk_done, i + 1)
                if later(i):
                    act.wait_ge(squares_summed, i)
                sc.activation(squares[:], bank_[:], ACT.Square).then_inc(sq_ready, 1)
            elif use == "v":
                c, t = idx // 2, idx % 2
                act.wait_ge(v_done, 4 * m + idx + 1)
                if later(m):
                    act.wait_ge(pv_done, PAIRS * (m - 1) + 4 * (c + 1))
                sc.copy(v[:, t, c * 512:(c + 1) * 512], bank_[:]).then_inc(v_moved, 1)
            elif use == "tr":
                c, which, t = idx // 4, (idx % 4) // 2, idx % 2
                act.wait_ge(tr_done, 8 * m + idx + 1)
                if later(m):
                    act.wait_ge(sim_done, 2 * (PAIRS * (m - 1) + 4 * (c + 1)))
                sc.copy(qkT[:, which, 4 * c:4 * c + 4, t * P:(t + 1) * P],
                        bank_[:].rearrange("p (a q) -> p a q", a=4)).then_inc(tr_moved, 1)
            elif use == "xt":
                act.wait_ge(xt_done, m + 1)
                if later(m):
                    act.wait_ge(v_done, 4 * m)
                sc.copy(xth[:, 0, 0:SEQ], bank_[:, 0:SEQ])
                sc.copy(xth[:, 1, 1:SEQ + 1], bank_[:, SEQ:2 * SEQ]).then_inc(xth_ready, 1)
            elif use == "xnt":
                act.wait_ge(xnf_ready, m + 1)
                if later(m):
                    act.wait_ge(up_done, 3 * m)
                sc.copy(xnh[:], xn[:]).then_inc(xnh_ready, 1)
            elif use == "up":
                i = idx
                act.wait_ge(h_ready, 3 * m + i + 1)
                if i == 2:
                    act.wait_ge(w2_done, 3 * m + 1)
                elif later(m):
                    act.wait_ge(w2_done, 3 * m)
                sc.copy(hh[0:FP, i % 2], hid[0:FP, 2 * i:2 * i + 2, :]).then_inc(hh_ready, 1)

        def gelu(m):
            act.wait_ge(gate_ready, 3 * m + 3)
            sc.activation(hid[0:FP], hid[0:FP], ACT.Gelu).then_inc(gelu_done, 1)

        def step(n):
            for j, slot in enumerate(ACT_SLOTS):
                for what, idx, lag in slot:
                    if what in PAIR_WORK:
                        g, p, r = PAIRS * (n - 1) + j - lag, (j - lag) % PAIRS, (j - lag) % 4
                        if not pair_on(g):
                            continue
                        if what == "exponentials":
                            exponentials(g, p, r)
                        elif what == "move turned":
                            move_turned(g)
                        elif what == "high outputs":
                            high_outputs(g, r, n - 1 - (lag > j), p)
                    elif what == "gelu":
                        if on(n - lag):
                            gelu(n - lag)
                    elif what in BANK_USES:
                        evacuate(n, what, idx, lag)

        act.wait_ge(zeroed, 4)
        for n in EDGES[0]:
            step(n)
        with act.Fori(*FULL) as n:
            step(n)
        for n in EDGES[1]:
            step(n)

    @block.gpsimd
    def _(pool):
        gp = nc.gpsimd

        def load_unit(l, u):
            i = NU * l + u
            pool.wait_ge(w_ready, i - (1 if u else 0))
            src = d_w[:, bass.ds(WCOLS * l + OFFS[u], UNITS[u])]
            pool.dma_start(raw[:, u % 2, 0:UNITS[u]], src).then_inc(raw_in[u % 2], 16)

        def split_unit(l, u):
            i = NU * l + u
            part = slice(OFFS[u], OFFS[u] + UNITS[u])
            src = raw[:, u % 2, 0:UNITS[u]]
            pool.wait_ge(raw_in[u % 2], 16 * (len(range(u % 2, NU, 2)) * l + u // 2 + 1 -
                                           len(range(u % 2, U_LATE, 2))))
            settle(pool)
            gp.tensor_copy(wh[:, part], src).then_inc(w_hi, 1)
            pool.wait_ge(w_hi, i + 1 - U_LATE)
            gp.tensor_tensor(wl[:, part], src, wh[:, part].bitcast(F32), ALU.subtract).then_inc(w_ready, 1)

        def freed(m, u):
            if u < U_QKV + 8:
                return qk_done, 8 * m + 2 * (u // 2) + 2
            if u < U_WO:
                return v_done, 4 * m + 2 * ((u - 8) // 2) + 2
            if u < U_GATE:
                return wo_done, 4 * m + u - U_WO + 1
            if u < U_UP:
                return gate_done, 3 * m + u - U_GATE + 1
            if u < U_W2:
                return up_done, 3 * m + u - U_UP + 1
            return w2_done, 3 * m + u - U_W2 + 1

        def reload(l, units):
            for u in units:
                if u + 1 < NU:
                    load_unit(l, u + 1)
                pool.wait_ge(*freed(BATCH * l - 1, u))
                split_unit(l, u)

        def rope_tables(l):
            pool.wait_ge(qks_in, 16 * (l + 1))
            if later(l):
                pool.wait_ge(qk_rotated, 8 * BATCH * l)
            settle(pool)
            gp.tensor_scalar(qks_swapped[:, :, 0, :], qks[:, :, 1, :], -1.0, 1.0, ALU.mult, ALU.mult)
            gp.tensor_copy(qks_swapped[:, :, 1, :], qks[:, :, 0, :]).then_inc(rope_part, 1)
            pool.wait_ge(rope_part, l + 1)
            for w in range(2):
                for f, scales in enumerate((qks, qks_swapped)):
                    for t in range(TILES):
                        mm = gp.tensor_tensor(rope[:, w, f, t, :].rearrange("p (s d) -> p s d", s=2), scales[:, w],
                                              rope_base[:, 2 * w + f, t, :].unsqueeze(1).broadcast_to([P, 2, 32]),
                                              ALU.mult)
            mm.then_inc(rope_ready, 1)

        def inverse_norms(m, c):
            i = 2 * m + c
            pool.wait_ge(squares_summed, 8 * m + 4 * c + 4)
            settle(pool)
            gp.tensor_scalar(ssc[:], ss[:], 1e-24, 3.0e38, ALU.max, ALU.min).then_inc(rn_part, 1)
            pool.wait_ge(rn_part, i + 1)
            if later(i):
                pool.wait_ge(qsc_ready, i)
            gp.tensor_tensor(rn[:].rearrange("p a b -> p (a b)"), ssc[:].rearrange("p a b -> p (a b)"), minus_half[:],
                             ALU.pow).then_inc(rn_ready, 1)

        def inverse_deviation(m):
            pool.wait_ge(mv_ready, m + 1)
            settle(pool)
            gp.tensor_scalar(vareps[:], mv[:, :, 1], 1.0, EPS, ALU.mult, ALU.add).then_inc(rs_part, 1)
            pool.wait_ge(rs_part, m + 1)
            gp.tensor_tensor(rstd[:], vareps[:], minus_half[:, 0:TILES], ALU.pow).then_inc(rstd_ready, 1)

        def step(n, l=None, part=None):
            if part == 1:
                reload(l, range(4, 6))
            if part == 3:
                reload(l, range(U_UP, U_W2))
            if on(n - 1):
                inverse_norms(n - 1, 1)
            if part == 1:
                rope_tables(l)
                reload(l, range(6, 8))
            if part == 2:
                reload(l, range(U_WO + 2, U_WO + 4))
            if part == 3:
                reload(l, range(U_W2, NU))
            if on(n - 2):
                inverse_deviation(n - 2)
            if part == 1:
                reload(l, range(8, U_WO))
            if on(n):
                inverse_norms(n, 0)
            if part == 0:
                load_unit(l, 0)
                reload(l, range(0, 4))
            if part == 1:
                reload(l, range(U_WO, U_WO + 2))
            if part == 2:
                reload(l, range(U_GATE, U_UP))

        gp.memset(minus_half[:], -0.5).then_inc(minus_ready, 1)
        pool.wait_ge(minus_ready, 1)
        gp.memset(ssc[:], 0.0).then_inc(w_ready, U_LATE)
        pool.wait_ge(w_ready, U_LATE)
        pool.wait_ge(const_in, 16 * CONSTS)
        rope_tables(0)
        for n in EDGES[0]:
            step(n)
            if n == 0:
                for u in range(U_LATE, NU):
                    load_unit(0, u)
                    split_unit(0, u)
        with pool.Fori(0, DEPTH - 1) as o:
            for s in range(BATCH):
                part = s - (BATCH - 1 - FULL[0])
                step(BATCH * o + FULL[0] + s, o + 1, part if part >= 0 else None)
        with pool.Fori(BATCH * (DEPTH - 1) + FULL[0], FULL[1]) as n:
            step(n)
        for n in EDGES[1]:
            step(n)

    @block.sync
    def _(sp):
        y5 = y[:].rearrange("p (s t d) -> p s t d", s=BATCH, t=TILES)

        def step(n):
            if on(n):
                sp.wait_ge(y_ready, n + 1)
                settle(sp)
                if later(n):
                    sp.wait_ge(xt_done, n)
                settle(sp)
                sp.dma_start(ycur[:].rearrange("p t d -> p (t d)"),
                             y[:, bass.ds(sample(n) * TILES * DIM, TILES * DIM)]).then_inc(ycur_in, 16)
            m = n - 2
            if on(m):
                sp.wait_ge(y_added, 4 * m + 4)
                settle(sp)
                sp.wait_ge(xn_free, m + 1)
                settle(sp)
                at = sample(m) * TILES * DIM
                for t in range(TILES):
                    sp.dma_start(xn[1:P, t, P:2 * P], y[0:P - 1, bass.ds(at + t * DIM + P, P)]).then_inc(shift_in, 16)
                sp.dma_start(xn[0:1, 1, P:2 * P], y[P - 1:P, bass.ds(at + P, P)]).then_inc(shift_in, 16)

        def load_scales(l):
            if later(l):
                sp.wait_ge(rope_ready, l)
                settle(sp)
            sp.dma_start(qks[:].rearrange("p a s d -> p (a s d)"), d_qks[:, bass.ds(2 * DH * l, 2 * DH)]).then_inc(qks_in, 16)

        def load_b2(l):
            if later(l):
                sp.wait_ge(y_ready, BATCH * l + BATCH)
                settle(sp)
            sp.dma_start(b2[:], d_b2[:, bass.ds(DIM * l, DIM)]).then_inc(b2_in, 16)

        sp.dma_start(rope_base[:], d_const[:, 0:4 * TILES * 32].rearrange("p (a t d) -> p a t d", a=4, t=TILES)).then_inc(const_in, 16)
        sp.dma_start(mask[:], d_const[:, 4 * TILES * 32:4 * TILES * 32 + SPANS]).then_inc(const_in, 16)
        sp.dma_start(ident[:], d_const[:, 4 * TILES * 32 + SPANS:4 * TILES * 32 + SPANS + P]).then_inc(const_in, 16)
        sp.dma_start(prm[:].rearrange("p l c -> p (l c)"), d_prm).then_inc(const_in, 16)
        load_scales(0)
        load_b2(0)
        for n in EDGES[0]:
            step(n)
        with sp.Fori(0, DEPTH - 1) as o:
            for s in range(BATCH):
                step(BATCH * o + FULL[0] + s)
                if s == 0:
                    load_scales(o + 1)
                if s == BATCH + 2 - FULL[0]:
                    load_b2(o + 1)
        with sp.Fori(BATCH * (DEPTH - 1) + FULL[0], FULL[1]) as n:
            step(n)
        for n in EDGES[1]:
            step(n)


XHEADS = 16
XDH = DIM // XHEADS
XPAIRS = XHEADS // 2
XW = 3 * DIM
XQ = XHEADS // 4
HID = 768
HT = HID // P
DW_UNITS = 3 * KD * HID // 512

VPART = 2 * XDH
VGROUP = 5 * VPART
VHALF = XQ * VGROUP
VROW = 2 * VHALF + VPART
VWINDOW = (0, VHALF, VHALF + 2 * VPART, VPART)
SPARE = (XQ + KD) * SEQ + VROW

X_BANK_USES = ("st", "v", "zt", "ct", "qk", "wo")
X_PAIR_WORK = ("low turned", "invert", "maxima")
X_POOL_LAG = 1
X_POOL_OUT = (6, 2)
X_PE_SLOTS = [
    [("weigh values", 0, 3), ("scores", 0, 0), ("turn probs", 0, 2), ("st", 6, 1)],
    [("st", 7, 1), ("turn probs", 0, 2), ("weigh values", 0, 3), ("scores", 0, 0)],
    [("ct", 0, 0), ("turn probs", 0, 2), ("weigh values", 0, 3), ("scores", 0, 0)],
    [("zt", 0, 0), ("turn probs", 0, 2), ("weigh values", 0, 3), ("scores", 0, 0), ("qk", 0, 0)],
    [("turn probs", 0, 2), ("weigh values", 0, 3), ("scores", 0, 0), ("qk", 1, 0), ("v", 0, 0)],
    [("turn probs", 0, 2), ("weigh values", 0, 3), ("scores", 0, 0), ("wo", 0, 2), ("st", 0, 0)],
    [("turn probs", 0, 2), ("weigh values", 0, 3), ("scores", 0, 0), ("st", 1, 0)],
    [("st", 2, 0), ("st", 3, 0), ("turn probs", 0, 2), ("weigh values", 0, 3), ("scores", 0, 0), ("st", 4, 0),
     ("st", 5, 0)],
]
X_DVE_SLOTS = [
    [("rows in", 0, 0), ("invert", 0, 1), ("maxima", 0, 0), ("low turned", 0, 2), ("norm in", 0, 0)],
    [("invert", 0, 1), ("maxima", 0, 0), ("low turned", 0, 2), ("low outputs", 0, 2)],
    [("invert", 0, 1), ("maxima", 0, 0), ("low turned", 0, 2), ("low values", 0, 1)],
    [("ct", 0, 0), ("zt", 0, 0), ("invert", 0, 1), ("maxima", 0, 0), ("low turned", 0, 2)],
    [("qk", 0, 0), ("low parts", 0, 0), ("invert", 0, 1), ("maxima", 0, 0), ("qk", 1, 0), ("low turned", 0, 2),
     ("low outputs", 1, 2)],
    [("low parts", 1, 0), ("invert", 0, 1), ("v", 0, 0), ("maxima", 0, 0), ("low turned", 0, 2), ("wo", 0, 2)],
    [("invert", 0, 1), ("maxima", 0, 0), ("low turned", 0, 2)],
    [("invert", 0, 1), ("maxima", 0, 0), ("low turned", 0, 2), ("norm out", 0, 2)],
]
X_ACT_SLOTS = [
    [("high outputs", 0, 2), ("st", 5, 1), ("high turned", 0, 2), ("exponentials", 0, 0), ("st", 6, 1)],
    [("st", 7, 1), ("high turned", 0, 2), ("exponentials", 0, 0)],
    [("high values", 0, 1), ("high turned", 0, 2), ("ct", 0, 0), ("zt", 0, 0), ("exponentials", 0, 0)],
    [("high turned", 0, 2), ("exponentials", 0, 0), ("qk", 0, 0), ("high outputs", 1, 2)],
    [("high turned", 0, 2), ("qk", 1, 0), ("exponentials", 0, 0)],
    [("high turned", 0, 2), ("exponentials", 0, 0), ("st", 0, 0)],
    [("high turned", 0, 2), ("st", 1, 0), ("st", 2, 0), ("st", 3, 0), ("exponentials", 0, 0)],
    [("high turned", 0, 2), ("st", 4, 0), ("exponentials", 0, 0)],
]


def attend_phase(nc, ctx, y, d_x, d_ctx, d_w, d_bias, d_ident, d_sum, first, pool_jobs, spare=None):

    tag = "a_" if first else "c_"

    def sb(name, shape, dt=F32):
        return ctx.enter_context(nc.sbuf_tensor(tag + name, shape, dt))

    def sem(name):
        return nc.alloc_semaphore(tag + name)

    ident = sb("ident", [P, P])
    w_h, w_l = sb("w_h", [P, KD, XW], F32R), sb("w_l", [P, KD, XW], F32R)
    wo_h, wo_l = sb("wo_h", [P, XQ, DIM], F32R), sb("wo_l", [P, XQ, DIM], F32R)
    bias = sb("bias", [P, 4 * DIM])
    x_in_tile = None if first else sb("x_in_tile", [P, TILES * DIM])
    c_in_tile = sb("c_in_tile", [P, TILES, DIM])
    z = sb("z", [P, TILES, DIM])
    bst = sb("bst", [P, 2, TILES, 6])
    mv = sb("mv", [P, 2, TILES, 2])
    vareps = sb("vareps", [P, 2, TILES])
    rstd = sb("rstd", [P, 2, TILES])
    minus_half = sb("minus_half", [P, TILES])
    cTh, cTl = (sb(c, [P, KD, SEQ], F32R)[:] for c in ("x_cTh", "x_cTl"))
    qk = sb("qk", [P, 2, XHEADS, XDH])
    parts = sb("parts", [P, TILES, 2, XHEADS, 2, 2, XDH], F32R)
    stacked = sb("stacked", [P, XPAIRS, 2, SEQ], F32R)
    spare_h, spare_l = spare if spare else (sb("spare_h", [P, SPARE], F32R), sb("spare_l", [P, SPARE], F32R))
    zTh, zTl = (w[:, XQ * SEQ:(XQ + KD) * SEQ].rearrange("p (k s) -> p k s", k=KD) for w in (spare_h, spare_l))
    v = sb("v", [P, TILES, DIM])
    v_rows = [w[:, (XQ + KD) * SEQ:(XQ + KD) * SEQ + VROW] for w in (spare_h, spare_l)]
    probs = sb("probs", [P, 2, 2, TILES, SEQ])
    raw_qkv = probs[:].rearrange("p r h t s -> p (r h t s)")[:, 0:KD * XW]
    raw_wo = (probs[:].rearrange("p r h t s -> p (r h t s)")[:, KD * XW:KD * XW + 512], v[:].rearrange("p t d -> p (t d)"))
    pth, ptl = sb("pth", [P, 2, 2, SEQ], F32R), sb("ptl", [P, 2, 2, SEQ], F32R)
    nmax = sb("nmax", [P, 4, 2, TILES])
    rsum = sb("rsum", [P, 4, 2, TILES])
    rinv = sb("rinv", [P, 4, 2, TILES])
    oth, otl = (w[:, 0:XQ * SEQ].rearrange("p (q s) -> p q s", q=XQ) for w in (spare_h, spare_l))

    def bank(name):
        return ctx.enter_context(nc.psum_tensor(tag + name, [P, 512], F32))

    ps_sim = [bank("ps_sim0"), bank("ps_sim1")]
    ps_pt = [bank("ps_pt0"), bank("ps_pt1")]
    ps_o = [bank("ps_o0"), bank("ps_o1")]
    ps_mm = [bank("ps_mm0"), bank("ps_mm1")]

    WEIGHTS = [(raw_qkv, w_h[:].rearrange("p k c -> p (k c)"), w_l[:].rearrange("p k c -> p (k c)"))]
    for i in range(2):
        half = slice(2 * i, 2 * i + 2)
        WEIGHTS.append((raw_wo[i], wo_h[:, half, :].rearrange("p q c -> p (q c)"),
                        wo_l[:, half, :].rearrange("p q c -> p (q c)")))

    zt_done, ct_done, proj_done, v_done = sem("zt_done"), sem("ct_done"), sem("proj_done"), sem("v_done")
    st_done, sim_done, pt_done, pv_done = sem("st_done"), sem("sim_done"), sem("pt_done"), sem("pv_done")
    wo_done = sem("wo_done")
    x_ready, stats_ready, mv_ready, z_ready = sem("x_ready"), sem("stats_ready"), sem("mv_ready"), sem("z_ready")
    ztl_ready, ctl_ready, qk_biased, parts_l = sem("ztl_ready"), sem("ctl_ready"), sem("qk_biased"), sem("parts_l")
    v_ready, vl_ready, max_ready, ptl_ready = sem("v_ready"), sem("vl_ready"), sem("max_ready"), sem("ptl_ready")
    rinv_ready, otl_ready, wo_read = sem("rinv_ready"), sem("otl_ready"), sem("wo_read")
    x_summed, stats2_ready, mv2_ready, y_normed = (sem("x_summed"), sem("stats2_ready"), sem("mv2_ready"),
                                                   sem("y_normed"))
    wl_ready, bias_scaled, zeroed = sem("wl_ready"), sem("bias_scaled"), sem("zeroed")
    wh_ready, zth_ready, cth_ready, parts_h = sem("wh_ready"), sem("zth_ready"), sem("cth_ready"), sem("parts_h")
    exp_done, pth_ready, oth_ready = sem("exp_done"), sem("pth_ready"), sem("oth_ready")
    vh_ready, st_moved = sem("vh_ready"), sem("st_moved")
    normed = sem("normed")
    minus_ready, rs_part, rstd_ready, rs2_part, rstd2_ready = (sem("minus_ready"), sem("rs_part"), sem("rstd_ready"),
                                                               sem("rs2_part"), sem("rstd2_ready"))
    ident_in, const_in, x_in, c_in, sum_out = (sem("ident_in"), sem("const_in"), sem("x_in"), sem("c_in"),
                                               sem("sum_out"))

    block = ctx.enter_context(nc.Block())
    FULL = (3, BATCH)
    EDGES = (range(0, FULL[0]), range(FULL[1], BATCH + 2))

    def on(m):
        return not isinstance(m, int) or 0 <= m < BATCH

    def later(m, first_=0):
        return not isinstance(m, int) or m > first_

    def pair_on(g):
        return not isinstance(g, int) or 0 <= g < BATCH * XPAIRS

    def settle(eng):
        eng.nop(nofuse=True)

    ORDER = [u for slot in X_PE_SLOTS for u in slot if u[0] in X_BANK_USES]
    assert len(ORDER) % 2 == 0
    FREED = {"st": (st_moved, 8), "v": (v_ready, 1), "zt": (ztl_ready, 1), "ct": (ctl_ready, 1), "qk": (qk_biased, 2),
             "wo": (wo_read, 1)}

    def mm_bank(use, idx):
        return ps_mm[[u[:2] for u in ORDER].index((use, idx)) % 2]

    def y_of(m):
        return y[:, bass.ds(m * TILES * DIM, TILES * DIM)]

    def value_views():
        for t in range(TILES):
            src = v[:, t, :].rearrange("p (q r d) -> p q r d", r=4, d=XDH)
            for base, places, heads in ((0, slice(0, 5, 4), slice(0, 4, 3)), (VHALF, slice(1, 5, 3), slice(1, 3))):
                dst = v_rows[t][:, base:base + VHALF].rearrange("p (q e c) -> p q e c", e=5, c=VPART)[:, :, places, :]
                yield src[:, :, heads, :], (dst[:, :, :, 0:XDH], dst[:, :, :, XDH:2 * XDH])

    def part_views(t, w):
        if w == 0:
            return parts[:, t, w, :, :, 0, :], parts[:, t, w, :, :, 1, :]
        return parts[:, t, w, :, 0, :, :], parts[:, t, w, :, 1, :, :]

    @block.tensor
    def _(pe):
        def split3(out, lhs_h, lhs_l, rhs_h, rhs_l, start, stop):
            pe.matmul(out, lhs_h, rhs_h, start=start, stop=False)
            pe.matmul(out, lhs_h, rhs_l, start=False, stop=False)
            return pe.matmul(out, lhs_l, rhs_h, start=False, stop=stop)

        def dense(n, use, idx, lag):
            m = n - lag
            if not on(m):
                return
            bank_ = mm_bank(use, idx)
            at = [u[:2] for u in ORDER].index((use, idx)) - 2
            while at > -4 * len(ORDER):
                before, i, blag = ORDER[at % len(ORDER)]
                bm = n - blag + at // len(ORDER)
                if on(bm):
                    signal, per = FREED[before]
                    pe.wait_ge(signal, per * bm + i + 1)
                    break
                at -= 2
            if use in ("zt", "ct"):
                if use == "zt":
                    pe.wait_ge(z_ready, m + 1)
                else:
                    pe.wait_ge(c_in, 16 * (m + 1))
                src = z if use == "zt" else c_in_tile
                for k in range(KD):
                    for t in range(TILES):
                        mm = pe.transpose(bank_[:, k * SEQ + t * P:k * SEQ + (t + 1) * P],
                                          src[:, t, k * P:(k + 1) * P], ident[:])
                mm.then_inc(zt_done if use == "zt" else ct_done, 1)
            elif use == "qk":
                if idx == 0:
                    pe.wait_ge(ztl_ready, m + 1)
                    pe.wait_ge(ctl_ready, m + 1)
                    if not later(m):
                        pe.wait_ge(wl_ready, len(WEIGHTS))
                t = idx
                for w, (h_, l_) in enumerate(((zTh, zTl), (cTh, cTl))):
                    for k in range(KD):
                        cols = slice(w * DIM, (w + 1) * DIM)
                        mm = split3(bank_[:, cols], h_[:, k, t * P:(t + 1) * P], l_[:, k, t * P:(t + 1) * P],
                                    w_h[:, k, cols], w_l[:, k, cols], k == 0, k == KD - 1)
                mm.then_inc(proj_done, 1)
            elif use == "v":
                cols = slice(2 * DIM, 3 * DIM)
                for t in range(TILES):
                    for k in range(KD):
                        mm = split3(bank_[:, t * DIM:(t + 1) * DIM], cTh[:, k, t * P:(t + 1) * P],
                                    cTl[:, k, t * P:(t + 1) * P], w_h[:, k, cols], w_l[:, k, cols], k == 0, k == KD - 1)
                mm.then_inc(v_done, 1)
            elif use == "st":
                pe.wait_ge(parts_l, 4 * m + 4)
                for w in range(2):
                    for t in range(TILES):
                        src = parts[:, t, w, 2 * idx:2 * idx + 2].bitcast(F32).rearrange("p h a b d -> p (h a b d)")
                        mm = pe.transpose(bank_[:, w * SEQ + t * P:w * SEQ + (t + 1) * P], src, ident[:])
                mm.then_inc(st_done, 1)
            elif use == "wo":
                pe.wait_ge(otl_ready, 2 * m + 2)
                for t in range(TILES):
                    for q in range(XQ):
                        mm = split3(bank_[:, t * DIM:(t + 1) * DIM], oth[:, q, t * P:(t + 1) * P],
                                    otl[:, q, t * P:(t + 1) * P], wo_h[:, q, :], wo_l[:, q, :], q == 0, q == XQ - 1)
                mm.then_inc(wo_done, 1)

        def scores(g, p, m):
            pe.wait_ge(st_moved, 8 * m + p + 1)
            for h in range(2):
                if later(g):
                    pe.wait_ge(exp_done, 2 * (g - 1) + h + 1)
                rows = slice(64 * h, 64 * h + 64)
                for t in range(TILES):
                    mm = pe.matmul(ps_sim[h][:, t * SEQ:(t + 1) * SEQ], stacked[rows, p, 0, t * P:(t + 1) * P],
                                   stacked[rows, p, 1, :], start=True, stop=True)
                mm.then_inc(sim_done, 1)

        def turn_probs(g, r):
            for h in range(2):
                pe.wait_ge(normed, 2 * g + h + 1)
                if later(g):
                    pe.wait_ge(ptl_ready, 2 * (g - 1) + h + 1)
                for c in range(2):
                    for t in range(TILES):
                        mm = pe.transpose(ps_pt[h][:, c * SEQ + t * P:c * SEQ + (t + 1) * P],
                                          probs[:, r, h, t, c * P:(c + 1) * P], ident[:])
                mm.then_inc(pt_done, 1)

        def weigh_values(g, p, m):
            pe.wait_ge(ptl_ready, 2 * g + 2)
            if p == 0:
                pe.wait_ge(vl_ready, m + 1)
            if p % 4 == 0 and later(m):
                pe.wait_ge(otl_ready, 2 * (m - 1) + p // 4 + 1)
            for h in range(2):
                head = 2 * p + h
                r, q = head % 4, head // 4
                out = ps_o[q // 2][:, (q % 2) * SEQ:(q % 2 + 1) * SEQ]
                at = VWINDOW[r] + VGROUP * q
                for c in range(2):
                    for i, part in enumerate((pth, ptl)):
                        mm = pe.matmul(out, v_rows[c][:, at:at + P], part[:, h, c, :], start=r + c + i == 0,
                                       stop=r == 3 and c == 1 and i == 1)
            mm.then_inc(pv_done, 1)

        def step(n):
            for j, slot in enumerate(X_PE_SLOTS):
                for what, idx, lag in slot:
                    if what in X_BANK_USES:
                        dense(n, what, idx, lag)
                        continue
                    g, p, m = XPAIRS * (n - 1) + j - lag, (j - lag) % XPAIRS, n - 1 - (lag > j)
                    if not pair_on(g):
                        continue
                    if what == "scores":
                        scores(g, p, m)
                    elif what == "turn probs":
                        turn_probs(g, (j - lag) % 2)
                    elif what == "weigh values":
                        weigh_values(g, p, m)

        pe.wait_ge(ident_in, 16)
        for n in EDGES[0]:
            step(n)
        with pe.Fori(*FULL) as n:
            step(n)
        for n in EDGES[1]:
            step(n)

    @block.vector
    def _(dve):
        ve = nc.vector

        def stats(m, which, signal, out_signal):
            for t in range(TILES):
                mm = ve.bn_stats(bst[:, which, t, :], y[:, bass.ds(m * TILES * DIM + t * DIM, DIM)])
            mm.then_inc(signal, 1)
            dve.wait_ge(signal, m + 1)
            settle(dve)
            for t in range(TILES):
                mm = ve.bn_aggr(mv[:, which, t, :], bst[:, which, t, :])
            mm.then_inc(out_signal, 1)

        def rows_in(m):
            dve.wait_ge(x_in, 16 * (m + 1))
            if not first:
                ve.tensor_tensor(y_of(m), y_of(m), x_in_tile[:], ALU.add).then_inc(x_ready, 1)
                dve.wait_ge(x_ready, m + 1)
            settle(dve)
            stats(m, 0, stats_ready, mv_ready)

        def norm_in(m):
            dve.wait_ge(rstd_ready, m + 1)
            if later(m):
                dve.wait_ge(zt_done, m)
            for t in range(TILES):
                mm = ve.tensor_scalar(z[:, t, :], y[:, bass.ds(m * TILES * DIM + t * DIM, DIM)], mv[:, 0, t, 0:1],
                                      rstd[:, 0, t:t + 1], ALU.subtract, ALU.mult)
            mm.then_inc(z_ready, 1)

        def norm_out(m):
            dve.wait_ge(rstd2_ready, m + 1)
            dve.wait_ge(sum_out, 16 * (m + 1))
            for t in range(TILES):
                yt = y[:, bass.ds(m * TILES * DIM + t * DIM, DIM)]
                mm = ve.tensor_scalar(yt, yt, mv[:, 1, t, 0:1], rstd[:, 1, t:t + 1], ALU.subtract, ALU.mult)
            mm.then_inc(y_normed, 1)

        def evacuate(n, use, idx, lag):
            m = n - lag
            if not on(m):
                return
            bank_ = mm_bank(use, idx)
            if use in ("zt", "ct"):
                hi, lo, got, done = ((zTh, zTl, zth_ready, ztl_ready) if use == "zt" else
                                     (cTh, cTl, cth_ready, ctl_ready))
                dve.wait_ge(got, m + 1)
                ve.tensor_tensor(lo.rearrange("p k s -> p (k s)"), bank_[:],
                                 hi.bitcast(F32).rearrange("p k s -> p (k s)"), ALU.subtract).then_inc(done, 1)
            elif use == "qk":
                i = 2 * m + idx
                dve.wait_ge(proj_done, i + 1)
                if later(i):
                    dve.wait_ge(parts_l, 2 * i)
                qkf = qk[:].rearrange("p w h d -> p w (h d)")
                ve.scalar_tensor_tensor(out=qkf[:, 0], in0=bank_[:, 0:DIM], scalar=XDH ** -0.5, in1=bias[:, 0:DIM],
                                        op0=ALU.mult, op1=ALU.add)
                ve.tensor_tensor(qkf[:, 1], bank_[:, DIM:2 * DIM], bias[:, DIM:2 * DIM], ALU.add).then_inc(qk_biased, 1)
            elif use == "v":
                dve.wait_ge(v_done, m + 1)
                if later(m):
                    dve.wait_ge(vl_ready, m)
                ve.tensor_tensor(v[:], bank_[:].rearrange("p (t d) -> p t d", t=TILES),
                                 bias[:, 2 * DIM:3 * DIM].unsqueeze(1).broadcast_to([P, TILES, DIM]),
                                 ALU.add).then_inc(v_ready, 1)
            elif use == "wo":
                dve.wait_ge(wo_done, m + 1)
                ve.tensor_tensor(y_of(m), bank_[:], y_of(m), ALU.add).then_inc(wo_read, 1)
                dve.wait_ge(wo_read, m + 1)
                y3 = y_of(m).rearrange("p (t d) -> p t d", t=TILES)
                ve.tensor_tensor(y3, y3, bias[:, 3 * DIM:4 * DIM].unsqueeze(1).broadcast_to([P, TILES, DIM]),
                                 ALU.add).then_inc(x_summed, 1)
                if first:
                    dve.wait_ge(x_summed, m + 1)
                    settle(dve)
                    stats(m, 1, stats2_ready, mv2_ready)

        def maxima(g, r):
            for h in range(2):
                dve.wait_ge(sim_done, 2 * g + h + 1)
                ve.tensor_reduce(nmax[:, r, h, :], ps_sim[h][:].rearrange("p (t s) -> p t s", t=TILES), AX.X, ALU.max,
                                 negate=True).then_inc(max_ready, 1)

        def low_parts(m, t):
            dve.wait_ge(parts_h, 4 * m + 2 * t + 2)
            for w in range(2):
                hi, lo = part_views(t, w)
                src = qk[:, w].unsqueeze(2).broadcast_to([P, XHEADS, 2, XDH])
                ve.tensor_tensor(lo, src, hi.bitcast(F32), ALU.subtract).then_inc(parts_l, 1)

        def low_values(m):
            dve.wait_ge(vh_ready, m + 1)
            for src, dst in value_views():
                high = dst[0]
                mm = ve.tensor_tensor(dst[1], src, high.bitcast(F32), ALU.subtract)
            mm.then_inc(vl_ready, 1)

        def invert_sums(g, r):
            dve.wait_ge(exp_done, 2 * g + 2)
            ve.reciprocal(rinv[:, r].rearrange("p h t -> p (h t)"),
                          rsum[:, r].rearrange("p h t -> p (h t)")).then_inc(rinv_ready, 1)

        def low_turned(g):
            for h in range(2):
                dve.wait_ge(pth_ready, 2 * g + h + 1)
                ve.tensor_tensor(ptl[:, h].rearrange("p c s -> p (c s)"), ps_pt[h][:],
                                 pth[:, h].bitcast(F32).rearrange("p c s -> p (c s)"), ALU.subtract).then_inc(ptl_ready, 1)

        def low_outputs(m, k):
            dve.wait_ge(oth_ready, 2 * m + k + 1)
            ve.tensor_tensor(otl[:, 2 * k:2 * k + 2, :].rearrange("p q s -> p (q s)"), ps_o[k][:],
                             oth[:, 2 * k:2 * k + 2, :].bitcast(F32).rearrange("p q s -> p (q s)"),
                             ALU.subtract).then_inc(otl_ready, 1)

        def step(n):
            for j, slot in enumerate(X_DVE_SLOTS):
                for what, idx, lag in slot:
                    m = n - lag
                    if what in X_BANK_USES:
                        evacuate(n, what, idx, lag)
                    elif what in X_PAIR_WORK:
                        g = XPAIRS * (n - 1) + j - lag
                        if not pair_on(g):
                            continue
                        if what == "low turned":
                            low_turned(g)
                        elif what == "invert":
                            invert_sums(g, (j - lag) % 4)
                        elif what == "maxima":
                            maxima(g, (j - lag) % 4)
                    elif not on(m):
                        continue
                    elif what in ("rows in", "norm in") and not later(m):
                        continue
                    elif what == "rows in":
                        rows_in(m)
                    elif what == "norm in":
                        norm_in(m)
                    elif what == "norm out":
                        if first:
                            norm_out(m)
                    elif what == "low parts":
                        low_parts(m, idx)
                    elif what == "low values":
                        low_values(m)
                    elif what == "low outputs":
                        low_outputs(m, idx)

        for row in v_rows:
            ve.memset(row.bitcast(F32), 0.0).then_inc(zeroed, 1)
        rows_in(0)
        norm_in(0)
        dve.wait_ge(const_in, 16 * 3)
        ve.tensor_scalar(bias[:, 0:DIM], bias[:, 0:DIM], XDH ** -0.5, None, ALU.mult).then_inc(bias_scaled, 1)
        dve.wait_ge(bias_scaled, 1)
        for i, (raw, high, low) in enumerate(WEIGHTS):
            dve.wait_ge(wh_ready, i + 1)
            ve.tensor_tensor(low, raw, high.bitcast(F32), ALU.subtract).then_inc(wl_ready, 1)
        for n in EDGES[0]:
            step(n)
        with dve.Fori(*FULL) as n:
            step(n)
        for n in EDGES[1]:
            step(n)

    @block.scalar
    def _(act):
        sc = nc.scalar

        def exponentials(g, r):
            for h in range(2):
                act.wait_ge(max_ready, 2 * g + h + 1)
                if later(g, 1):
                    act.wait_ge(pt_done, 2 * (g - 2) + h + 1)
                for t in range(TILES):
                    mm = sc.activation(probs[:, r % 2, h, t, :], ps_sim[h][:, t * SEQ:(t + 1) * SEQ], ACT.Exp,
                                       bias=nmax[:, r, h, t:t + 1], accum_out=rsum[:, r, h, t:t + 1])
                mm.then_inc(exp_done, 1)

        def high_turned(g):
            for h in range(2):
                act.wait_ge(pt_done, 2 * g + h + 1)
                if later(g):
                    act.wait_ge(pv_done, g)
                sc.copy(pth[:, h].rearrange("p c s -> p (c s)"), ps_pt[h][:]).then_inc(pth_ready, 1)

        def high_values(m):
            act.wait_ge(v_ready, m + 1)
            if later(m):
                act.wait_ge(pv_done, XPAIRS * m)
            for src, dst in value_views():
                mm = sc.copy(dst[0], src)
            mm.then_inc(vh_ready, 1)

        def high_outputs(m, k):
            act.wait_ge(pv_done, XPAIRS * m + 4 * k + 4)
            if later(m):
                act.wait_ge(wo_done, m)
            sc.copy(oth[:, 2 * k:2 * k + 2, :].rearrange("p q s -> p (q s)"), ps_o[k][:]).then_inc(oth_ready, 1)

        def evacuate(n, use, idx, lag):
            m = n - lag
            if not on(m):
                return
            bank_ = mm_bank(use, idx)
            if use in ("zt", "ct"):
                hi, done, ready = (zTh, zt_done, zth_ready) if use == "zt" else (cTh, ct_done, cth_ready)
                act.wait_ge(done, m + 1)
                if later(m):
                    act.wait_ge(v_done, m)
                sc.copy(hi.rearrange("p k s -> p (k s)"), bank_[:]).then_inc(ready, 1)
            elif use == "qk":
                i = 2 * m + idx
                act.wait_ge(qk_biased, i + 1)
                if later(m):
                    act.wait_ge(st_done, 8 * m)
                for w in range(2):
                    sc.copy(part_views(idx, w)[0], qk[:, w].unsqueeze(2).broadcast_to([P, XHEADS, 2, XDH])).then_inc(parts_h, 1)
            elif use == "st":
                act.wait_ge(st_done, 8 * m + idx + 1)
                if later(m):
                    act.wait_ge(sim_done, 2 * (XPAIRS * (m - 1) + idx + 1))
                sc.copy(stacked[:, idx].rearrange("p w s -> p (w s)"), bank_[:]).then_inc(st_moved, 1)

        def step(n):
            for j, slot in enumerate(X_ACT_SLOTS):
                for what, idx, lag in slot:
                    if what in X_BANK_USES:
                        evacuate(n, what, idx, lag)
                        continue
                    if what in ("high values", "high outputs"):
                        if on(n - lag):
                            if what == "high values":
                                high_values(n - lag)
                            else:
                                high_outputs(n - lag, idx)
                        continue
                    g = XPAIRS * (n - 1) + j - lag
                    if not pair_on(g):
                        continue
                    if what == "high turned":
                        high_turned(g)
                    elif what == "exponentials":
                        exponentials(g, (j - lag) % 4)

        act.wait_ge(const_in, 16 * 3)
        for raw, high, low in WEIGHTS:
            sc.copy(high, raw).then_inc(wh_ready, 1)
        act.wait_ge(zeroed, TILES)
        act.wait_ge(wl_ready, len(WEIGHTS))
        for n in EDGES[0]:
            step(n)
        with act.Fori(*FULL) as n:
            step(n)
        for n in EDGES[1]:
            step(n)

    @block.gpsimd
    def _(pool):
        gp = nc.gpsimd

        def inverse_deviation(m, which, got, part_signal, signal):
            pool.wait_ge(got, m + 1)
            gp.tensor_scalar(vareps[:, which, :], mv[:, which, :, 1], 1.0, EPS, ALU.mult, ALU.add).then_inc(part_signal, 1)
            pool.wait_ge(part_signal, m + 1)
            gp.tensor_tensor(rstd[:, which, :], vareps[:, which, :], minus_half[:], ALU.pow).then_inc(signal, 1)

        gp.memset(minus_half[:], -0.5).then_inc(minus_ready, 1)
        pool.wait_ge(minus_ready, 1)
        def normalise(g, r):
            pool.wait_ge(rinv_ready, g + 1)
            for h in range(2):
                part = probs[:, r % 2, h]
                gp.tensor_tensor(part, part, rinv[:, r, h, :].unsqueeze(2).broadcast_to([P, TILES, SEQ]),
                                 ALU.mult).then_inc(normed, 1)

        jobs = pool_jobs(pool)
        for n in range(BATCH + 2):
            for j in range(XPAIRS):
                g = XPAIRS * (n - 1) + j - X_POOL_LAG
                if pair_on(g):
                    normalise(g, g % 4)
                if j == 0 and on(n):
                    inverse_deviation(n, 0, mv_ready, rs_part, rstd_ready)
                elif first and j == X_POOL_OUT[0] and on(n - X_POOL_OUT[1]):
                    inverse_deviation(n - X_POOL_OUT[1], 1, mv2_ready, rs2_part, rstd2_ready)
                else:
                    next(jobs, None)
        for _ in jobs:
            pass

    @block.sync
    def _(sp):
        x_rows = d_x.rearrange("(s t p) d -> s p t d", t=TILES, p=P)
        c_rows = d_ctx.rearrange("(s t p) d -> s p t d", t=TILES, p=P)
        sum_rows = d_sum.rearrange("(s t p) d -> s p t d", t=TILES, p=P) if first else None

        def step(n):
            if on(n):
                if later(n) and not first:
                    sp.wait_ge(x_ready, n)
                if later(n) and first:
                    sp.wait_ge(x_in, 16 * n)
                settle(sp)
                dst = y_of(n) if first else x_in_tile[:]
                sp.dma_start(dst.rearrange("p (t d) -> p t d", t=TILES), x_rows[n]).then_inc(x_in, 16)
                if later(n):
                    sp.wait_ge(ct_done, n)
                settle(sp)
                sp.dma_start(c_in_tile[:], c_rows[n]).then_inc(c_in, 16)
            if first and on(n - 2):
                sp.wait_ge(x_summed, n - 1)
                settle(sp)
                sp.dma_start(sum_rows[n - 2], y_of(n - 2).rearrange("p (t d) -> p t d", t=TILES)).then_inc(sum_out, 16)

        step(0)
        sp.dma_start(ident[:], d_ident).then_inc(ident_in, 16)
        sp.dma_start(probs[:].rearrange("p r h t s -> p (r h t s)"), d_w[:, 0:KD * XW + 512]).then_inc(const_in, 16)
        sp.dma_start(v[:].rearrange("p t d -> p (t d)"), d_w[:, KD * XW + 512:]).then_inc(const_in, 16)
        sp.dma_start(bias[:], d_bias).then_inc(const_in, 16)
        for n in range(1, BATCH + 2):
            step(n)
        if first:
            sp.wait_ge(sum_out, 16 * BATCH)


def ffn_phase(nc, ctx, y, d_ident, d_out, wd_h, wd_l):

    def sb(name, shape, dt=F32):
        return ctx.enter_context(nc.sbuf_tensor(name, shape, dt))

    def sem(name):
        return nc.alloc_semaphore(name)

    def bank(name):
        return ctx.enter_context(nc.psum_tensor(name, [P, 512], F32))

    ident = sb("f_ident", [P, P])
    minus_half = sb("f_minus_half", [P, TILES])
    z = sb("f_z", [P, TILES, DIM])
    bst, mv = sb("f_bst", [P, TILES, 6]), sb("f_mv", [P, TILES, 2])
    vareps, rstd = sb("f_vareps", [P, TILES]), sb("f_rstd", [P, TILES])
    zTh, zTl = sb("f_zTh", [P, KD, SEQ], F32R), sb("f_zTl", [P, KD, SEQ], F32R)
    hid = sb("f_hid", [P, HT, SEQ])
    hh, hl = sb("f_hh", [P, HT, SEQ], F32R), sb("f_hl", [P, HT, SEQ], F32R)
    out_tile = sb("f_out", [P, TILES, DIM])
    GROUPS = HT // 2
    ps_gate = [bank(f"f_ps_gate{i}") for i in range(GROUPS)]
    ps_up = [bank(f"f_ps_up{i}") for i in range(GROUPS)]
    ps_turn, ps_down = bank("f_ps_turn"), bank("f_ps_down")

    zt_done, gate_done, up_done, down_done = sem("f_zt_done"), sem("f_gate_done"), sem("f_up_done"), sem("f_down_done")
    stats_ready, mv_ready, z_ready, ztl_ready = (sem("f_stats_ready"), sem("f_mv_ready"), sem("f_z_ready"),
                                                 sem("f_ztl_ready"))
    h_ready, hl_ready, out_ready = sem("f_h_ready"), sem("f_hl_ready"), sem("f_out_ready")
    zth_ready, silu_done, hh_ready = sem("f_zth_ready"), sem("f_silu_done"), sem("f_hh_ready")
    minus_ready, rs_part, rstd_ready = sem("f_minus_ready"), sem("f_rs_part"), sem("f_rstd_ready")
    const_in, out_stored = sem("f_const_in"), sem("f_out_stored")

    block = ctx.enter_context(nc.Block())
    FULL = (3, BATCH)

    def on(m):
        return not isinstance(m, int) or 0 <= m < BATCH

    def later(m):
        return not isinstance(m, int) or m > 0

    def steps(eng, step):
        for n in range(FULL[0]):
            step(n)
        with eng.Fori(*FULL) as n:
            step(n)
        step(BATCH)
        step(BATCH + 1)

    def y_tile(m, t):
        return y[:, bass.ds(m * TILES * DIM + t * DIM, DIM)]

    def wcols(w, at, k, f):
        return w[:, (at * KD + k) * HID + f * P:(at * KD + k) * HID + (f + 1) * P]

    @block.tensor
    def _(pe):
        def split3(out, lhs_h, lhs_l, rhs_h, rhs_l, start, stop, **kw):
            pe.matmul(out, lhs_h, rhs_h, start=start, stop=False, **kw)
            pe.matmul(out, lhs_h, rhs_l, start=False, stop=False, **kw)
            return pe.matmul(out, lhs_l, rhs_h, start=False, stop=stop, **kw)

        def step(n):
            m = n - 1
            if on(m):
                pe.wait_ge(ztl_ready, m + 1)
                for i in range(GROUPS):
                    for at, ps, read, done in ((0, ps_gate, silu_done, gate_done), (1, ps_up, h_ready, up_done)):
                        if later(m):
                            pe.wait_ge(read, GROUPS * (m - 1) + i + 1)
                        for j in range(2):
                            for k in range(KD):
                                mm = split3(ps[i][:, j * SEQ:(j + 1) * SEQ], wcols(wd_h, at, k, 2 * i + j),
                                            wcols(wd_l, at, k, 2 * i + j), zTh[:, k, :], zTl[:, k, :],
                                            k == 0, k == KD - 1)
                        mm.then_inc(done, 1)
            if on(n):
                pe.wait_ge(z_ready, n + 1)
                if later(n):
                    pe.wait_ge(ztl_ready, n)
                for k in range(KD):
                    for t in range(TILES):
                        mm = pe.transpose(ps_turn[:, k * SEQ + t * P:k * SEQ + (t + 1) * P], z[:, t, k * P:(k + 1) * P],
                                          ident[:])
                mm.then_inc(zt_done, 1)
            m = n - 2
            if on(m):
                if later(m):
                    pe.wait_ge(out_ready, m)
                for f in range(HT):
                    if f % 2 == 0:
                        pe.wait_ge(hl_ready, GROUPS * m + f // 2 + 1)
                    cols = slice((2 * KD * HID) + f * DIM, (2 * KD * HID) + (f + 1) * DIM)
                    for t in range(TILES):
                        mm = split3(ps_down[:, t * DIM:(t + 1) * DIM], hh[:, f, t * P:(t + 1) * P],
                                    hl[:, f, t * P:(t + 1) * P], wd_h[:, cols], wd_l[:, cols],
                                    f == 0 and t == 0, f == HT - 1, skip_group_check=True)
                mm.then_inc(down_done, 1)

        pe.wait_ge(const_in, 16)
        steps(pe, step)

    @block.vector
    def _(dve):
        ve = nc.vector

        def step(n):
            m = n - 1
            if on(n):
                for t in range(TILES):
                    mm = ve.bn_stats(bst[:, t, :], y_tile(n, t))
                mm.then_inc(stats_ready, 1)
                dve.wait_ge(stats_ready, n + 1)
                dve.nop(nofuse=True)
                for t in range(TILES):
                    mm = ve.bn_aggr(mv[:, t, :], bst[:, t, :])
                mm.then_inc(mv_ready, 1)
            if on(m):
                for i in range(GROUPS):
                    dve.wait_ge(up_done, GROUPS * m + i + 1)
                    dve.wait_ge(silu_done, GROUPS * m + i + 1)
                    rows = hid[:, 2 * i:2 * i + 2, :].rearrange("p f s -> p (f s)")
                    ve.tensor_tensor(rows, ps_up[i][:], rows, ALU.mult).then_inc(h_ready, 1)
            if on(n):
                dve.wait_ge(rstd_ready, n + 1)
                if later(n):
                    dve.wait_ge(zt_done, n)
                for t in range(TILES):
                    mm = ve.tensor_scalar(z[:, t, :], y_tile(n, t), mv[:, t, 0:1], rstd[:, t:t + 1],
                                          ALU.subtract, ALU.mult)
                mm.then_inc(z_ready, 1)
            if on(n):
                dve.wait_ge(zth_ready, n + 1)
                ve.tensor_tensor(zTl[:].rearrange("p k s -> p (k s)"), ps_turn[:],
                                 zTh[:].bitcast(F32).rearrange("p k s -> p (k s)"), ALU.subtract).then_inc(ztl_ready, 1)
            m = n - 2
            if on(m):
                dve.wait_ge(down_done, m + 1)
                if later(m):
                    dve.wait_ge(out_stored, 16 * m)
                ve.tensor_tensor(out_tile[:].rearrange("p t d -> p (t d)"), ps_down[:],
                                 y[:, bass.ds(m * TILES * DIM, TILES * DIM)], ALU.add).then_inc(out_ready, 1)
            m = n - 1
            if on(m):
                for i in range(GROUPS):
                    dve.wait_ge(hh_ready, GROUPS * m + i + 1)
                    part = slice(2 * i, 2 * i + 2)
                    ve.tensor_tensor(hl[:, part, :], hid[:, part, :], hh[:, part, :].bitcast(F32),
                                     ALU.subtract).then_inc(hl_ready, 1)

        steps(dve, step)

    @block.scalar
    def _(act):
        sc = nc.scalar

        def step(n):
            m = n - 1
            if on(m):
                for i in range(GROUPS):
                    act.wait_ge(gate_done, GROUPS * m + i + 1)
                    if later(m):
                        act.wait_ge(hl_ready, GROUPS * (m - 1) + i + 1)
                    sc.activation(hid[:, 2 * i:2 * i + 2, :].rearrange("p f s -> p (f s)"), ps_gate[i][:],
                                  ACT.Silu).then_inc(silu_done, 1)
            if on(n):
                act.wait_ge(zt_done, n + 1)
                if later(n):
                    act.wait_ge(up_done, GROUPS * n)
                sc.copy(zTh[:].rearrange("p k s -> p (k s)"), ps_turn[:]).then_inc(zth_ready, 1)
            if on(m):
                for i in range(GROUPS):
                    act.wait_ge(h_ready, GROUPS * m + i + 1)
                    if later(m):
                        act.wait_ge(down_done, m)
                    part = slice(2 * i, 2 * i + 2)
                    sc.copy(hh[:, part, :], hid[:, part, :]).then_inc(hh_ready, 1)

        steps(act, step)

    @block.gpsimd
    def _(pool):
        gp = nc.gpsimd

        def step(n):
            if not on(n):
                return
            pool.wait_ge(mv_ready, n + 1)
            pool.nop(nofuse=True)
            gp.tensor_scalar(vareps[:], mv[:, :, 1], 1.0, EPS, ALU.mult, ALU.add).then_inc(rs_part, 1)
            pool.wait_ge(rs_part, n + 1)
            gp.tensor_tensor(rstd[:], vareps[:], minus_half[:], ALU.pow).then_inc(rstd_ready, 1)

        gp.memset(minus_half[:], -0.5).then_inc(minus_ready, 1)
        pool.wait_ge(minus_ready, 1)
        steps(pool, step)

    @block.sync
    def _(sp):
        out_rows = d_out.rearrange("(s t p) d -> s p t d", t=TILES, p=P)
        sp.dma_start(ident[:], d_ident).then_inc(const_in, 16)
        for m in range(BATCH):
            sp.wait_ge(out_ready, m + 1)
            sp.dma_start(out_rows[m], out_tile[:]).then_inc(out_stored, 16)
        sp.wait_ge(out_stored, 16 * BATCH)


def split_ffn_weights(nc, pool, raw_int, raw, d_w, wd_h, wd_l, sems):
    gp = nc.gpsimd
    int_in, scaled, w_hi, w_done = sems
    for u in range(DW_UNITS):
        cols = slice(512 * u, 512 * (u + 1))
        if u:
            pool.wait_ge(w_done, u)
        pool.dma_start(raw_int[:], d_w[:, cols]).then_inc(int_in, 16)
        yield
        pool.wait_ge(int_in, 16 * (u + 1))
        gp.tensor_scalar(raw[:], raw_int[:], 1.0, 1.0 / 127.0, ALU.mult, ALU.mult).then_inc(scaled, 1)
        pool.wait_ge(scaled, u + 1)
        gp.tensor_copy(wd_h[:, cols], raw[:]).then_inc(w_hi, 1)
        pool.wait_ge(w_hi, u + 1)
        gp.tensor_tensor(wd_l[:, cols], raw[:], wd_h[:, cols].bitcast(F32), ALU.subtract).then_inc(w_done, 1)
        yield


def split_stack_weights(nc, pool, raw, d_w, wh, wl, sems):
    gp = nc.gpsimd
    raw_in, w_hi, w_done = sems
    for u in range(U_LATE):
        part = slice(OFFS[u], OFFS[u] + UNITS[u])
        if u:
            pool.wait_ge(w_done, u)
        pool.dma_start(raw[:, 0:UNITS[u]], d_w[:, part]).then_inc(raw_in, 16)
        yield
        pool.wait_ge(raw_in, 16 * (u + 1))
        gp.tensor_copy(wh[:, part], raw[:, 0:UNITS[u]]).then_inc(w_hi, 1)
        pool.wait_ge(w_hi, u + 1)
        gp.tensor_tensor(wl[:, part], raw[:, 0:UNITS[u]], wh[:, part].bitcast(F32), ALU.subtract).then_inc(w_done, 1)
        yield


def transformer_kernel(nc, d_x, d_ctx, d_a_w, d_a_bias, d_stack_w, d_prm, d_qks, d_b2, d_const, d_c_w, d_c_bias,
                       d_ffn_w, d_ident, d_out):
    d_sum = nc.dram_tensor("x_after_attention", [BATCH * SEQ, DIM], F32).ap()
    with ExitStack() as whole:
        y = whole.enter_context(nc.sbuf_tensor("y", [P, BATCH * TILES * DIM], F32))
        with ExitStack() as weights:
            wh = weights.enter_context(nc.sbuf_tensor("wh", [P, WCOLS], F32R))
            wl = weights.enter_context(nc.sbuf_tensor("wl", [P, WCOLS], F32R))
            with nc.cleanup_on_exit(), ExitStack() as ctx:
                raw = ctx.enter_context(nc.sbuf_tensor("a_raw", [P, 512], F32))
                sems = [nc.alloc_semaphore(s) for s in ("a_raw_in", "a_raw_hi", "a_raw_done")]
                attend_phase(nc, ctx, y, d_x, d_ctx, d_a_w, d_a_bias, d_ident, d_sum, True,
                             lambda pool: split_stack_weights(nc, pool, raw, d_stack_w, wh, wl, sems),
                             (wh[:, OFFS[U_LATE]:WCOLS], wl[:, OFFS[U_LATE]:WCOLS]))
            with nc.cleanup_on_exit(), ExitStack() as ctx:
                stack_phase(nc, ctx, y, wh, wl, d_stack_w, d_prm, d_qks, d_b2, d_const)
        wd_h = whole.enter_context(nc.sbuf_tensor("wd_h", [P, 512 * DW_UNITS], F32R))
        wd_l = whole.enter_context(nc.sbuf_tensor("wd_l", [P, 512 * DW_UNITS], F32R))
        with nc.cleanup_on_exit(), ExitStack() as ctx:
            raw = ctx.enter_context(nc.sbuf_tensor("c_raw", [P, 512], F32))
            raw_int = ctx.enter_context(nc.sbuf_tensor("c_raw_int", [P, 512], mybir.dt.int32))
            sems = [nc.alloc_semaphore(s) for s in ("c_int_in", "c_scaled", "c_raw_hi", "c_raw_done")]
            attend_phase(nc, ctx, y, d_sum, d_ctx, d_c_w, d_c_bias, d_ident, None, False,
                         lambda pool: split_ffn_weights(nc, pool, raw_int, raw, d_ffn_w, wd_h, wd_l, sems))
        with nc.cleanup_on_exit(), ExitStack() as ctx:
            ffn_phase(nc, ctx, y, d_ident, d_out, wd_h, wd_l)


def attend_weights(ws):
    qkv = np.concatenate(ws[:3], axis=1).reshape(KD, P, XW).transpose(1, 0, 2).reshape(P, KD * XW)
    wo = np.broadcast_to(ws[3].reshape(XQ, 4, 1, XDH, DIM), (XQ, 4, 2, XDH, DIM))
    return np.ascontiguousarray(np.concatenate([qkv, wo.transpose(1, 2, 3, 0, 4).reshape(P, XQ * DIM)], axis=1))


def shape_constants():
    half = np.arange(0, DH, 2, dtype=np.float32)
    inv_freq = (np.float32(1.0) / np.float32(10000.0) ** (half / np.float32(DH))).astype(np.float32)
    t = np.arange(SEQ, dtype=np.float32)
    freqs = (t[:, None] * inv_freq[None, :]).astype(np.float32)
    base = ((half + np.float32(0.4 * DH)) / np.float32(1.4 * DH)).astype(np.float32)
    power = ((t - SEQ // 2) / np.float32(WINDOW // 2)).astype(np.float32)
    scale = (base[None, :] ** power[:, None]).astype(np.float32)
    cos, sin = np.cos(freqs), np.sin(freqs)
    inv = (np.float32(1.0) / scale).astype(np.float32)
    tables = np.stack([cos * scale, sin * scale, cos * inv, sin * inv]).astype(np.float32)
    tables = tables.reshape(4, TILES, P, 32).transpose(2, 0, 1, 3).reshape(P, -1)
    r = np.arange(P)[:, None]
    masks = []
    for q0, k0, w in ((0, 0, P), (P, P - WINDOW, P + WINDOW)):
        d = (r + q0) - (np.arange(w)[None, :] + k0)
        masks.append(np.where((d >= 0) & (d <= WINDOW), 0.0, -1.0e30).astype(np.float32))
    return np.ascontiguousarray(np.concatenate([tables] + masks + [np.eye(P, dtype=np.float32)], axis=1))


def pack_stack_weights(Wqkv, Wo, W1, W2):
    out = np.zeros((DEPTH, P, WCOLS), Wqkv.dtype)
    kt = Wqkv.reshape(DEPTH, KD, P, 3 * INNER)
    for c, at in enumerate((0, INNER, 512, INNER + 512, 2 * INNER, 2 * INNER + 512)):
        for k in range(KD):
            o = OFFS[U_QKV + 2 * c + k]
            out[:, :, o:o + 512] = kt[:, k, :, at:at + 512]
    wo = Wo.reshape(DEPTH, PAIRS, P, DIM)
    for i in range(4):
        for q in range(2):
            o = OFFS[U_WO + i] + q * DIM
            out[:, :, o:o + DIM] = wo[:, 2 * i + q]
    w1 = np.zeros((DEPTH, KD, P, 2, FT * FP), W1.dtype)
    w1[..., :FF] = W1.reshape(DEPTH, KD, P, 2, FF)
    for i in range(3):
        for k in range(KD):
            for which, u in ((1, U_GATE), (0, U_UP)):
                o = OFFS[u + i] + k * 2 * FP
                out[:, :, o:o + 2 * FP] = w1[:, k, :, which, 2 * FP * i:2 * FP * (i + 1)]
    w2 = np.zeros((DEPTH, FT * FP, DIM), W2.dtype)
    w2[:, :FF] = W2
    w2 = w2.reshape(DEPTH, FT, FP, DIM)
    for i in range(3):
        for j in range(2):
            o = OFFS[U_W2 + i] + j * DIM
            out[:, :FP, o:o + DIM] = w2[:, 2 * i + j]
    return np.ascontiguousarray(out.transpose(1, 0, 2).reshape(P, DEPTH * WCOLS))


def pack_stack_params(ln_g, ln_b, b1):
    out = np.zeros((P, DEPTH, NPRM), ln_g.dtype)
    out[:, :, 0:KD] = ln_g.reshape(DEPTH, KD, P).transpose(2, 0, 1)
    out[:, :, KD:2 * KD] = ln_b.reshape(DEPTH, KD, P).transpose(2, 0, 1)
    for which, at in ((1, 2 * KD), (0, 2 * KD + FT)):
        b = np.zeros((DEPTH, FT * FP), b1.dtype)
        b[:, :FF] = b1[:, which * FF:(which + 1) * FF]
        out[:FP, :, at:at + FT] = b.reshape(DEPTH, FT, FP).transpose(2, 0, 1)
    return np.ascontiguousarray(out.reshape(P, -1))


def kernel(**inputs):
    import concourse.bacc as bacc
    from concourse.bass_utils import run_bass_kernel_spmd

    a = {k: np.asarray(x) for k, x in inputs.items()}

    def rows(vectors):
        return np.ascontiguousarray(np.broadcast_to(np.concatenate([x.reshape(-1) for x in vectors]), (P, sum(x.size for x in vectors))))

    def hidden_major(w):
        return w.T.reshape(KD, P, HID).transpose(1, 0, 2).reshape(P, KD * HID)

    f = {k[len("L0_ffn_"):]: x for k, x in a.items() if k.startswith("L0_ffn_")}
    p, q = "L0_xattn_", "L1_xattn_"
    arrays = {
        "x": a["x"].reshape(BATCH * SEQ, DIM),
        "ctx": a["ctx_1024"].reshape(BATCH * SEQ, DIM),
        "a_w": attend_weights([a[p + s].T for s in ("wq_w", "wk_w", "wv_w", "wo_w")]),
        "a_bias": rows([a[p + s] for s in ("wq_b", "wk_b", "wv_b", "wo_b")]),
        "stack_w": pack_stack_weights(f["Wqkv"], f["Wo"], f["W1"], f["W2"]),
        "prm": pack_stack_params(f["ln_g"], f["ln_b"], f["b1"]),
        "qks": rows([x[i] for i in range(DEPTH) for x in (f["q_scale"], f["k_scale"])]),
        "b2": rows([f["b2"]]),
        "const": shape_constants(),
        "c_w": attend_weights([a[q + s] for s in ("Wq", "Wk", "Wv", "Wo")]),
        "c_bias": rows([a[q + s] for s in ("bq", "bk", "bv", "bo")]),
        "ffn_w": np.concatenate([hidden_major(a["L1_ffn_w_gate"]), hidden_major(a["L1_ffn_w_up"]),
                                 a["L1_ffn_w_down"].T.reshape(HT, P, DIM).transpose(1, 0, 2).reshape(P, HT * DIM)],
                                axis=1),
        "ident": np.eye(P, dtype=np.float32),
    }
    nc = bacc.Bacc("TRN2", target_bir_lowering=False, num_devices=1)
    feeds, args = {}, []
    for name, x in arrays.items():
        x = np.ascontiguousarray(x)
        feeds[f"in_{name}"] = x
        args.append(nc.dram_tensor(f"in_{name}", x.shape, mybir.dt.from_np(x.dtype), kind="ExternalInput").ap())
    args.append(nc.dram_tensor("out_x", [BATCH * SEQ, DIM], F32, kind="ExternalOutput").ap())
    transformer_kernel(nc, *args)
    r = run_bass_kernel_spmd(nc, [feeds], core_ids=[0])
    return r.results[0]["out_x"].reshape(BATCH, SEQ, DIM)
```
